# Optimizing a Trainium2 kernel written in Bass

```python
import numpy as np
import jax
import jax.numpy as jnp

def _softmax(x, axis=-1):
    return jax.nn.softmax(x, axis=axis)

def _gelu(x):
    return jax.nn.gelu(x, approximate=True)

def _silu(x):
    return jax.nn.silu(x)

def _sigmoid(x):
    return jax.nn.sigmoid(x)

def _layernorm(x, axis=-1, eps=1e-05):
    m = jnp.mean(x, axis=axis, keepdims=True)
    v = jnp.var(x, axis=axis, keepdims=True)
    return (x - m) / jnp.sqrt(v + eps)

def _scatter_add(tgt, idx, src, axis=0):
    return tgt.at[idx].add(src)

def _segment_sum(src, seg, n):
    return jax.ops.segment_sum(src, seg, n)
kernel_name = 'mk_pixart_seq_d4_seqx_r8_69a87d'

def setup_inputs(seed: int=0):
    np.random.seed(seed)
    _w = jnp.asarray

    def _rec_inputs():
        import jax
        import jax.numpy as jnp
        _rk = jax.random.key(seed)
        x = -0.0003929 + 0.9999 * jax.random.normal(jax.random.fold_in(_rk, 1), (4, 256, 128), jnp.float32)
        _lenS = 256 - jax.random.randint(jax.random.fold_in(_rk, 7), (4,), 0, max(1, 256 // 4) + 1, jnp.int32)
        _lenS2 = 256 - jax.random.randint(jax.random.fold_in(_rk, 8), (4,), 0, max(1, 256 // 4) + 1, jnp.int32)
        cond_1024 = 0.00782532 + 1.00527 * jax.random.normal(jax.random.fold_in(_rk, 11), (4, 128), jnp.float32)
        _ctx_1024P = jax.random.normal(jax.random.fold_in(_rk, 12), (4, 16, 128), jnp.float32)
        _ctx_1024c = jax.random.dirichlet(jax.random.fold_in(_rk, 512), 0.3 * jnp.ones((16,), jnp.float32), (4, 256))
        _ctx_1024t = jnp.einsum('bsk,bkd->bsd', _ctx_1024c, _ctx_1024P)
        _ctx_1024t = _ctx_1024t * jax.lax.rsqrt(jnp.mean(jnp.square(_ctx_1024t)) + 1e-12) * 0.953939
        ctx_1024 = -0.000761806 + 0.999296 * (_ctx_1024t + 0.3 * jax.random.normal(jax.random.fold_in(_rk, 612), (4, 256, 128), jnp.float32))
        return (x, cond_1024, ctx_1024)
    x, cond_1024, ctx_1024 = _rec_inputs()

    def _L0_xcond_setup():
        import jax, jax.numpy as jnp
        import numpy as np
        H = 128
        RH = 2 * H
        E = 3
        B, T, P = (8, 256, 64)
        LN_EPS = 1e-05

        def _layer_norm(x, gamma, beta):
            mu = jnp.mean(x, axis=-1, keepdims=True)
            var = jnp.mean(jnp.square(x - mu), axis=-1, keepdims=True)
            return (x - mu) * jax.lax.rsqrt(var + LN_EPS) * gamma + beta
        key = jax.random.key(seed)
        ks = jax.random.split(key, 24)
        s = lambda fan_in: 1.0 / np.sqrt(fan_in)
        inp = {'mix_hidden_states': jax.random.normal(ks[0], (B, T, H), jnp.float32), 'global_anchor': jax.random.normal(ks[1], (B, H), jnp.float32), 'prototype_bank': jax.random.normal(ks[2], (B, P, H), jnp.float32), 'ln_gamma': jnp.ones((H,), jnp.float32), 'ln_beta': jnp.zeros((H,), jnp.float32), 'Wq': jax.random.normal(ks[3], (H, H), jnp.float32) * s(H), 'Wk': jax.random.normal(ks[4], (H, H), jnp.float32) * s(H), 'Wv': jax.random.normal(ks[5], (H, H), jnp.float32) * s(H), 'router_W': jax.random.normal(ks[6], (3 * H, E), jnp.float32) * s(3 * H), 'router_b': jnp.zeros((E,), jnp.float32), 'e_w1': jax.random.normal(ks[7], (E, 3 * H, RH), jnp.float32) * s(3 * H), 'e_b1': jnp.zeros((E, RH), jnp.float32), 'e_w2': jax.random.normal(ks[8], (E, RH, H), jnp.float32) * s(RH), 'e_b2': jnp.zeros((E, H), jnp.float32), 'gate_w1': jax.random.normal(ks[9], (3 * H, H), jnp.float32) * s(3 * H), 'gate_b1': jnp.zeros((H,), jnp.float32), 'gate_w2': jax.random.normal(ks[10], (H, H), jnp.float32) * s(H), 'gate_b2': jnp.zeros((H,), jnp.float32), 'out_w': jax.random.normal(ks[11], (H, H), jnp.float32) * s(H), 'out_b': jnp.zeros((H,), jnp.float32)}
        return inp
    _L0_xcond_all = _L0_xcond_setup()
    _L0_xcond_in = {k: v for k, v in _L0_xcond_all.items() if k in ('ln_gamma', 'ln_beta', 'Wq', 'Wk', 'Wv', 'router_W', 'router_b', 'e_w1', 'e_b1', 'e_w2', 'e_b2', 'gate_w1', 'gate_b1', 'gate_w2', 'gate_b2', 'out_w', 'out_b')}
    del _L0_xcond_all

    def _L1_xcond_setup():
        import jax, jax.numpy as jnp
        import numpy as np
        EPS = 1e-05

        def _ada_ln(x, c, W_ss, b_ss):
            mu = jnp.mean(x, axis=-1, keepdims=True)
            var = jnp.mean((x - mu) ** 2, axis=-1, keepdims=True)
            h = (x - mu) / jnp.sqrt(var + EPS)
            ss = jax.nn.silu(c) @ W_ss + b_ss
            scale, bias = jnp.split(ss, 2, axis=-1)
            return (1.0 + scale)[:, None, :] * h + bias[:, None, :]
        key = jax.random.key(seed)
        ks = jax.random.split(key, 12)
        B, Lq, Lkv, H = (8, 256, 64, 128)
        s = 0.02
        return {'x_q': jax.random.normal(ks[0], (B, Lq, H), jnp.float32), 'x_kv': jax.random.normal(ks[1], (B, Lkv, H), jnp.float32), 't_vec': jax.random.normal(ks[2], (B, H), jnp.float32), 'Wq': jax.random.normal(ks[3], (H, H), jnp.float32) * s, 'bq': jnp.zeros((H,), jnp.float32), 'Wkv': jax.random.normal(ks[4], (H, 2 * H), jnp.float32) * s, 'bkv': jnp.zeros((2 * H,), jnp.float32), 'Wp': jax.random.normal(ks[5], (H, H), jnp.float32) * s, 'bp': jnp.zeros((H,), jnp.float32), 'Wss_q': jax.random.normal(ks[6], (H, 2 * H), jnp.float32) * s, 'bss_q': jnp.zeros((2 * H,), jnp.float32), 'Wss_kv': jax.random.normal(ks[7], (H, 2 * H), jnp.float32) * s, 'bss_kv': jnp.zeros((2 * H,), jnp.float32)}
    _L1_xcond_all = _L1_xcond_setup()
    _L1_xcond_in = {k: v for k, v in _L1_xcond_all.items() if k in ('Wq', 'bq', 'Wkv', 'bkv', 'Wp', 'bp', 'Wss_q', 'bss_q', 'Wss_kv', 'bss_kv')}
    del _L1_xcond_all

    def _L2_xcond_setup():
        import jax, jax.numpy as jnp
        import numpy as np
        EPS = 1e-06
        H = 16

        def layer_norm(x, gamma=None, beta=None):
            x32 = x.astype(jnp.float32)
            mu = jnp.mean(x32, axis=-1, keepdims=True)
            var = jnp.var(x32, axis=-1, keepdims=True)
            y = (x32 - mu) * jax.lax.rsqrt(var + EPS)
            if gamma is not None:
                y = y * gamma + beta
            return y.astype(x.dtype)

        def mha(q, k, v):
            B, Nq, C = q.shape
            d = C // H
            qh = q.reshape(B, Nq, H, d)
            kh = k.reshape(B, k.shape[1], H, d)
            vh = v.reshape(B, v.shape[1], H, d)
            scores = jnp.einsum('bqhd,bkhd->bhqk', qh, kh) / jnp.sqrt(jnp.asarray(d, q.dtype))
            attn = jax.nn.softmax(scores, axis=-1)
            out = jnp.einsum('bhqk,bkhd->bqhd', attn, vh)
            return out.reshape(B, Nq, C)
        key = jax.random.key(seed)
        ks = jax.random.split(key, 24)
        B, N, C, M, Cc = (4, 256, 128, 128, 128)
        hid = 4 * C
        s = 0.02
        return {'x': jax.random.normal(ks[0], (B, N, C), jnp.float32), 'mod': jax.random.normal(ks[1], (B, C), jnp.float32), 'context': jax.random.normal(ks[2], (B, M, Cc), jnp.float32), 'ada_w': jax.random.normal(ks[3], (C, 6 * C), jnp.float32) * s, 'ada_b': jnp.zeros((6 * C,), jnp.float32), 'qkv_w': jax.random.normal(ks[4], (C, 3 * C), jnp.float32) * s, 'qkv_b': jnp.zeros((3 * C,), jnp.float32), 'self_o_w': jax.random.normal(ks[5], (C, C), jnp.float32) * s, 'self_o_b': jnp.zeros((C,), jnp.float32), 'norm2_g': jnp.ones((C,), jnp.float32), 'norm2_b': jnp.zeros((C,), jnp.float32), 'q_w': jax.random.normal(ks[6], (C, C), jnp.float32) * s, 'q_b': jnp.zeros((C,), jnp.float32), 'kv_w': jax.random.normal(ks[7], (Cc, 2 * C), jnp.float32) * s, 'kv_b': jnp.zeros((2 * C,), jnp.float32), 'cross_o_w': jax.random.normal(ks[8], (C, C), jnp.float32) * s, 'cross_o_b': jnp.zeros((C,), jnp.float32), 'mlp_w1': jax.random.normal(ks[9], (C, hid), jnp.float32) * s, 'mlp_b1': jnp.zeros((hid,), jnp.float32), 'mlp_w2': jax.random.normal(ks[10], (hid, C), jnp.float32) * s, 'mlp_b2': jnp.zeros((C,), jnp.float32)}
    _L2_xcond_all = _L2_xcond_setup()
    _L2_xcond_in = {k: v for k, v in _L2_xcond_all.items() if k in ('ada_w', 'ada_b', 'qkv_w', 'qkv_b', 'self_o_w', 'self_o_b', 'norm2_g', 'norm2_b', 'q_w', 'q_b', 'kv_w', 'kv_b', 'cross_o_w', 'cross_o_b', 'mlp_w1', 'mlp_b1', 'mlp_w2', 'mlp_b2')}
    del _L2_xcond_all

    def _L3_xcond_setup():
        import jax, jax.numpy as jnp
        import numpy as np
        C = 128
        H = 16
        D = C // H
        WIN = 64
        SHIFT = 32
        TOPK = 16
        HID = 512
        EPS = 1e-06

        def _ln(x):
            x32 = x.astype(jnp.float32)
            m = x32.mean(-1, keepdims=True)
            v = jnp.mean((x32 - m) ** 2, axis=-1, keepdims=True)
            return ((x32 - m) * jax.lax.rsqrt(v + EPS)).astype(x.dtype)

        def _self_attn(h, w_qkv, b_qkv, w_so, b_so):
            B, L, _ = h.shape
            qkv = h @ w_qkv + b_qkv
            qkv = jnp.roll(qkv, -SHIFT, axis=1)
            nw = L // WIN
            qkv = qkv.reshape(B, nw, WIN, 3, H, D)
            q, k, v = (qkv[:, :, :, 0], qkv[:, :, :, 1], qkv[:, :, :, 2])
            scores = jnp.einsum('bnqhd,bnkhd->bnhqk', q, k) / jnp.sqrt(jnp.float32(D)).astype(h.dtype)
            attn = jax.nn.softmax(scores, axis=-1)
            o = jnp.einsum('bnhqk,bnkhd->bnqhd', attn, v).reshape(B, L, C)
            o = jnp.roll(o, SHIFT, axis=1)
            return o @ w_so + b_so

        def _topk_cross_attn(h, ctx, w_q, b_q, w_kv, b_kv, w_co, b_co):
            B, L, _ = h.shape
            Lc = ctx.shape[1]
            q = (h @ w_q + b_q).reshape(B, L, H, D)
            kv = (ctx @ w_kv + b_kv).reshape(B, Lc, 2, H, D)
            k, v = (kv[:, :, 0], kv[:, :, 1])
            scores = jnp.einsum('bqhd,bkhd->bhqk', q, k) / jnp.sqrt(jnp.float32(D)).astype(h.dtype)
            top_s, top_i = jax.lax.top_k(scores, TOPK)
            attn = jax.nn.softmax(top_s, axis=-1)
            v_bh = jnp.transpose(v, (0, 2, 1, 3))
            vg = jnp.take_along_axis(v_bh[:, :, None, :, :], top_i[..., None], axis=3)
            o = jnp.einsum('bhqk,bhqkd->bqhd', attn, vg).reshape(B, L, C)
            return o @ w_co + b_co

        def _swiglu(h, w_m1, b_m1, w_m2, b_m2):
            u = h @ w_m1 + b_m1
            a, b = (u[..., :HID], u[..., HID:])
            return jax.nn.silu(a) * b @ w_m2 + b_m2
        key = jax.random.key(seed)
        ks = jax.random.split(key, 24)
        s = 0.02
        inp = {'x': jax.random.normal(ks[0], (2, 512, C), jnp.float32), 'mod': jax.random.normal(ks[1], (2, C), jnp.float32), 'context': jax.random.normal(ks[2], (2, 128, C), jnp.float32), 'w_ada': jax.random.normal(ks[3], (C, 9 * C), jnp.float32) * s, 'b_ada': jnp.zeros((9 * C,), jnp.float32), 'w_qkv': jax.random.normal(ks[4], (C, 3 * C), jnp.float32) * s, 'b_qkv': jnp.zeros((3 * C,), jnp.float32), 'w_so': jax.random.normal(ks[5], (C, C), jnp.float32) * s, 'b_so': jnp.zeros((C,), jnp.float32), 'w_q': jax.random.normal(ks[6], (C, C), jnp.float32) * s, 'b_q': jnp.zeros((C,), jnp.float32), 'w_kv': jax.random.normal(ks[7], (C, 2 * C), jnp.float32) * s, 'b_kv': jnp.zeros((2 * C,), jnp.float32), 'w_co': jax.random.normal(ks[8], (C, C), jnp.float32) * s, 'b_co': jnp.zeros((C,), jnp.float32), 'w_m1': jax.random.normal(ks[9], (C, 2 * HID), jnp.float32) * s, 'b_m1': jnp.zeros((2 * HID,), jnp.float32), 'w_m2': jax.random.normal(ks[10], (HID, C), jnp.float32) * s, 'b_m2': jnp.zeros((C,), jnp.float32)}
        return inp
    _L3_xcond_all = _L3_xcond_setup()
    _L3_xcond_in = {k: v for k, v in _L3_xcond_all.items() if k in ('w_ada', 'b_ada', 'w_qkv', 'b_qkv', 'w_so', 'b_so', 'w_q', 'b_q', 'w_kv', 'b_kv', 'w_co', 'b_co', 'w_m1', 'b_m1', 'w_m2', 'b_m2')}
    del _L3_xcond_all
    return {'x': x, 'cond_1024': cond_1024, 'ctx_1024': ctx_1024, 'L0_xcond_ln_gamma': _L0_xcond_in['ln_gamma'], 'L0_xcond_ln_beta': _L0_xcond_in['ln_beta'], 'L0_xcond_Wq': _L0_xcond_in['Wq'], 'L0_xcond_Wk': _L0_xcond_in['Wk'], 'L0_xcond_Wv': _L0_xcond_in['Wv'], 'L0_xcond_router_W': _L0_xcond_in['router_W'], 'L0_xcond_router_b': _L0_xcond_in['router_b'], 'L0_xcond_e_w1': _L0_xcond_in['e_w1'], 'L0_xcond_e_b1': _L0_xcond_in['e_b1'], 'L0_xcond_e_w2': _L0_xcond_in['e_w2'], 'L0_xcond_e_b2': _L0_xcond_in['e_b2'], 'L0_xcond_gate_w1': _L0_xcond_in['gate_w1'], 'L0_xcond_gate_b1': _L0_xcond_in['gate_b1'], 'L0_xcond_gate_w2': _L0_xcond_in['gate_w2'], 'L0_xcond_gate_b2': _L0_xcond_in['gate_b2'], 'L0_xcond_out_w': _L0_xcond_in['out_w'], 'L0_xcond_out_b': _L0_xcond_in['out_b'], 'L1_xcond_Wq': _L1_xcond_in['Wq'], 'L1_xcond_bq': _L1_xcond_in['bq'], 'L1_xcond_Wkv': _L1_xcond_in['Wkv'], 'L1_xcond_bkv': _L1_xcond_in['bkv'], 'L1_xcond_Wp': _L1_xcond_in['Wp'], 'L1_xcond_bp': _L1_xcond_in['bp'], 'L1_xcond_Wss_q': _L1_xcond_in['Wss_q'], 'L1_xcond_bss_q': _L1_xcond_in['bss_q'], 'L1_xcond_Wss_kv': _L1_xcond_in['Wss_kv'], 'L1_xcond_bss_kv': _L1_xcond_in['bss_kv'], 'L2_xcond_ada_w': _L2_xcond_in['ada_w'], 'L2_xcond_ada_b': _L2_xcond_in['ada_b'], 'L2_xcond_qkv_w': _L2_xcond_in['qkv_w'], 'L2_xcond_qkv_b': _L2_xcond_in['qkv_b'], 'L2_xcond_self_o_w': _L2_xcond_in['self_o_w'], 'L2_xcond_self_o_b': _L2_xcond_in['self_o_b'], 'L2_xcond_norm2_g': _L2_xcond_in['norm2_g'], 'L2_xcond_norm2_b': _L2_xcond_in['norm2_b'], 'L2_xcond_q_w': _L2_xcond_in['q_w'], 'L2_xcond_q_b': _L2_xcond_in['q_b'], 'L2_xcond_kv_w': _L2_xcond_in['kv_w'], 'L2_xcond_kv_b': _L2_xcond_in['kv_b'], 'L2_xcond_cross_o_w': _L2_xcond_in['cross_o_w'], 'L2_xcond_cross_o_b': _L2_xcond_in['cross_o_b'], 'L2_xcond_mlp_w1': _L2_xcond_in['mlp_w1'], 'L2_xcond_mlp_b1': _L2_xcond_in['mlp_b1'], 'L2_xcond_mlp_w2': _L2_xcond_in['mlp_w2'], 'L2_xcond_mlp_b2': _L2_xcond_in['mlp_b2'], 'L3_xcond_w_ada': _L3_xcond_in['w_ada'], 'L3_xcond_b_ada': _L3_xcond_in['b_ada'], 'L3_xcond_w_qkv': _L3_xcond_in['w_qkv'], 'L3_xcond_b_qkv': _L3_xcond_in['b_qkv'], 'L3_xcond_w_so': _L3_xcond_in['w_so'], 'L3_xcond_b_so': _L3_xcond_in['b_so'], 'L3_xcond_w_q': _L3_xcond_in['w_q'], 'L3_xcond_b_q': _L3_xcond_in['b_q'], 'L3_xcond_w_kv': _L3_xcond_in['w_kv'], 'L3_xcond_b_kv': _L3_xcond_in['b_kv'], 'L3_xcond_w_co': _L3_xcond_in['w_co'], 'L3_xcond_b_co': _L3_xcond_in['b_co'], 'L3_xcond_w_m1': _L3_xcond_in['w_m1'], 'L3_xcond_b_m1': _L3_xcond_in['b_m1'], 'L3_xcond_w_m2': _L3_xcond_in['w_m2'], 'L3_xcond_b_m2': _L3_xcond_in['b_m2']}

def reference(x, cond_1024, ctx_1024, L0_xcond_ln_gamma, L0_xcond_ln_beta, L0_xcond_Wq, L0_xcond_Wk, L0_xcond_Wv, L0_xcond_router_W, L0_xcond_router_b, L0_xcond_e_w1, L0_xcond_e_b1, L0_xcond_e_w2, L0_xcond_e_b2, L0_xcond_gate_w1, L0_xcond_gate_b1, L0_xcond_gate_w2, L0_xcond_gate_b2, L0_xcond_out_w, L0_xcond_out_b, L1_xcond_Wq, L1_xcond_bq, L1_xcond_Wkv, L1_xcond_bkv, L1_xcond_Wp, L1_xcond_bp, L1_xcond_Wss_q, L1_xcond_bss_q, L1_xcond_Wss_kv, L1_xcond_bss_kv, L2_xcond_ada_w, L2_xcond_ada_b, L2_xcond_qkv_w, L2_xcond_qkv_b, L2_xcond_self_o_w, L2_xcond_self_o_b, L2_xcond_norm2_g, L2_xcond_norm2_b, L2_xcond_q_w, L2_xcond_q_b, L2_xcond_kv_w, L2_xcond_kv_b, L2_xcond_cross_o_w, L2_xcond_cross_o_b, L2_xcond_mlp_w1, L2_xcond_mlp_b1, L2_xcond_mlp_w2, L2_xcond_mlp_b2, L3_xcond_w_ada, L3_xcond_b_ada, L3_xcond_w_qkv, L3_xcond_b_qkv, L3_xcond_w_so, L3_xcond_b_so, L3_xcond_w_q, L3_xcond_b_q, L3_xcond_w_kv, L3_xcond_b_kv, L3_xcond_w_co, L3_xcond_b_co, L3_xcond_w_m1, L3_xcond_b_m1, L3_xcond_w_m2, L3_xcond_b_m2):
    import jax
    import jax.numpy as jnp

    def _L0_xcond_ref(mix_hidden_states, global_anchor, prototype_bank, ln_gamma, ln_beta, Wq, Wk, Wv, router_W, router_b, e_w1, e_b1, e_w2, e_b2, gate_w1, gate_b1, gate_w2, gate_b2, out_w, out_b):
        import jax, jax.numpy as jnp
        import numpy as np
        H = 128
        RH = 2 * H
        E = 3
        B, T, P = (8, 256, 64)
        LN_EPS = 1e-05

        def _layer_norm(x, gamma, beta):
            mu = jnp.mean(x, axis=-1, keepdims=True)
            var = jnp.mean(jnp.square(x - mu), axis=-1, keepdims=True)
            return (x - mu) * jax.lax.rsqrt(var + LN_EPS) * gamma + beta
        x = mix_hidden_states
        nx = _layer_norm(x, ln_gamma, ln_beta)
        q = nx @ Wq
        k = prototype_bank @ Wk
        v = prototype_bank @ Wv
        scores = jnp.einsum('bth,bph->btp', q, k) * H ** (-0.5)
        weights = jax.nn.softmax(scores, axis=-1)
        evidence = jnp.einsum('btp,bph->bth', weights, v)
        anchor = jnp.broadcast_to(global_anchor[:, None, :], nx.shape)
        combined = jnp.concatenate([nx, evidence, anchor], axis=-1)
        router_logits = combined @ router_W + router_b
        router_probs = jax.nn.softmax(router_logits, axis=-1)
        h = jax.nn.silu(jnp.einsum('btc,ecr->bter', combined, e_w1) + e_b1)
        expert_out = jnp.einsum('bter,erh->bteh', h, e_w2) + e_b2
        routed = jnp.sum(expert_out * router_probs[..., None], axis=-2)
        g = jax.nn.sigmoid(jax.nn.silu(combined @ gate_w1 + gate_b1) @ gate_w2 + gate_b2)
        refined_delta = g * (routed @ out_w + out_b)
        return x + refined_delta

    def _L1_xcond_ref(x_q, x_kv, t_vec, Wq, bq, Wkv, bkv, Wp, bp, Wss_q, bss_q, Wss_kv, bss_kv):
        import jax, jax.numpy as jnp
        import numpy as np
        EPS = 1e-05

        def _ada_ln(x, c, W_ss, b_ss):
            mu = jnp.mean(x, axis=-1, keepdims=True)
            var = jnp.mean((x - mu) ** 2, axis=-1, keepdims=True)
            h = (x - mu) / jnp.sqrt(var + EPS)
            ss = jax.nn.silu(c) @ W_ss + b_ss
            scale, bias = jnp.split(ss, 2, axis=-1)
            return (1.0 + scale)[:, None, :] * h + bias[:, None, :]
        B, Lq, H = x_q.shape
        Lkv = x_kv.shape[1]
        nh = 16
        dh = H // nh
        xq = _ada_ln(x_q, t_vec, Wss_q, bss_q)
        xkv = _ada_ln(x_kv, t_vec, Wss_kv, bss_kv)
        q = (xq @ Wq + bq).reshape(B, Lq, nh, dh)
        kv = (xkv @ Wkv + bkv).reshape(B, Lkv, 2, nh, dh)
        k = kv[:, :, 0]
        v = kv[:, :, 1]
        scores = jnp.einsum('bqhd,bkhd->bhqk', q, k) / jnp.sqrt(jnp.float32(dh))
        attn = jax.nn.softmax(scores, axis=-1)
        out = jnp.einsum('bhqk,bkhd->bqhd', attn, v).reshape(B, Lq, H)
        return x_q + (out @ Wp + bp)

    def _L2_xcond_ref(x, mod, context, ada_w, ada_b, qkv_w, qkv_b, self_o_w, self_o_b, norm2_g, norm2_b, q_w, q_b, kv_w, kv_b, cross_o_w, cross_o_b, mlp_w1, mlp_b1, mlp_w2, mlp_b2):
        import jax, jax.numpy as jnp
        import numpy as np
        EPS = 1e-06
        H = 16

        def layer_norm(x, gamma=None, beta=None):
            x32 = x.astype(jnp.float32)
            mu = jnp.mean(x32, axis=-1, keepdims=True)
            var = jnp.var(x32, axis=-1, keepdims=True)
            y = (x32 - mu) * jax.lax.rsqrt(var + EPS)
            if gamma is not None:
                y = y * gamma + beta
            return y.astype(x.dtype)

        def mha(q, k, v):
            B, Nq, C = q.shape
            d = C // H
            qh = q.reshape(B, Nq, H, d)
            kh = k.reshape(B, k.shape[1], H, d)
            vh = v.reshape(B, v.shape[1], H, d)
            scores = jnp.einsum('bqhd,bkhd->bhqk', qh, kh) / jnp.sqrt(jnp.asarray(d, q.dtype))
            attn = jax.nn.softmax(scores, axis=-1)
            out = jnp.einsum('bhqk,bkhd->bqhd', attn, vh)
            return out.reshape(B, Nq, C)
        C = x.shape[-1]
        m = jax.nn.silu(mod) @ ada_w + ada_b
        shift_msa, scale_msa, gate_msa, shift_mlp, scale_mlp, gate_mlp = [c[:, None, :] for c in jnp.split(m, 6, axis=-1)]
        h = layer_norm(x)
        h = h * (1.0 + scale_msa) + shift_msa
        qkv = h @ qkv_w + qkv_b
        q, k, v = jnp.split(qkv, 3, axis=-1)
        h = mha(q, k, v) @ self_o_w + self_o_b
        x = x + h * gate_msa
        h = layer_norm(x, norm2_g, norm2_b)
        q = h @ q_w + q_b
        kv = context @ kv_w + kv_b
        k, v = jnp.split(kv, 2, axis=-1)
        h = mha(q, k, v) @ cross_o_w + cross_o_b
        x = x + h
        h = layer_norm(x)
        h = h * (1.0 + scale_mlp) + shift_mlp
        h = jax.nn.gelu(h @ mlp_w1 + mlp_b1) @ mlp_w2 + mlp_b2
        x = x + h * gate_mlp
        return x

    def _L3_xcond_ref(x, mod, context, w_ada, b_ada, w_qkv, b_qkv, w_so, b_so, w_q, b_q, w_kv, b_kv, w_co, b_co, w_m1, b_m1, w_m2, b_m2):
        import jax, jax.numpy as jnp
        import numpy as np
        C = 128
        H = 16
        D = C // H
        WIN = 64
        SHIFT = 32
        TOPK = 16
        HID = 512
        EPS = 1e-06

        def _ln(x):
            x32 = x.astype(jnp.float32)
            m = x32.mean(-1, keepdims=True)
            v = jnp.mean((x32 - m) ** 2, axis=-1, keepdims=True)
            return ((x32 - m) * jax.lax.rsqrt(v + EPS)).astype(x.dtype)

        def _self_attn(h, w_qkv, b_qkv, w_so, b_so):
            B, L, _ = h.shape
            qkv = h @ w_qkv + b_qkv
            qkv = jnp.roll(qkv, -SHIFT, axis=1)
            nw = L // WIN
            qkv = qkv.reshape(B, nw, WIN, 3, H, D)
            q, k, v = (qkv[:, :, :, 0], qkv[:, :, :, 1], qkv[:, :, :, 2])
            scores = jnp.einsum('bnqhd,bnkhd->bnhqk', q, k) / jnp.sqrt(jnp.float32(D)).astype(h.dtype)
            attn = jax.nn.softmax(scores, axis=-1)
            o = jnp.einsum('bnhqk,bnkhd->bnqhd', attn, v).reshape(B, L, C)
            o = jnp.roll(o, SHIFT, axis=1)
            return o @ w_so + b_so

        def _topk_cross_attn(h, ctx, w_q, b_q, w_kv, b_kv, w_co, b_co):
            B, L, _ = h.shape
            Lc = ctx.shape[1]
            q = (h @ w_q + b_q).reshape(B, L, H, D)
            kv = (ctx @ w_kv + b_kv).reshape(B, Lc, 2, H, D)
            k, v = (kv[:, :, 0], kv[:, :, 1])
            scores = jnp.einsum('bqhd,bkhd->bhqk', q, k) / jnp.sqrt(jnp.float32(D)).astype(h.dtype)
            top_s, top_i = jax.lax.top_k(scores, TOPK)
            attn = jax.nn.softmax(top_s, axis=-1)
            v_bh = jnp.transpose(v, (0, 2, 1, 3))
            vg = jnp.take_along_axis(v_bh[:, :, None, :, :], top_i[..., None], axis=3)
            o = jnp.einsum('bhqk,bhqkd->bqhd', attn, vg).reshape(B, L, C)
            return o @ w_co + b_co

        def _swiglu(h, w_m1, b_m1, w_m2, b_m2):
            u = h @ w_m1 + b_m1
            a, b = (u[..., :HID], u[..., HID:])
            return jax.nn.silu(a) * b @ w_m2 + b_m2
        m = jax.nn.silu(mod) @ w_ada + b_ada
        sh_msa, sc_msa, g_msa, sh_mca, sc_mca, g_mca, sh_mlp, sc_mlp, g_mlp = [m[:, i * C:(i + 1) * C][:, None, :] for i in range(9)]
        h = _ln(x) * (1 + sc_msa) + sh_msa
        h = _self_attn(h, w_qkv, b_qkv, w_so, b_so)
        x = x + h * g_msa
        h = _ln(x) * (1 + sc_mca) + sh_mca
        h = _topk_cross_attn(h, context, w_q, b_q, w_kv, b_kv, w_co, b_co)
        x = x + h * g_mca
        h = _ln(x) * (1 + sc_mlp) + sh_mlp
        h = _swiglu(h, w_m1, b_m1, w_m2, b_m2)
        x = x + h * g_mlp
        return x
    x = _L0_xcond_ref(x, cond_1024, ctx_1024, L0_xcond_ln_gamma, L0_xcond_ln_beta, L0_xcond_Wq, L0_xcond_Wk, L0_xcond_Wv, L0_xcond_router_W, L0_xcond_router_b, L0_xcond_e_w1, L0_xcond_e_b1, L0_xcond_e_w2, L0_xcond_e_b2, L0_xcond_gate_w1, L0_xcond_gate_b1, L0_xcond_gate_w2, L0_xcond_gate_b2, L0_xcond_out_w, L0_xcond_out_b)
    x = _L1_xcond_ref(x, ctx_1024, cond_1024, L1_xcond_Wq, L1_xcond_bq, L1_xcond_Wkv, L1_xcond_bkv, L1_xcond_Wp, L1_xcond_bp, L1_xcond_Wss_q, L1_xcond_bss_q, L1_xcond_Wss_kv, L1_xcond_bss_kv)
    x = _L2_xcond_ref(x, cond_1024, ctx_1024, L2_xcond_ada_w, L2_xcond_ada_b, L2_xcond_qkv_w, L2_xcond_qkv_b, L2_xcond_self_o_w, L2_xcond_self_o_b, L2_xcond_norm2_g, L2_xcond_norm2_b, L2_xcond_q_w, L2_xcond_q_b, L2_xcond_kv_w, L2_xcond_kv_b, L2_xcond_cross_o_w, L2_xcond_cross_o_b, L2_xcond_mlp_w1, L2_xcond_mlp_b1, L2_xcond_mlp_w2, L2_xcond_mlp_b2)
    x = _L3_xcond_ref(x, cond_1024, ctx_1024, L3_xcond_w_ada, L3_xcond_b_ada, L3_xcond_w_qkv, L3_xcond_b_qkv, L3_xcond_w_so, L3_xcond_b_so, L3_xcond_w_q, L3_xcond_b_q, L3_xcond_w_kv, L3_xcond_b_kv, L3_xcond_w_co, L3_xcond_b_co, L3_xcond_w_m1, L3_xcond_b_m1, L3_xcond_w_m2, L3_xcond_b_m2)
    return x

_drawn_inputs = setup_inputs


def setup_inputs(seed=0):
    import zlib

    import numpy as np

    out = dict(_drawn_inputs(seed))
    spreads = {'L0_xcond_ln_gamma': (1.0, 0.2),
     'L0_xcond_ln_beta': (0.0, 0.622),
     'L0_xcond_router_b': (0.0, 0.8),
     'L0_xcond_e_b1': (0.0, 0.365),
     'L0_xcond_e_b2': (0.0, 0.1),
     'L0_xcond_gate_b1': (0.0, 0.8),
     'L0_xcond_gate_b2': (0.0, 0.8),
     'L0_xcond_out_b': (0.0, 0.1),
     'L1_xcond_bq': (0.0, 2.0),
     'L1_xcond_bkv': (0.0, 0.342),
     'L1_xcond_bp': (0.0, 0.1),
     'L1_xcond_bss_q': (0.0, 0.8),
     'L1_xcond_bss_kv': (0.0, 0.8),
     'L2_xcond_ada_b': (0.0, 0.585),
     'L2_xcond_qkv_b': (0.0, 0.8),
     'L2_xcond_self_o_b': (0.0, 0.538),
     'L2_xcond_norm2_g': (1.0, 0.6),
     'L2_xcond_norm2_b': (0.0, 2.0),
     'L2_xcond_q_b': (0.0, 2.0),
     'L2_xcond_kv_b': (0.0, 0.438),
     'L2_xcond_cross_o_b': (0.0, 0.1),
     'L2_xcond_mlp_b1': (0.0, 0.8),
     'L2_xcond_mlp_b2': (0.0, 0.526),
     'L3_xcond_b_ada': (0.0, 0.456),
     'L3_xcond_b_qkv': (0.0, 0.8),
     'L3_xcond_b_so': (0.0, 0.395),
     'L3_xcond_b_q': (0.0, 0.8),
     'L3_xcond_b_kv': (0.0, 0.8),
     'L3_xcond_b_co': (0.0, 0.44),
     'L3_xcond_b_m1': (0.0, 0.8),
     'L3_xcond_b_m2': (0.0, 1.324)}
    factors = {'L1_xcond_Wq': 8.0,
     'L1_xcond_Wss_q': 8.0,
     'L1_xcond_Wss_kv': 7.343,
     'L2_xcond_ada_w': 2.68,
     'L2_xcond_qkv_w': 8.0,
     'L2_xcond_self_o_w': 8.0,
     'L2_xcond_q_w': 64.0,
     'L2_xcond_mlp_w1': 5.979,
     'L2_xcond_mlp_w2': 5.509,
     'L3_xcond_w_qkv': 8.0,
     'L3_xcond_w_so': 8.0,
     'L3_xcond_w_q': 8.0,
     'L3_xcond_w_kv': 8.0,
     'L3_xcond_w_co': 7.828,
     'L3_xcond_w_m1': 8.0,
     'L3_xcond_w_m2': 8.0,
     'L2_xcond_kv_w': 5.024}
    for name, (base, spread) in spreads.items():
        noise = np.random.default_rng([zlib.crc32(name.encode()), seed]).standard_normal(out[name].shape)
        drawn = base * np.exp(spread * noise) if base else spread * noise
        out[name] = jnp.asarray(drawn.astype(out[name].dtype))
    for name, factor in factors.items():
        out[name] = (out[name] * factor).astype(out[name].dtype)
    return out
```

```python
from contextlib import ExitStack

import concourse.bass as bass
from concourse import mybir

F32 = mybir.dt.float32
BF16 = mybir.dt.bfloat16
ALU = mybir.AluOpType
ACT = mybir.ActivationFunctionType
AX_X = mybir.AxisListType.X

B, T, C = 4, 256, 128
NT = T // 128
SLOTS = 2
H, D = 16, 8
HP = H // 2
E3, HID0 = 3, 256
HID = 512
WIN, SHIFT = 64, 32
PARTS = 3
BLOCKS = 6
ROWS = BLOCKS * D
ROWSM = ROWS + 2
TURN_LAG = 2
NEG = -3.0e37

SCALE0 = float(C) ** -0.5
SCALE = float(D) ** -0.5

MATS = {
    "early": [("l0_q", C), ("l0_k", C), ("l0_v", C)],
    "l0": [("l0_router", 3 * E3)] + [(f"l0_w1_{e}_{i}", HID0) for e in range(E3) for i in range(3)]
    + [(f"l0_w2_{e}_{i}", C) for e in range(E3) for i in range(2)]
    + [(f"l0_g1_{i}", C) for i in range(3)] + [("l0_g2", C), ("l0_out", C)],
    "mod": [("mod", 14 * C), ("gate", 5 * C)],
    "l1": [("q0", C), ("k0", C), ("v0", C), ("o0", C)],
    "l2": [("q1", C), ("k1", C), ("v1", C), ("o1", C), ("q2", C), ("k2", C), ("v2", C), ("o2", C),
           ("l2_w1", HID), ("l2_w2", 4 * C)],
    "l3": [("q3", C), ("k3", C), ("v3", C), ("o3", C), ("q4", C), ("k4", C), ("v4", C), ("o4", C),
           ("l3_w1", 2 * HID), ("l3_w2", 4 * C)],
}
MAT_AT, _n = {}, 0
GROUP_AT = {}
for _g, _list in MATS.items():
    GROUP_AT[_g] = _n
    for _name, _cols in _list:
        MAT_AT[_name] = (_n, _cols)
        _n += _cols
MAT_COLS = _n

COLS = ["ln_g", "ln_b"] + [f"mod{i}" for i in range(14)] + [f"anchor{i}" for i in range(7)]
COLS += [f"{x}{a}" for a in range(5) for x in ("bq", "bk")]
COLS += ["n2_g", "n2_b"] + [f"l2_b1_{i}" for i in range(4)] + [f"l3_b1_{i}" for i in range(8)]
COL = {n: i for i, n in enumerate(COLS)}

ROWV = ["router", "e0", "e1", "e2", "g2", "out"] + [f"{x}{a}" for a in range(5) for x in ("bv", "bo")]
ROWV += ["l2_b2", "l3_b2"] + [f"gate{i}" for i in range(5)]
ROW = {n: i for i, n in enumerate(ROWV)}

SC = dict(q=0, kv=1, l2a=2, l2m=3, l3a=4, l3c=5, l3m=6)
SH = {k: v + 7 for k, v in SC.items()}
GATE = dict(l2a=0, l2m=1, l3a=2, l3c=3, l3m=4)

LN_L0, LN_Q, LN_KV, LN_2A, LN_2C, LN_2M, LN_3A, LN_3C, LN_3M = range(9)
EPS = [1e-5, 1e-5, 1e-5, 1e-6, 1e-6, 1e-6, 1e-6, 1e-6, 1e-6]
UPDATES_BEFORE = [0, 1, 0, 2, 3, 4, 5, 6, 7]

A_L1, A_2S, A_2C, A_3W, A_3C = range(5)
NORMS_FOR = [LN_KV, LN_2A, LN_2C, LN_3A, LN_3C]


def psum_plan():
    big, small = [], []

    def attention(s_list, a):
        for s in s_list:
            small.append((s, "qk", a))
            small.append((s, "v", a))
        units = 2 if a == A_3W else HP
        if a == A_3C:
            for s in s_list:
                for j in range(HP + TURN_LAG):
                    if j < HP:
                        big.append((s, "top", j))
                    if j >= TURN_LAG:
                        big.append((s, "topT", j - TURN_LAG))
                small.append((s, "o", a))
        else:
            for s in s_list:
                big.extend((s, "s", a, j) for j in range(units))
            for s in s_list:
                small.append((s, "maxT", a))
            for s in s_list:
                big.extend((s, "sT", a, j) for j in range(units))
                small.append((s, "o", a))
        for s in s_list:
            small.append((s, "oT", a))
        for s in s_list:
            small.append((s, "proj", a))

    def per_slot(target, *keys):
        for s in range(SLOTS):
            for k in keys:
                target.append((s, *k))

    both = range(SLOTS)
    per_slot(small, ("mod",))
    per_slot(big, ("gate",))
    per_slot(small, ("ln", LN_L0))
    per_slot(small, ("qk0",), ("v0",))
    per_slot(small, ("s0",))
    per_slot(small, ("p0T",))
    per_slot(small, ("ev",))
    per_slot(small, ("router",))
    per_slot(big, ("hid0", 0), ("hid0", 1))
    per_slot(big, ("exp0",))
    per_slot(small, ("rT",))
    per_slot(small, ("g0",), ("out0",))
    per_slot(small, ("ln", LN_Q), ("ln", LN_KV))
    attention(both, A_L1)
    per_slot(small, ("ln", LN_2A))
    attention(both, A_2S)
    per_slot(small, ("ln", LN_2C))
    attention(both, A_2C)
    per_slot(small, ("ln", LN_2M))
    per_slot(big, ("hid2",))
    per_slot(small, ("mlp2",))
    per_slot(small, ("ln", LN_3A))
    attention(both, A_3W)
    per_slot(small, ("ln", LN_3C))
    attention(both, A_3C)
    per_slot(small, ("ln", LN_3M))
    per_slot(big, ("hid3", 0), ("hid3", 1))
    per_slot(small, ("mlp3",))
    return big, small


NBIG, NSMALL = 3, 2


class Ring:

    def __init__(self, keys, size):
        self.size = size
        self.use = {k: n for n, k in enumerate(keys)}
        assert len(self.use) == len(keys)
        self.per_round = [len(range(e, len(keys), size)) for e in range(size)]

    def at(self, key):
        n = self.use[key]
        return n % self.size, n // self.size


def chain_kernel(nc: bass.Bass, ins, out):
    big_keys, small_keys = psum_plan()
    big_ring, small_ring = Ring(big_keys, NBIG), Ring(small_keys, NSMALL)

    with ExitStack() as ctx:
        def sb(name, shape, dt=F32):
            return ctx.enter_context(nc.sbuf_tensor(name, shape, dt))

        def sem(name):
            return ctx.enter_context(nc.semaphore(name))

        def per_slot_sb(name, shape, dt=F32):
            return [sb(f"{name}{s}", shape, dt) for s in range(SLOTS)]

        W = sb("weights", [128, MAT_COLS])
        cols = sb("cols", [128, len(COLS)])
        ident = sb("ident", [128, 128])
        rows3 = sb("rows3", [3, len(ROWV), C], BF16)
        ones3 = sb("ones3", [3, 128], BF16)
        twos3 = sb("twos3", [3, 128], BF16)
        partmask = sb("partmask", [3, 2])
        minus_half = sb("minus_half", [128, NT])
        half_b = sb("half_b", [128, 4])

        x = per_slot_sb("x", [128, NT, C])
        cx = per_slot_sb("cx", [128, NT, C])
        cT = per_slot_sb("cT", [128, T])
        cond = per_slot_sb("cond", [128, 1])
        tc_ = per_slot_sb("tanh_cond", [128, 1])
        silu = per_slot_sb("silu_cond", [128, 1])
        condB = per_slot_sb("condB", [128, 128])
        siluB = per_slot_sb("siluB", [128, 128])
        mod = per_slot_sb("mod", [128, 21])
        half_anchor = per_slot_sb("half_anchor", [128, 7])
        gates = per_slot_sb("gates", [128, 5, C])
        stats = per_slot_sb("stats", [128, 2, NT, 6])
        mv = per_slot_sb("mv", [128, 2, NT, 2])
        ve = per_slot_sb("ve", [128, 2, NT])
        rstd = per_slot_sb("rstd", [128, 2, NT])
        xn = per_slot_sb("xn", [128, 2, NT, C])
        hT = per_slot_sb("hT", [128, T])
        kvT = per_slot_sb("kvT", [128, T])
        parts = per_slot_sb("parts", [128, PARTS, 2, T], BF16)
        resid = per_slot_sb("resid", [128, 2, T])
        Qs = per_slot_sb("Qs", [128, HP, T], BF16)
        Ks = per_slot_sb("Ks", [128, HP, T], BF16)
        V = per_slot_sb("V", [128, NT * H, D + 1])
        rowmax = per_slot_sb("rowmax", [128, NT, 2, HP])
        negmax = per_slot_sb("negmax", [16, 2, T], BF16)
        PT = per_slot_sb("PT", [128, H, NT, T])
        rden = per_slot_sb("rden", [128, NT * H])
        oT = per_slot_sb("oT", [128, T])
        upd = per_slot_sb("upd", [128, NT, C])
        m0 = per_slot_sb("m0", [128, NT])
        nm0 = per_slot_sb("nm0", [128, NT])
        z0 = per_slot_sb("z0", [128, NT])
        rl = per_slot_sb("rl", [128, NT, E3])
        rm = per_slot_sb("rm", [128, NT])
        qk0 = resid
        on = [resid[s][:, 0, :].rearrange("p (t c) -> p t c", t=NT) for s in range(SLOTS)]
        hid = [PT[s][:, 0:4, :, :].rearrange("p a b t -> p (a b) t") for s in range(SLOTS)]
        th = [PT[s][:, 4:8, :, :].rearrange("p a b t -> p (a b) t") for s in range(SLOTS)]
        p0 = [PT[s][:, 8, :, :] for s in range(SLOTS)]
        p0T = [PT[s][:, 9, :, :] for s in range(SLOTS)]
        NR = len(ROWV) * C
        rowf = PT[0][0:3].rearrange("p a b t -> p (a b t)")[:, 0:NR]
        rowr = PT[1][0:3].rearrange("p a b t -> p (a b t)")[:, 0:NR]

        s1 = sb("s1", [128, 2, 4, T])
        m8 = sb("m8", [128, 2, 2, 4, 8])
        ntop = sb("ntop", [128, 2, 4])
        e_all = sb("e_all", [128, 2, 4, T])
        e_rest = sb("e_rest", [128, 2, 4, T])
        ptop = sb("ptop", [128, 2, 4, T])

        BIG = [ctx.enter_context(nc.psum_tensor(f"big{e}", [128, 2, 512], F32)) for e in range(NBIG)]
        SMALL = [ctx.enter_context(nc.psum_tensor(f"small{e}", [128, 512], F32)) for e in range(NSMALL)]
        scratch = [nc.dram_tensor(f"parts_scratch{s}", (2, BLOCKS, 128, T), BF16, kind="Internal").ap()
                   for s in range(SLOTS)]

        big_full = [sem(f"big_full{e}") for e in range(NBIG)]
        big_free = [sem(f"big_free{e}") for e in range(NBIG)]
        small_full = [sem(f"small_full{e}") for e in range(NSMALL)]
        small_free = [sem(f"small_free{e}") for e in range(NSMALL)]
        cols_loaded, ident_loaded, rows_loaded, mask_loaded = (
            sem("cols_loaded"), sem("ident_loaded"), sem("rows_loaded"), sem("mask_loaded"))
        group_loaded = {g: sem(f"{g}_loaded") for g in MATS}
        const_set = sem("const_set")
        pool_const = sem("pool_const")
        passed = {e: sem(f"passed_{e}") for e in ("sp", "pe", "dve", "pool")}
        split_step = sem("split_step")
        rows_split = sem("rows_split")

        PER_SEQ = dict(
            loaded=64, stored=16, tanh_cond=1, silu_step=4, mod_step=2,
            bn_done=9, mv_done=9, ve_done=9, rstd_done=9, xn_done=9,
            softmax0_step=4, router_step=4, router_exp=1, tanh0_done=2, silu0_step=2, routed_step=2,
            updated_half=8, x_updated=8,
            part1_done=5, part2_done=5, parts_done=5, scratch_written=5 * 96, stacked=5 * 64,
            negmax_step=4, maxrow_loaded=4 * 64, rden_done=5, tanh3_done=1, swiglu_step=1,
        )
        S = {n: [sem(f"{n}{s}") for s in range(SLOTS)] for n in PER_SEQ}
        top_step = sem("top_step")
        e_done = sem("e_done")
        p_done = sem("p_done")

        CONSTS = 2 + SLOTS + 1

        block = ctx.enter_context(nc.Block())

        def w(name, lo=0, n=None):
            at, width = MAT_AT[name]
            return W[:, at + lo:at + (width if n is None else lo + n)]

        def col(name, n=1):
            return cols[:, COL[name]:COL[name] + n]

        def row(name):
            return rows3[:, ROW[name]:ROW[name] + 1, :].to_broadcast([3, NT, C])

        def of(name, s, it, k):
            assert 0 < k <= PER_SEQ[name], (name, k)
            return S[name][s], it * PER_SEQ[name] + k

        def big_filled(it, key):
            e, k = big_ring.at(key)
            return big_full[e], it * big_ring.per_round[e] + k + 1

        def big_is_free(it, key):
            e, k = big_ring.at(key)
            return big_free[e], it * big_ring.per_round[e] + k + 1

        def small_filled(it, key):
            e, k = small_ring.at(key)
            return small_full[e], it * small_ring.per_round[e] + k + 1

        def small_is_free(it, key):
            e, k = small_ring.at(key)
            return small_free[e], it * small_ring.per_round[e] + k + 1

        def big_taken(it, key):
            f, v = big_is_free(it, key)
            return f, v + 1

        def small_taken(it, key):
            f, v = small_is_free(it, key)
            return f, v + 1

        def tiles(it, free=(), taken=()):
            need = {}
            for keys, extra in ((free, 1), (taken, 2)):
                for key in keys:
                    ring, sems, ready = (small_ring, small_free, "s") if key in small_ring.use else (big_ring, big_free, "b")
                    e, k = ring.at(key)
                    need[ready, e] = max(need.get((ready, e), (0,))[0], k + extra), sems[e], ring.per_round[e]
            return [(f, it * n + k) for k, f, n in need.values()]

        def big(key):
            return BIG[big_ring.at(key)[0]]

        def small(key):
            return SMALL[small_ring.at(key)[0]]

        def big_freed(key):
            return big_free[big_ring.at(key)[0]]

        def small_freed(key):
            return small_free[small_ring.at(key)[0]]

        def big_ready(key):
            return big_full[big_ring.at(key)[0]]

        def small_ready(key):
            return small_full[small_ring.at(key)[0]]

        def nat(ap):
            return ap[:, 0:T].rearrange("p (t c) -> p t c", t=NT)

        @block.sync
        def _(sp):
            sp.dma_start(cols[:, :], ins["cols"]).then_inc(cols_loaded, 16)
            sp.dma_start(ident[:, :], ins["ident"]).then_inc(ident_loaded, 16)
            sp.dma_start(rowf, ins["rows"]).then_inc(rows_loaded, 16)
            sp.dma_start(partmask[:, :], ins["partmask"]).then_inc(mask_loaded, 16)

            def load_inputs(s, it):
                b = it * SLOTS + s
                sp.dma_start(x[s][:, :, :], ins["x"][bass.ds(b, 1)].rearrange("b (t p) c -> p (b t) c", p=128)).then_inc(S["loaded"][s], 16)
                sp.dma_start(cond[s][:, :], ins["condT"][bass.ds(b, 1)].rearrange("b p o -> p (b o)")).then_inc(S["loaded"][s], 16)
                sp.dma_start(cT[s][:, :], ins["ctxT"][bass.ds(b, 1)].rearrange("b p t -> p (b t)")).then_inc(S["loaded"][s], 16)
                sp.dma_start(cx[s][:, :, :], ins["ctx"][bass.ds(b, 1)].rearrange("b (t p) c -> p (b t) c", p=128)).then_inc(S["loaded"][s], 16)

            def stack(s, it, a):
                wr = S["scratch_written"][s]
                q_scr = scratch[s][0].rearrange("r c t -> c r t")
                k_scr = scratch[s][1].rearrange("r c t -> c r t")
                sp.wait_ge(*of("part1_done", s, it, a + 1))
                sp.dma_start(q_scr[:, 0:3], parts[s][:, 0:1, 0, :].to_broadcast([128, 3, T])).then_inc(wr, 16)
                sp.dma_start(k_scr[:, 5:6], parts[s][:, 0:1, 1, :]).then_inc(wr, 16)
                sp.wait_ge(*of("parts_done", s, it, a + 1))
                sp.dma_start(k_scr[:, 0:3], parts[s][:, 0:3, 1, :]).then_inc(wr, 16)
                sp.dma_start(k_scr[:, 3:5], parts[s][:, 0:2, 1, :]).then_inc(wr, 16)
                sp.dma_start(q_scr[:, 3:5], parts[s][:, 1:2, 0, :].to_broadcast([128, 2, T])).then_inc(wr, 16)
                sp.dma_start(q_scr[:, 5:6], parts[s][:, 2:3, 0, :]).then_inc(wr, 16)
                sp.wait_ge(*of("scratch_written", s, it, 96 * (a + 1)))
                for i, stacked in enumerate((Qs[s], Ks[s])):
                    for p in range(2):
                        src = scratch[s][i].rearrange("r (d p h) t -> p (r d) (h t)", p=2, d=D)[p]
                        dst = stacked[64 * p:64 * p + ROWS].rearrange("r h t -> r (h t)")
                        sp.dma_start(dst, src).then_inc(S["stacked"][s], 16)

            def max_rows(s, it, a):
                sp.wait_ge(*small_taken(it, (s, "maxT", a)))
                for part in range(2):
                    for p in range(2):
                        r = 64 * p + ROWS + part
                        sp.dma_start(Qs[s][r:r + 1, :, :], negmax[s][HP * p:HP * p + HP, part, :]).then_inc(S["maxrow_loaded"][s], 16)

            with sp.Fori(0, B // SLOTS) as it:
                for s in range(SLOTS):
                    load_inputs(s, it)
                for a in range(5):
                    for s in range(SLOTS):
                        stack(s, it, a)
                    if a != A_3C:
                        for s in range(SLOTS):
                            max_rows(s, it, a)
                for s in range(SLOTS):
                    b = it * SLOTS + s
                    sp.wait_ge(*of("x_updated", s, it, 8))
                    sp.sem_inc(passed["sp"], 1)
                    sp.dma_start(out[bass.ds(b, 1)].rearrange("b (t p) c -> p (b t) c", p=128), x[s][:, :, :]).then_inc(S["stored"][s], 16)
                for s in range(SLOTS):
                    sp.wait_ge(*of("stored", s, it, 16))
                sp.sem_inc(passed["sp"], 1)

        @block.tensor
        def _(pe):
            def turn(key, s, src, it, taken=()):
                for t in tiles(it, free=[key], taken=taken):
                    pe.wait_ge(*t)
                for t in range(NT):
                    mm = pe.transpose(small(key)[:, t * 128:(t + 1) * 128], src(t), ident[:, :])
                mm.then_inc(small_ready(key), 1)

            def bias_rows(dst, name, ones, start=True):
                return pe.matmul(dst, ones[:, :], row(name), start=start, stop=False, skip_group_check=True)

            def natural(key, it, terms, name, ones=None, taken=()):
                for t in tiles(it, free=[key], taken=taken):
                    pe.wait_ge(*t)
                dst = small(key)
                bias_rows(nat(dst), name, ones3 if ones is None else ones)
                for t in range(NT):
                    for i, (a, m) in enumerate(terms):
                        mm = pe.matmul(dst[:, t * 128:(t + 1) * 128], a[:, t * 128:(t + 1) * 128], m, start=False,
                                       stop=(i == len(terms) - 1), skip_group_check=True)
                mm.then_inc(small_ready(key), 1)

            def mods(s, it):
                key = (s, "mod")
                pe.wait_ge(*of("silu_step", s, it, 2))
                pe.wait_ge(*small_is_free(it, key))
                for i in range(14):
                    pe.matmul(small(key)[:, i:i + 1], w("mod", i * C, C), silu[s][:, :], start=True, stop=True)
                for i in range(7):
                    m = w(f"l0_w1_{i // 2}_2", (i % 2) * C, C) if i < 6 else w("l0_g1_2")
                    mm = pe.matmul(small(key)[:, 14 + i:15 + i], m, cond[s][:, :], start=True, stop=True)
                mm.then_inc(small_ready(key), 1)

            def gate_rows(s, it):
                key = (s, "gate")
                pe.wait_ge(*of("silu_step", s, it, 4))
                pe.wait_ge(*big_is_free(it, key))
                for bank, lo, n in ((0, 0, 2), (1, 2, 3)):
                    dst = big(key)[:, bank, 0:n * C]
                    pe.matmul(dst, ones3[:, :], rows3[:, ROW["gate0"] + lo:ROW["gate0"] + lo + n, :], start=True, stop=False, skip_group_check=True)
                    mm = pe.matmul(dst, siluB[s][:, :], w("gate", lo * C, n * C), start=False, stop=True, skip_group_check=True)
                mm.then_inc(big_ready(key), 1)

            def norm_turn(s, it, n):
                pe.wait_ge(*of("xn_done", s, it, n + 1))
                turn((s, "ln", n), s, lambda t: xn[s][:, n % 2, t, :], it)

            def l0_qkv(s, it):
                key = (s, "qk0")
                for t in tiles(it, free=[key], taken=[(s, "ln", LN_L0)]):
                    pe.wait_ge(*t)
                pe.matmul(small(key)[:, 0:T], w("l0_q"), hT[s][:, :], start=True, stop=True)
                pe.matmul(small(key)[:, T:2 * T], w("l0_k"), cT[s][:, :], start=True, stop=True).then_inc(small_ready(key), 1)
                key = (s, "v0")
                pe.wait_ge(*small_is_free(it, key))
                for t in range(NT):
                    mm = pe.matmul(small(key)[:, t * C:(t + 1) * C], cT[s][:, t * 128:(t + 1) * 128], w("l0_v"), start=True, stop=True)
                mm.then_inc(small_ready(key), 1)

            def l0_scores(s, it):
                key = (s, "s0")
                for t in tiles(it, free=[key], taken=[(s, "qk0")]):
                    pe.wait_ge(*t)
                for t in range(NT):
                    mm = pe.matmul(small(key)[:, t * T:(t + 1) * T], qk0[s][:, 0, t * 128:(t + 1) * 128], qk0[s][:, 1, :], start=True, stop=True)
                mm.then_inc(small_ready(key), 1)

            def l0_probs_turn(s, it):
                key = (s, "p0T")
                pe.wait_ge(*of("softmax0_step", s, it, 4))
                pe.wait_ge(*small_is_free(it, key))
                for k in range(NT):
                    for t in range(NT):
                        mm = pe.transpose(small(key)[:, k * T + t * 128:k * T + (t + 1) * 128], p0[s][:, t, k * 128:(k + 1) * 128], ident[:, :])
                mm.then_inc(small_ready(key), 1)

            def l0_evidence(s, it):
                key = (s, "ev")
                for t in tiles(it, free=[key], taken=[(s, "v0"), (s, "p0T")]):
                    pe.wait_ge(*t)
                for k in range(NT):
                    mm = pe.matmul(small(key)[:, 0:T], upd[s][:, k, :], p0T[s][:, k, :], start=(k == 0), stop=(k == NT - 1))
                mm.then_inc(small_ready(key), 1)

            def l0_router(s, it):
                key = (s, "router")
                for t in tiles(it, free=[key], taken=[(s, "ev")]):
                    pe.wait_ge(*t)
                rw = w("l0_router")
                for t in range(NT):
                    dst = small(key)[:, 4 * t:4 * t + E3]
                    tt = slice(t * 128, (t + 1) * 128)
                    pe.matmul(dst, ones3[:, :], rows3[:, ROW["router"], 0:E3], start=True, stop=False, skip_group_check=True)
                    pe.matmul(dst, hT[s][:, tt], rw[:, 0:E3], start=False, stop=False, skip_group_check=True)
                    pe.matmul(dst, kvT[s][:, tt], rw[:, E3:2 * E3], start=False, stop=False, skip_group_check=True)
                    mm = pe.matmul(dst, condB[s][:, :], rw[:, 2 * E3:3 * E3], start=False, stop=True, skip_group_check=True)
                mm.then_inc(small_ready(key), 1)

            def l0_hidden(s, it, half):
                key = (s, "hid0", half)
                pe.wait_ge(*big_is_free(it, key))
                for i in range(4 * half, min(4 * half + 4, 7)):
                    n = i - 4 * half
                    dst = big(key)[:, n // 2, (n % 2) * T:(n % 2 + 1) * T]
                    for j, act in enumerate((hT[s], kvT[s])):
                        m = w(f"l0_w1_{i // 2}_{j}", (i % 2) * C, C) if i < 6 else w(f"l0_g1_{j}")
                        mm = pe.matmul(dst, m, act[:, :], start=(j == 0), stop=(j == 1))
                mm.then_inc(big_ready(key), 1)

            def l0_experts(s, it):
                key = (s, "exp0")
                for t in tiles(it, free=[key], taken=[(s, "hid0", 1)]):
                    pe.wait_ge(*t)
                for t in range(NT):
                    pe.matmul(big(key)[:, t, 0:E3 * C], twos3[:, :], rows3[:, ROW["e0"]:ROW["e0"] + E3, :], start=True, stop=False, skip_group_check=True)
                    for e in range(E3):
                        for c in range(2):
                            mm = pe.matmul(big(key)[:, t, e * C:(e + 1) * C], hid[s][:, 2 * e + c, t * 128:(t + 1) * 128], w(f"l0_w2_{e}_{c}"),
                                           start=False, stop=(c == 1), skip_group_check=True)
                mm.then_inc(big_ready(key), 1)

            def l0_routed_turn(s, it):
                pe.wait_ge(*big_taken(it, (s, "exp0")))
                turn((s, "rT"), s, lambda t: upd[s][:, t, :], it)

            def l0_out(s, it):
                natural((s, "g0"), it, [(hid[s][:, 6, :], w("l0_g2"))], "g2", twos3)
                natural((s, "out0"), it, [(oT[s], w("l0_out"))], "out", taken=[(s, "rT")])

            def qkv(s, it, a):
                kv = {A_L1: kvT, A_2S: hT, A_2C: cT, A_3W: hT, A_3C: cT}[a][s]
                key = (s, "qk", a)
                norms = [(s, "ln", NORMS_FOR[a])] + [(s, "ln", LN_Q)] * (a == A_L1)
                for t in tiles(it, free=[key], taken=norms):
                    pe.wait_ge(*t)
                pe.matmul(small(key)[:, 0:T], w(f"q{a}"), hT[s][:, :], start=True, stop=True)
                pe.matmul(small(key)[:, T:2 * T], w(f"k{a}"), kv[:, :], start=True, stop=True).then_inc(small_ready(key), 1)
                natural((s, "v", a), it, [(kv, w(f"v{a}"))], f"bv{a}")

            def scores(s, it, a):
                pe.wait_ge(*of("stacked", s, it, 64 * (a + 1)))
                for j in range(HP):
                    key = (s, "s", a, j)
                    pe.wait_ge(*big_is_free(it, key))
                    for p in range(2):
                        r = slice(64 * p, 64 * p + ROWS)
                        for t in range(NT):
                            mm = pe.matmul(big(key)[:, p, t * T:(t + 1) * T], Qs[s][r, j, t * 128:(t + 1) * 128], Ks[s][r, j, :], start=True, stop=True)
                    mm.then_inc(big_ready(key), 1)

            def scores_window(s, it, a, turned, rows):
                for u in range(2):
                    key = (s, "sT" if turned else "s", a, u)
                    pe.wait_ge(*big_is_free(it, key))
                    pe.sem_inc(passed["pe"], 1)
                    for p in range(2):
                        r = slice(64 * p, 64 * p + rows)
                        for i in range(4):
                            for wdw in range(T // WIN):
                                q = Qs[s][r, 4 * u + i, wdw * WIN:(wdw + 1) * WIN]
                                k = Ks[s][r, 4 * u + i, wdw * WIN:(wdw + 1) * WIN]
                                c0 = ((wdw // 2) * 4 + i) * WIN
                                dst = big(key)[64 * (wdw % 2):64 * (wdw % 2) + 64, p, c0:c0 + WIN]
                                mm = pe.matmul(dst, k if turned else q, q if turned else k, start=True, stop=True)
                    mm.then_inc(big_ready(key), 1)
                    if turned and u >= 1:
                        values_window(s, it, a, u - 1)
                if turned:
                    values_window(s, it, a, 1)

            def max_turn(s, it, a):
                key = (s, "maxT", a)
                pe.wait_ge(*big_taken(it, (s, "s", a, 1 if a == A_3W else HP - 1)))
                pe.wait_ge(*small_is_free(it, key))
                for t in range(NT):
                    mm = pe.transpose(small(key)[0:16, t * 128:(t + 1) * 128], rowmax[s][:, t].rearrange("p a h -> p (a h)"), ident[:, :])
                mm.then_inc(small_ready(key), 1)

            def values(s, it, a, j):
                key = (s, "o", a)
                probs = (s, "topT", j) if a == A_3C else (s, "sT", a, j)
                for t in tiles(it, free=[key] * (j == 0), taken=[probs] + [(s, "v", a)] * (j == 0)):
                    pe.wait_ge(*t)
                for h in (2 * j, 2 * j + 1):
                    for t in range(NT):
                        c0 = (t * H + h) * (D + 1)
                        for k in range(NT):
                            mm = pe.matmul(small(key)[:, c0:c0 + D + 1], PT[s][:, h, k, t * 128:(t + 1) * 128], V[s][:, k * H + h, :],
                                           start=(k == 0), stop=(k == NT - 1))
                if j == HP - 1:
                    mm.then_inc(small_ready(key), 1)

            def values_window(s, it, a, u):
                key = (s, "o", a)
                for t in tiles(it, free=[key] * (u == 0), taken=[(s, "sT", a, u)] + [(s, "v", a)] * (u == 0)):
                    pe.wait_ge(*t)
                pe.sem_inc(passed["pe"], 1)
                for i in range(4):
                    for p in range(2):
                        h = 2 * (4 * u + i) + p
                        for wdw in range(T // WIN):
                            r = slice(64 * (wdw % 2), 64 * (wdw % 2) + 64)
                            c0 = ((wdw // 2) * H + h) * (D + 1)
                            probs = PT[s][r, u * 2 + p].rearrange("p k t -> p (k t)")
                            b0 = ((wdw // 2) * 4 + i) * WIN
                            mm = pe.matmul(small(key)[r, c0:c0 + D + 1], probs[:, b0:b0 + WIN], V[s][r, (wdw // 2) * H + h, :],
                                           start=True, stop=True)
                if u == 1:
                    mm.then_inc(small_ready(key), 1)

            def probs_values(s, it, a):
                pe.wait_ge(*of("maxrow_loaded", s, it, 64 * (a + 1)))
                for j in range(HP + 1):
                    if j < HP:
                        key = (s, "sT", a, j)
                        pe.wait_ge(*big_is_free(it, key))
                        for p in range(2):
                            r = slice(64 * p, 64 * p + ROWSM)
                            for k in range(NT):
                                mm = pe.matmul(big(key)[:, p, k * T:(k + 1) * T], Ks[s][r, j, k * 128:(k + 1) * 128], Qs[s][r, j, :], start=True, stop=True)
                        mm.then_inc(big_ready(key), 1)
                    if j >= 1:
                        values(s, it, a, j - 1)

            def top_k(s, it):
                pe.wait_ge(*of("stacked", s, it, 64 * (A_3C + 1)))
                for j in range(HP + TURN_LAG + 1):
                    if j < HP:
                        key = (s, "top", j)
                        pe.wait_ge(*big_is_free(it, key))
                        for p in range(2):
                            r = slice(64 * p, 64 * p + ROWS)
                            for t in range(NT):
                                mm = pe.matmul(big(key)[:, p, t * T:(t + 1) * T], Qs[s][r, j, t * 128:(t + 1) * 128], Ks[s][r, j, :], start=True, stop=True)
                        mm.then_inc(big_ready(key), 1)
                    if TURN_LAG <= j < HP + TURN_LAG:
                        key = (s, "topT", j - TURN_LAG)
                        g = s * HP + j - TURN_LAG
                        pe.wait_ge(p_done, it * (SLOTS * HP) + g + 1)
                        pe.wait_ge(*big_is_free(it, key))
                        for p in range(2):
                            for k in range(NT):
                                for t in range(NT):
                                    c0 = k * T + t * 128
                                    mm = pe.transpose(big(key)[:, p, c0:c0 + 128], ptop[:, g % 2, 2 * p + t, k * 128:(k + 1) * 128], ident[:, :])
                        mm.then_inc(big_ready(key), 1)
                    if j >= TURN_LAG + 1:
                        values(s, it, A_3C, j - TURN_LAG - 1)

            def turn_output(s, it, a):
                turn((s, "oT", a), s, lambda t: on[s][:, t, :], it, taken=[(s, "o", a)])

            def project(s, it, a):
                natural((s, "proj", a), it, [(oT[s], w(f"o{a}"))], f"bo{a}", taken=[(s, "oT", a)])

            def hidden(s, it, key, n, mat, lo):
                pe.wait_ge(*small_taken(it, (s, "ln", n)))
                pe.wait_ge(*big_is_free(it, key))
                for i in range(4):
                    mm = pe.matmul(big(key)[:, i // 2, (i % 2) * T:(i % 2 + 1) * T], w(mat, lo + i * C, C), hT[s][:, :], start=True, stop=True)
                mm.then_inc(big_ready(key), 1)

            def mlp_out(s, it, key, done, mat, name, ones):
                pe.wait_ge(*big_taken(it, done))
                natural(key, it, [(hid[s][:, i, :], w(mat, i * C, C)) for i in range(4)], name, ones)

            def attention(it, a):
                for s in range(SLOTS):
                    qkv(s, it, a)
                if a == A_3C:
                    for s in range(SLOTS):
                        top_k(s, it)
                elif a == A_3W:
                    for s in range(SLOTS):
                        pe.wait_ge(*of("stacked", s, it, 64 * (a + 1)))
                        pe.sem_inc(passed["pe"], 1)
                        scores_window(s, it, a, False, ROWS)
                    for s in range(SLOTS):
                        max_turn(s, it, a)
                    for s in range(SLOTS):
                        pe.wait_ge(*of("maxrow_loaded", s, it, 64 * 4))
                        pe.sem_inc(passed["pe"], 1)
                        scores_window(s, it, a, True, ROWSM)
                else:
                    for s in range(SLOTS):
                        scores(s, it, a)
                    for s in range(SLOTS):
                        max_turn(s, it, a)
                    for s in range(SLOTS):
                        probs_values(s, it, a)
                for s in range(SLOTS):
                    turn_output(s, it, a)
                for s in range(SLOTS):
                    project(s, it, a)

            pe.wait_ge(ident_loaded, 16)
            pe.wait_ge(rows_split, 1)
            pe.wait_ge(const_set, CONSTS)
            both = range(SLOTS)
            with pe.Fori(0, B // SLOTS) as it:
                pe.wait_ge(group_loaded["mod"], 16)
                pe.wait_ge(group_loaded["l0"], 16)
                for s in both:
                    mods(s, it)
                for s in both:
                    gate_rows(s, it)
                for s in both:
                    norm_turn(s, it, LN_L0)
                pe.wait_ge(group_loaded["early"], 16)
                for s in both:
                    l0_qkv(s, it)
                for s in both:
                    l0_scores(s, it)
                for s in both:
                    l0_probs_turn(s, it)
                for s in both:
                    l0_evidence(s, it)
                for s in both:
                    l0_router(s, it)
                for s in both:
                    l0_hidden(s, it, 0)
                    l0_hidden(s, it, 1)
                for s in both:
                    l0_experts(s, it)
                for s in both:
                    l0_routed_turn(s, it)
                for s in both:
                    l0_out(s, it)
                for s in both:
                    norm_turn(s, it, LN_Q)
                    norm_turn(s, it, LN_KV)
                pe.wait_ge(group_loaded["l1"], 16)
                attention(it, A_L1)
                pe.wait_ge(group_loaded["l2"], 16)
                for s in both:
                    norm_turn(s, it, LN_2A)
                attention(it, A_2S)
                for s in both:
                    norm_turn(s, it, LN_2C)
                attention(it, A_2C)
                for s in both:
                    norm_turn(s, it, LN_2M)
                for s in both:
                    hidden(s, it, (s, "hid2"), LN_2M, "l2_w1", 0)
                for s in both:
                    mlp_out(s, it, (s, "mlp2"), (s, "hid2"), "l2_w2", "l2_b2", ones3)
                pe.wait_ge(group_loaded["l3"], 16)
                for s in both:
                    norm_turn(s, it, LN_3A)
                attention(it, A_3W)
                for s in both:
                    norm_turn(s, it, LN_3C)
                attention(it, A_3C)
                for s in both:
                    norm_turn(s, it, LN_3M)
                for s in both:
                    hidden(s, it, (s, "hid3", 0), LN_3M, "l3_w1", 0)
                    hidden(s, it, (s, "hid3", 1), LN_3M, "l3_w1", HID)
                for s in both:
                    mlp_out(s, it, (s, "mlp3"), (s, "hid3", 1), "l3_w2", "l3_b2", twos3)

        @block.scalar
        def _(act):
            def tanh_cond(s, it):
                act.wait_ge(*of("loaded", s, it, 64))
                nc.scalar.activation(tc_[s][:, :], cond[s][:, :], ACT.Tanh, scale=0.5).then_inc(S["tanh_cond"][s], 1)

            def gates_out(s, it):
                key = (s, "gate")
                act.wait_ge(*big_filled(it, key))
                nc.scalar.copy(gates[s][:, 0:2, :].rearrange("p g c -> p (g c)"), big(key)[:, 0, 0:2 * C])
                nc.scalar.copy(gates[s][:, 2:5, :].rearrange("p g c -> p (g c)"), big(key)[:, 1, 0:3 * C]).then_inc(big_freed(key), 1)

            def take(s, it, key, dst, src):
                act.wait_ge(*small_filled(it, key))
                nc.scalar.copy(dst, src).then_inc(small_freed(key), 1)

            def norm_out(s, it, n):
                key = (s, "ln", n)
                if n == LN_L0:
                    sc, sh = col("ln_g"), col("ln_b")
                elif n == LN_2C:
                    sc, sh = col("n2_g"), col("n2_b")
                else:
                    m = {LN_Q: "q", LN_KV: "kv", LN_2A: "l2a", LN_2M: "l2m", LN_3A: "l3a", LN_3C: "l3c", LN_3M: "l3m"}[n]
                    sc, sh = mod[s][:, SC[m]:SC[m] + 1], mod[s][:, SH[m]:SH[m] + 1]
                act.wait_ge(*small_filled(it, key))
                dst, src = (kvT if n == LN_KV else hT)[s], small(key)
                if n == LN_3A:
                    nc.scalar.activation(dst[:, 0:T - SHIFT], src[:, SHIFT:T], ACT.Identity, scale=sc, bias=sh)
                    nc.scalar.activation(dst[:, T - SHIFT:T], src[:, 0:SHIFT], ACT.Identity, scale=sc, bias=sh).then_inc(small_freed(key), 1)
                else:
                    nc.scalar.activation(dst[:, :], src[:, 0:T], ACT.Identity, scale=sc, bias=sh).then_inc(small_freed(key), 1)

            def l0_exp(s, it):
                key = (s, "s0")
                act.wait_ge(*of("softmax0_step", s, it, 2))
                for t in range(NT):
                    last = nc.scalar.activation(p0[s][:, t, :], small(key)[:, t * T:(t + 1) * T], ACT.Exp, scale=SCALE0,
                                                bias=nm0[s][:, t:t + 1], accum_out=z0[s][:, t:t + 1])
                last.then_inc(small_freed(key), 1)

            def l0_router_exp(s, it):
                act.wait_ge(*small_taken(it, (s, "router")))
                nc.scalar.activation(rl[s][:, :, :], rl[s][:, :, :], ACT.Exp).then_inc(S["router_exp"][s], 1)

            def l0_tanh(s, it, half):
                key = (s, "hid0", half)
                if half == 0:
                    act.wait_ge(*of("mod_step", s, it, 2))
                act.wait_ge(*big_filled(it, key))
                for i in range(4 * half, min(4 * half + 4, 7)):
                    n = i - 4 * half
                    last = nc.scalar.activation(th[s][:, i, :], big(key)[:, n // 2, (n % 2) * T:(n % 2 + 1) * T], ACT.Tanh,
                                                scale=0.5, bias=half_anchor[s][:, i:i + 1])
                last.then_inc(S["tanh0_done"][s], 1)

            def l0_gate_tanh(s, it):
                key = (s, "g0")
                act.wait_ge(*small_filled(it, key))
                nc.scalar.activation(th[s][:, 7, :], small(key)[:, 0:T], ACT.Tanh, scale=0.25).then_inc(small_freed(key), 1)

            def first_parts(s, it, a):
                key = (s, "qk", a)
                act.wait_ge(*small_filled(it, key))
                nc.scalar.activation(parts[s][:, 0, 0, :], small(key)[:, 0:T], ACT.Identity, bias=col(f"bq{a}"))
                nc.scalar.activation(parts[s][:, 0, 1, :], small(key)[:, T:2 * T], ACT.Identity, bias=col(f"bk{a}")).then_inc(S["part1_done"][s], 1)
                key = (s, "v", a)
                take(s, it, key, V[s][:, :, 0:D], small(key)[:, 0:T].rearrange("p (h d) -> p h d", d=D))

            def probabilities(s, it, a, j):
                key = (s, "sT", a, j)
                act.wait_ge(*big_filled(it, key))
                nc.scalar.activation(PT[s][:, 2 * j:2 * j + 2].rearrange("p a b t -> p a (b t)"), big(key)[:, :, :], ACT.Exp,
                                     scale=SCALE).then_inc(big_freed(key), 1)

            def output_out(s, it, a):
                key = (s, "oT", a)
                if a == A_3W:
                    act.wait_ge(*small_filled(it, key))
                    nc.scalar.copy(oT[s][:, SHIFT:T], small(key)[:, 0:T - SHIFT])
                    nc.scalar.copy(oT[s][:, 0:SHIFT], small(key)[:, T - SHIFT:T]).then_inc(small_freed(key), 1)
                else:
                    take(s, it, key, oT[s][:, :], small(key)[:, 0:T])

            def top_exp(s, it):
                def take_turned(j):
                    key = (s, "topT", j)
                    act.wait_ge(*big_filled(it, key))
                    nc.scalar.copy(PT[s][:, 2 * j:2 * j + 2].rearrange("p a b t -> p a (b t)"), big(key)[:, :, :]).then_inc(big_freed(key), 1)

                for j in range(HP + TURN_LAG):
                    if j < HP:
                        key = (s, "top", j)
                        g = s * HP + j
                        act.wait_ge(top_step, it * (SLOTS * HP * 4) + 4 * g + 2)
                        if g >= 2:
                            act.wait_ge(p_done, it * (SLOTS * HP) + g - 1)
                        for i in range(4):
                            last = nc.scalar.activation(e_all[:, g % 2, i, :], big(key)[:, i // 2, (i % 2) * T:(i % 2 + 1) * T], ACT.Exp,
                                                        scale=SCALE, bias=ntop[:, g % 2, i:i + 1])
                        last.then_inc(big_freed(key), 1)
                        act.wait_ge(top_step, it * (SLOTS * HP * 4) + 4 * g + 4)
                        for i in range(4):
                            last = nc.scalar.activation(e_rest[:, g % 2, i, :], s1[:, g % 2, i, :], ACT.Exp,
                                                        scale=SCALE, bias=ntop[:, g % 2, i:i + 1])
                        last.then_inc(e_done, 1)
                    if j >= TURN_LAG:
                        take_turned(j - TURN_LAG)

            def gelu(s, it):
                key = (s, "hid2")
                act.wait_ge(*big_filled(it, key))
                for i in range(4):
                    last = nc.scalar.activation(hid[s][:, i, :], big(key)[:, i // 2, (i % 2) * T:(i % 2 + 1) * T], ACT.Gelu_apprx_tanh,
                                                bias=col(f"l2_b1_{i}"))
                last.then_inc(big_freed(key), 1)

            def swiglu_tanh(s, it):
                key = (s, "hid3", 0)
                act.wait_ge(*big_filled(it, key))
                for i in range(4):
                    last = nc.scalar.activation(th[s][:, i, :], big(key)[:, i // 2, (i % 2) * T:(i % 2 + 1) * T], ACT.Tanh,
                                                scale=0.5, bias=half_b[:, i:i + 1])
                last.then_inc(S["tanh3_done"][s], 1)

            def attention(it, a):
                for s in both:
                    first_parts(s, it, a)
                if a == A_3C:
                    for s in both:
                        top_exp(s, it)
                else:
                    for s in both:
                        for j in range(2 if a == A_3W else HP):
                            probabilities(s, it, a, j)
                for s in both:
                    output_out(s, it, a)

            both = range(SLOTS)
            for g in MATS:
                lo = GROUP_AT[g]
                n = sum(c for _, c in MATS[g])
                act.dma_start(W[:, lo:lo + n], ins["mats"][:, lo:lo + n]).then_inc(group_loaded[g], 16)
            act.wait_ge(cols_loaded, 16)
            act.wait_ge(const_set, CONSTS)
            with act.Fori(0, B // SLOTS) as it:
                for s in both:
                    tanh_cond(s, it)
                for s in both:
                    gates_out(s, it)
                for s in both:
                    norm_out(s, it, LN_L0)
                for s in both:
                    take(s, it, (s, "qk0"), qk0[s][:, :, :].rearrange("p a t -> p (a t)"), small((s, "qk0"))[:, :])
                    take(s, it, (s, "v0"), upd[s][:, :, :], nat(small((s, "v0"))))
                for s in both:
                    l0_exp(s, it)
                for s in both:
                    take(s, it, (s, "p0T"), p0T[s][:, :, :].rearrange("p k t -> p (k t)"), small((s, "p0T"))[:, :])
                for s in both:
                    take(s, it, (s, "ev"), kvT[s][:, :], small((s, "ev"))[:, 0:T])
                for s in both:
                    l0_router_exp(s, it)
                for s in both:
                    l0_tanh(s, it, 0)
                    l0_tanh(s, it, 1)
                for s in both:
                    take(s, it, (s, "rT"), oT[s][:, :], small((s, "rT"))[:, 0:T])
                for s in both:
                    l0_gate_tanh(s, it)
                for s in both:
                    norm_out(s, it, LN_Q)
                    norm_out(s, it, LN_KV)
                attention(it, A_L1)
                for s in both:
                    norm_out(s, it, LN_2A)
                attention(it, A_2S)
                for s in both:
                    norm_out(s, it, LN_2C)
                attention(it, A_2C)
                for s in both:
                    norm_out(s, it, LN_2M)
                for s in both:
                    gelu(s, it)
                for s in both:
                    norm_out(s, it, LN_3A)
                attention(it, A_3W)
                for s in both:
                    norm_out(s, it, LN_3C)
                attention(it, A_3C)
                for s in both:
                    norm_out(s, it, LN_3M)
                for s in both:
                    swiglu_tanh(s, it)

        @block.vector
        def _(dve):
            def cond_silu(s, it):
                dve.wait_ge(*of("tanh_cond", s, it, 1))
                nc.vector.scalar_tensor_tensor(out=silu[s][:, :], in0=tc_[s][:, :], scalar=1.0, in1=cond[s][:, :],
                                               op0=ALU.add, op1=ALU.mult).then_inc(S["silu_step"][s], 1)
                dve.wait_ge(*of("silu_step", s, it, 1))
                nc.vector.tensor_scalar(silu[s][:, :], silu[s][:, :], 0.5, None, ALU.mult).then_inc(S["silu_step"][s], 1)
                nc.vector.tensor_copy(condB[s][:, :], cond[s][:, 0:1].to_broadcast([128, 128])).then_inc(S["silu_step"][s], 1)
                dve.wait_ge(*of("silu_step", s, it, 2))
                nc.vector.tensor_copy(siluB[s][:, :], silu[s][:, 0:1].to_broadcast([128, 128])).then_inc(S["silu_step"][s], 1)

            def mods_out(s, it):
                key = (s, "mod")
                dve.wait_ge(*small_filled(it, key))
                nc.vector.tensor_tensor(mod[s][:, :], small(key)[:, 0:21], col("mod0", 21), ALU.add).then_inc(small_freed(key), 1)
                dve.wait_ge(*small_taken(it, key))
                nc.vector.tensor_scalar(mod[s][:, 0:7], mod[s][:, 0:7], 1.0, None, ALU.add).then_inc(S["mod_step"][s], 1)
                nc.vector.tensor_scalar(half_anchor[s][:, :], mod[s][:, 14:21], 0.5, None, ALU.mult).then_inc(S["mod_step"][s], 1)

            def norm_stats(s, it, n):
                src = cx if n == LN_KV else x
                if n == LN_L0:
                    dve.wait_ge(*of("loaded", s, it, 64))
                elif n != LN_KV:
                    dve.wait_ge(*of("x_updated", s, it, UPDATES_BEFORE[n]))
                for t in range(NT):
                    last = nc.vector.bn_stats(stats[s][:, n % 2, t, :], src[s][:, t, :])
                last.then_inc(S["bn_done"][s], 1)
                dve.wait_ge(*of("bn_done", s, it, n + 1))
                dve.sem_inc(passed["dve"], 1)
                for t in range(NT):
                    last = nc.vector.bn_aggr(mv[s][:, n % 2, t, :], stats[s][:, n % 2, t, :])
                last.then_inc(S["mv_done"][s], 1)

            def norm_apply(s, it, n):
                src = cx if n == LN_KV else x
                dve.wait_ge(*of("rstd_done", s, it, n + 1))
                for t in range(NT):
                    last = nc.vector.tensor_scalar(xn[s][:, n % 2, t, :], src[s][:, t, :], mv[s][:, n % 2, t, 0:1],
                                                   rstd[s][:, n % 2, t:t + 1], ALU.subtract, ALU.mult)
                last.then_inc(S["xn_done"][s], 1)

            def l0_max(s, it):
                key = (s, "s0")
                dve.wait_ge(*small_filled(it, key))
                nc.vector.tensor_reduce(m0[s][:, :], small(key)[:, :].rearrange("p (t k) -> p t k", t=NT), AX_X, ALU.max)\
                    .then_inc(S["softmax0_step"][s], 1)
                dve.wait_ge(*of("softmax0_step", s, it, 1))
                nc.vector.tensor_scalar(nm0[s][:, :], m0[s][:, :], -SCALE0, None, ALU.mult).then_inc(S["softmax0_step"][s], 1)

            def l0_normalise(s, it):
                dve.wait_ge(*small_taken(it, (s, "s0")))
                nc.vector.reciprocal(m0[s][:, :], z0[s][:, :]).then_inc(S["softmax0_step"][s], 1)
                dve.wait_ge(*of("softmax0_step", s, it, 3))
                for t in range(NT):
                    last = nc.vector.tensor_scalar(p0[s][:, t, :], p0[s][:, t, :], m0[s][:, t:t + 1], None, ALU.mult)
                last.then_inc(S["softmax0_step"][s], 1)

            def l0_router_max(s, it):
                key = (s, "router")
                dve.wait_ge(*small_filled(it, key))
                logits = small(key)[:, 0:4 * NT].rearrange("p (t e) -> p t e", e=4)[:, :, 0:E3]
                nc.vector.tensor_reduce(rm[s][:, :], logits, AX_X, ALU.max).then_inc(S["router_step"][s], 1)
                dve.wait_ge(*of("router_step", s, it, 1))
                nc.vector.tensor_tensor(rl[s][:, :, :], logits, rm[s][:, :].unsqueeze(2).to_broadcast([128, NT, E3]), ALU.subtract)\
                    .then_inc(small_freed(key), 1)

            def l0_router_norm(s, it):
                dve.wait_ge(*of("router_exp", s, it, 1))
                nc.vector.tensor_reduce(rm[s][:, :], rl[s][:, :, :], AX_X, ALU.add).then_inc(S["router_step"][s], 1)
                dve.wait_ge(*of("router_step", s, it, 2))
                nc.vector.reciprocal(rm[s][:, :], rm[s][:, :]).then_inc(S["router_step"][s], 1)
                dve.wait_ge(*of("router_step", s, it, 3))
                nc.vector.scalar_tensor_tensor(out=rl[s][:, :, :], in0=rl[s][:, :, :], scalar=0.5,
                                               in1=rm[s][:, :].unsqueeze(2).to_broadcast([128, NT, E3]),
                                               op0=ALU.mult, op1=ALU.mult).then_inc(S["router_step"][s], 1)

            def l0_silu(s, it, half):
                key = (s, "hid0", half)
                lo, hi = 4 * half, min(4 * half + 4, 7)
                dve.wait_ge(*of("tanh0_done", s, it, half + 1))
                nc.vector.tensor_scalar(th[s][:, lo:hi, :], th[s][:, lo:hi, :], 1.0, None, ALU.add).then_inc(S["silu0_step"][s], 1)
                dve.wait_ge(*of("silu0_step", s, it, half + 1))
                for i in range(lo, hi):
                    n = i - lo
                    last = nc.vector.scalar_tensor_tensor(out=hid[s][:, i, :], in0=big(key)[:, n // 2, (n % 2) * T:(n % 2 + 1) * T],
                                                          scalar=mod[s][:, 14 + i:15 + i], in1=th[s][:, i, :], op0=ALU.add, op1=ALU.mult)
                last.then_inc(big_freed(key), 1)

            def l0_route(s, it):
                key = (s, "exp0")
                dve.wait_ge(*of("router_step", s, it, 4))
                dve.wait_ge(*big_filled(it, key))
                for e in range(E3):
                    if e:
                        dve.wait_ge(*of("routed_step", s, it, e))
                    for t in range(NT):
                        src, prob = big(key)[:, t, e * C:(e + 1) * C], rl[s][:, t, e:e + 1]
                        if e == 0:
                            last = nc.vector.tensor_scalar(upd[s][:, t, :], src, prob, None, ALU.mult)
                        else:
                            last = nc.vector.scalar_tensor_tensor(out=upd[s][:, t, :], in0=src, scalar=prob, in1=upd[s][:, t, :],
                                                                  op0=ALU.mult, op1=ALU.add)
                    last.then_inc(S["routed_step"][s] if e < E3 - 1 else big_freed(key), 1)

            def l0_update(s, it):
                key = (s, "out0")
                dve.wait_ge(*small_taken(it, (s, "g0")))
                dve.wait_ge(*small_filled(it, key))
                nc.vector.scalar_tensor_tensor(out=upd[s][:, :, :], in0=th[s][:, 7, :].rearrange("p (t c) -> p t c", t=NT), scalar=1.0,
                                               in1=nat(small(key)), op0=ALU.add, op1=ALU.mult).then_inc(small_freed(key), 1)
                dve.wait_ge(*small_taken(it, key))
                nc.vector.scalar_tensor_tensor(out=x[s][:, :, :], in0=upd[s][:, :, :], scalar=0.5, in1=x[s][:, :, :],
                                               op0=ALU.mult, op1=ALU.add).then_inc(S["x_updated"][s], 1)

            def update(s, it, key, gate=None, factor=1.0):
                dve.wait_ge(*small_filled(it, key))
                if gate is None:
                    nc.vector.tensor_tensor(upd[s][:, :, :], nat(small(key)), x[s][:, :, :], ALU.add).then_inc(small_freed(key), 1)
                    dve.wait_ge(*small_taken(it, key))
                    nc.vector.tensor_copy(x[s][:, :, :], upd[s][:, :, :]).then_inc(S["x_updated"][s], 1)
                else:
                    g = GATE[gate]
                    nc.vector.scalar_tensor_tensor(out=upd[s][:, :, :], in0=nat(small(key)), scalar=factor,
                                                   in1=gates[s][:, g:g + 1, :].to_broadcast([128, NT, C]),
                                                   op0=ALU.mult, op1=ALU.mult).then_inc(small_freed(key), 1)
                    dve.wait_ge(*small_taken(it, key))
                    nc.vector.tensor_tensor(x[s][:, :, :], upd[s][:, :, :], x[s][:, :, :], ALU.add).then_inc(S["x_updated"][s], 1)

            def residues(s, it, a):
                key = (s, "qk", a)
                dve.wait_ge(*of("part1_done", s, it, a + 1))
                for i, b in enumerate((f"bq{a}", f"bk{a}")):
                    last = nc.vector.scalar_tensor_tensor(out=resid[s][:, i, :], in0=small(key)[:, i * T:(i + 1) * T], scalar=col(b),
                                                          in1=parts[s][:, 0, i, :], op0=ALU.add, op1=ALU.subtract)
                last.then_inc(small_freed(key), 1)

            def maxima(s, it, a):
                if a == A_3W:
                    for u in range(2):
                        key = (s, "s", a, u)
                        dve.wait_ge(*big_filled(it, key))
                        for p in range(2):
                            last = nc.vector.tensor_reduce(rowmax[s][:, :, p, 4 * u:4 * u + 4],
                                                           big(key)[:, p, :].rearrange("q (w i k) -> q w i k", w=NT, k=WIN), AX_X, ALU.max)
                        last.then_inc(big_freed(key), 1)
                    return
                for j in range(HP):
                    key = (s, "s", a, j)
                    dve.wait_ge(*big_filled(it, key))
                    nc.vector.tensor_reduce(rowmax[s][:, :, :, j].rearrange("q t p -> q p t"),
                                            big(key)[:, :, :].rearrange("q p (t k) -> q p t k", t=NT), AX_X, ALU.max)\
                        .then_inc(big_freed(key), 1)

            def minus_maxima(s, it, a):
                key = (s, "maxT", a)
                dve.wait_ge(*small_filled(it, key))
                nc.vector.tensor_scalar(negmax[s][:, 0, :], small(key)[0:16, 0:T], -1.0, None, ALU.mult).then_inc(S["negmax_step"][s], 1)
                dve.wait_ge(*of("negmax_step", s, it, a + 1))
                nc.vector.scalar_tensor_tensor(out=negmax[s][:, 1, :], in0=small(key)[0:16, 0:T], scalar=-1.0, in1=negmax[s][:, 0, :],
                                               op0=ALU.mult, op1=ALU.subtract).then_inc(small_freed(key), 1)

            def normalise(s, it, a):
                key = (s, "o", a)
                dve.wait_ge(*small_filled(it, key))
                o = small(key)[:, 0:NT * H * (D + 1)].rearrange("p (h d) -> p h d", d=D + 1)
                nc.vector.reciprocal(rden[s][:, :], o[:, :, D]).then_inc(S["rden_done"][s], 1)
                dve.wait_ge(*of("rden_done", s, it, a + 1))
                nc.vector.tensor_tensor(on[s][:, :, :].rearrange("p t (h d) -> p (t h) d", d=D), o[:, :, 0:D],
                                        rden[s][:, :].unsqueeze(2).to_broadcast([128, NT * H, D]), ALU.mult).then_inc(small_freed(key), 1)

            def top_16(s, it):
                for j in range(HP):
                    key = (s, "top", j)
                    g = s * HP + j
                    b = g % 2
                    tile = [big(key)[:, i // 2, (i % 2) * T:(i % 2 + 1) * T] for i in range(4)]
                    done = it * (SLOTS * HP * 4) + 4 * g
                    dve.wait_ge(*big_filled(it, key))
                    dve.sem_inc(passed["dve"], 1)
                    for i in range(4):
                        last = nc.vector.max(m8[:, b, 0, i, :], tile[i])
                    last.then_inc(top_step, 1)
                    if g >= 2:
                        dve.wait_ge(e_done, it * (SLOTS * HP) + g - 1)
                    dve.wait_ge(top_step, done + 1)
                    nc.vector.tensor_scalar(ntop[:, b, :], m8[:, b, 0, :, 0], -SCALE, None, ALU.mult)
                    for i in range(4):
                        last = nc.vector.match_replace(s1[:, b, i, :], m8[:, b, 0, i, :], tile[i], NEG)
                    last.then_inc(top_step, 1)
                    dve.wait_ge(top_step, done + 2)
                    dve.sem_inc(passed["dve"], 1)
                    for i in range(4):
                        last = nc.vector.max(m8[:, b, 1, i, :], s1[:, b, i, :])
                    last.then_inc(top_step, 1)
                    dve.wait_ge(top_step, done + 3)
                    dve.sem_inc(passed["dve"], 1)
                    for i in range(4):
                        last = nc.vector.match_replace(s1[:, b, i, :], m8[:, b, 1, i, :], s1[:, b, i, :], NEG)
                    last.then_inc(top_step, 1)

            def swiglu(s, it):
                ka, kb = (s, "hid3", 0), (s, "hid3", 1)
                dve.wait_ge(*of("tanh3_done", s, it, 1))
                nc.vector.tensor_scalar(th[s][:, 0:4, :], th[s][:, 0:4, :], 1.0, None, ALU.add).then_inc(S["swiglu_step"][s], 1)
                dve.wait_ge(*of("swiglu_step", s, it, 1))
                for i in range(4):
                    last = nc.vector.scalar_tensor_tensor(out=hid[s][:, i, :], in0=big(ka)[:, i // 2, (i % 2) * T:(i % 2 + 1) * T],
                                                          scalar=col(f"l3_b1_{i}"), in1=th[s][:, i, :], op0=ALU.add, op1=ALU.mult)
                last.then_inc(big_freed(ka), 1)
                dve.wait_ge(*big_taken(it, ka))
                dve.wait_ge(*big_filled(it, kb))
                for i in range(4):
                    last = nc.vector.scalar_tensor_tensor(out=hid[s][:, i, :], in0=big(kb)[:, i // 2, (i % 2) * T:(i % 2 + 1) * T],
                                                          scalar=col(f"l3_b1_{4 + i}"), in1=hid[s][:, i, :], op0=ALU.add, op1=ALU.mult)
                last.then_inc(big_freed(kb), 1)

            def norm(it, *ns):
                for s in both:
                    for n in ns:
                        norm_stats(s, it, n)
                for s in both:
                    for n in ns:
                        norm_apply(s, it, n)

            def attention(it, a, gate=None):
                for s in both:
                    residues(s, it, a)
                if a == A_3C:
                    for s in both:
                        top_16(s, it)
                    for s in both:
                        normalise(s, it, a)
                else:
                    for s in both:
                        maxima(s, it, a)
                    for s in both:
                        minus_maxima(s, it, a)
                    for s in both:
                        normalise(s, it, a)
                for s in both:
                    update(s, it, (s, "proj", a), gate)

            both = range(SLOTS)
            for f in big_free + small_free:
                dve.sem_inc(f, 1)
            nc.vector.memset(ones3[:, :], 1.0).then_inc(const_set, 1)
            nc.vector.memset(twos3[:, :], 2.0).then_inc(const_set, 1)
            for s in both:
                for p in (32, 96):
                    nc.vector.memset(Ks[s][p:p + 32, :, :], 1.0)
                nc.vector.memset(V[s][:, :, :], 1.0).then_inc(const_set, 1)
            dve.wait_ge(cols_loaded, 16)
            nc.vector.tensor_scalar(half_b[:, :], col("l3_b1_0", 4), 0.5, None, ALU.mult).then_inc(const_set, 1)
            dve.wait_ge(rows_loaded, 16)
            dve.wait_ge(mask_loaded, 16)
            flat3 = rows3[:, :, :].rearrange("p r c -> p (r c)")
            nc.vector.tensor_copy(flat3, rowf).then_inc(split_step, 1)
            dve.wait_ge(split_step, 1)
            nc.vector.scalar_tensor_tensor(out=rowr, in0=flat3, scalar=partmask[:, 0:1], in1=rowf, op0=ALU.mult, op1=ALU.add)\
                .then_inc(split_step, 1)
            dve.wait_ge(split_step, 2)
            nc.vector.tensor_copy(flat3, rowr).then_inc(split_step, 1)
            dve.wait_ge(split_step, 3)
            nc.vector.scalar_tensor_tensor(out=rowr, in0=flat3, scalar=partmask[:, 1:2], in1=rowr, op0=ALU.mult, op1=ALU.add)\
                .then_inc(split_step, 1)
            dve.wait_ge(split_step, 4)
            nc.vector.tensor_copy(flat3, rowr).then_inc(rows_split, 1)

            with dve.Fori(0, B // SLOTS) as it:
                for s in both:
                    cond_silu(s, it)
                for s in both:
                    mods_out(s, it)
                norm(it, LN_L0)
                for s in both:
                    l0_max(s, it)
                for s in both:
                    l0_normalise(s, it)
                for s in both:
                    l0_router_max(s, it)
                for s in both:
                    l0_router_norm(s, it)
                for s in both:
                    l0_silu(s, it, 0)
                    l0_silu(s, it, 1)
                for s in both:
                    l0_route(s, it)
                for s in both:
                    l0_update(s, it)
                norm(it, LN_Q, LN_KV)
                attention(it, A_L1)
                norm(it, LN_2A)
                attention(it, A_2S, "l2a")
                norm(it, LN_2C)
                attention(it, A_2C)
                norm(it, LN_2M)
                for s in both:
                    update(s, it, (s, "mlp2"), "l2m")
                norm(it, LN_3A)
                attention(it, A_3W, "l3a")
                norm(it, LN_3C)
                attention(it, A_3C, "l3c")
                norm(it, LN_3M)
                for s in both:
                    swiglu(s, it)
                for s in both:
                    update(s, it, (s, "mlp3"), "l3m", 0.5)

        @block.gpsimd
        def _(pool):
            def inverse_root(s, it, n):
                pool.wait_ge(*of("mv_done", s, it, n + 1))
                pool.sem_inc(passed["pool"], 1)
                nc.gpsimd.tensor_scalar(ve[s][:, n % 2, :], mv[s][:, n % 2, :, 1], EPS[n], None, ALU.add).then_inc(S["ve_done"][s], 1)
                pool.wait_ge(*of("ve_done", s, it, n + 1))
                nc.gpsimd.tensor_tensor(rstd[s][:, n % 2, :], ve[s][:, n % 2, :], minus_half[:, :], ALU.pow).then_inc(S["rstd_done"][s], 1)

            def further_parts(s, it, a):
                pool.wait_ge(*small_taken(it, (s, "qk", a)))
                pool.sem_inc(passed["pool"], 1)
                nc.gpsimd.tensor_copy(parts[s][:, 1, :, :], resid[s][:, :, :]).then_inc(S["part2_done"][s], 1)
                pool.wait_ge(*of("part2_done", s, it, a + 1))
                nc.gpsimd.tensor_tensor(parts[s][:, 2, :, :], resid[s][:, :, :], parts[s][:, 1, :, :], ALU.subtract)\
                    .then_inc(S["parts_done"][s], 1)

            def chosen(s, it):
                for j in range(HP):
                    g = s * HP + j
                    pool.wait_ge(e_done, it * (SLOTS * HP) + g + 1)
                    if g >= 2:
                        pool.wait_ge(*big_filled(it, ((g - 2) // HP, "topT", (g - 2) % HP)))
                    nc.gpsimd.tensor_tensor(ptop[:, g % 2, :, :], e_all[:, g % 2, :, :], e_rest[:, g % 2, :, :], ALU.subtract)\
                        .then_inc(p_done, 1)

            both = range(SLOTS)
            nc.gpsimd.memset(minus_half[:, :], -0.5).then_inc(pool_const, 1)
            pool.wait_ge(pool_const, 1)
            with pool.Fori(0, B // SLOTS) as it:
                def norms(*ns):
                    for s in both:
                        for n in ns:
                            inverse_root(s, it, n)

                def split(a):
                    for s in both:
                        further_parts(s, it, a)

                norms(LN_L0)
                norms(LN_Q, LN_KV)
                split(A_L1)
                norms(LN_2A)
                split(A_2S)
                norms(LN_2C)
                split(A_2C)
                norms(LN_2M)
                norms(LN_3A)
                split(A_3W)
                norms(LN_3C)
                split(A_3C)
                for s in both:
                    chosen(s, it)
                norms(LN_3M)


def kernel(**inputs):
    import numpy as np
    import concourse.bacc as bacc
    from concourse.bass_utils import run_bass_kernel_spmd

    a = {k: np.asarray(v) for k, v in inputs.items()}
    l0, l1, l2, l3 = ({k[len(p):]: v for k, v in a.items() if k.startswith(p)} for p in
                      ("L0_xcond_", "L1_xcond_", "L2_xcond_", "L3_xcond_"))
    turn = [(2 * h2 + p) * D + d for d in range(D) for p in range(2) for h2 in range(HP)]
    plain = list(range(C))

    def thirds(m, i):
        return m[..., i * C:(i + 1) * C]

    qkvo = [
        (l1["Wq"], l1["bq"], thirds(l1["Wkv"], 0), thirds(l1["bkv"], 0), thirds(l1["Wkv"], 1), thirds(l1["bkv"], 1), l1["Wp"], l1["bp"]),
        (*(f(l2[n], i) for i in (0, 1, 2) for f, n in ((thirds, "qkv_w"), (thirds, "qkv_b"))), l2["self_o_w"], l2["self_o_b"]),
        (l2["q_w"], l2["q_b"], thirds(l2["kv_w"], 0), thirds(l2["kv_b"], 0), thirds(l2["kv_w"], 1), thirds(l2["kv_b"], 1), l2["cross_o_w"], l2["cross_o_b"]),
        (*(f(l3[n], i) for i in (0, 1, 2) for f, n in ((thirds, "w_qkv"), (thirds, "b_qkv"))), l3["w_so"], l3["b_so"]),
        (l3["w_q"], l3["b_q"], thirds(l3["w_kv"], 0), thirds(l3["b_kv"], 0), thirds(l3["w_kv"], 1), thirds(l3["b_kv"], 1), l3["w_co"], l3["b_co"]),
    ]
    q_ss, kv_ss, ada2, ada3 = (l1["Wss_q"], l1["bss_q"]), (l1["Wss_kv"], l1["bss_kv"]), (l2["ada_w"], l2["ada_b"]), (l3["w_ada"], l3["b_ada"])
    scales = [(*q_ss, 0), (*kv_ss, 0), (*ada2, 1), (*ada2, 4), (*ada3, 1), (*ada3, 4), (*ada3, 7)]
    shifts = [(*q_ss, 1), (*kv_ss, 1), (*ada2, 0), (*ada2, 3), (*ada3, 0), (*ada3, 3), (*ada3, 6)]
    gates = [(*ada2, 2), (*ada2, 5), (*ada3, 2), (*ada3, 5), (*ada3, 8)]

    def by_rows(m):
        return np.concatenate([m[i * C:(i + 1) * C] for i in range(m.shape[0] // C)], axis=1)

    mats = {"l0_q": l0["Wq"], "l0_k": l0["Wk"], "l0_v": l0["Wv"], "l0_router": by_rows(l0["router_W"]), "l0_g2": l0["gate_w2"], "l0_out": l0["out_w"],
            "mod": np.concatenate([thirds(m, i) for m, _, i in scales + shifts], axis=1),
            "gate": np.concatenate([thirds(m, i) for m, _, i in gates], axis=1),
            "l2_w1": l2["mlp_w1"], "l2_w2": by_rows(l2["mlp_w2"]), "l3_w1": l3["w_m1"], "l3_w2": by_rows(l3["w_m2"])}
    vecs = {"ln_g": l0["ln_gamma"], "ln_b": l0["ln_beta"], "n2_g": l2["norm2_g"], "n2_b": l2["norm2_b"], "anchor6": l0["gate_b1"]}
    rows = {"router": l0["router_b"], "g2": l0["gate_b2"], "out": l0["out_b"], "l2_b2": l2["mlp_b2"], "l3_b2": l3["b_m2"]}
    for i in range(3):
        mats[f"l0_g1_{i}"] = l0["gate_w1"][i * C:(i + 1) * C]
    for e in range(E3):
        rows[f"e{e}"] = l0["e_b2"][e]
        for i in range(3):
            mats[f"l0_w1_{e}_{i}"] = l0["e_w1"][e, i * C:(i + 1) * C]
        for i in range(2):
            mats[f"l0_w2_{e}_{i}"] = l0["e_w2"][e, i * C:(i + 1) * C]
            vecs[f"anchor{2 * e + i}"] = l0["e_b1"][e, i * C:(i + 1) * C]
    for i, (_, b, n) in enumerate(scales + shifts):
        vecs[f"mod{i}"] = thirds(b, n)
    for i, (_, b, n) in enumerate(gates):
        rows[f"gate{i}"] = thirds(b, n)
    for n, (wq, bq, wk, bk, wv, bv, wo, bo) in enumerate(qkvo):
        mats[f"q{n}"], mats[f"k{n}"], mats[f"v{n}"], mats[f"o{n}"] = wq[:, turn], wk[:, turn], wv[:, plain], wo
        vecs[f"bq{n}"], vecs[f"bk{n}"], rows[f"bv{n}"], rows[f"bo{n}"] = bq[turn], bk[turn], bv, bo
    for i in range(4):
        vecs[f"l2_b1_{i}"] = l2["mlp_b1"][i * C:(i + 1) * C]
    for i in range(8):
        vecs[f"l3_b1_{i}"] = l3["b_m1"][i * C:(i + 1) * C]

    row_block = np.zeros((len(ROWV), C), np.float32)
    for name, i in ROW.items():
        row_block[i, :rows[name].shape[0]] = rows[name]
    arrays = {
        "x": np.ascontiguousarray(a["x"]),
        "ctx": np.ascontiguousarray(a["ctx_1024"]),
        "ctxT": np.ascontiguousarray(np.transpose(a["ctx_1024"], (0, 2, 1))),
        "condT": np.ascontiguousarray(a["cond_1024"][:, :, None]),
        "mats": np.ascontiguousarray(np.concatenate([mats[n] for g in MATS.values() for n, _ in g], axis=1)),
        "cols": np.ascontiguousarray(np.stack([vecs[n] for n in COLS], axis=1)),
        "rows": np.ascontiguousarray(np.stack([row_block.reshape(-1)] * PARTS)),
        "ident": np.eye(128, dtype=np.float32),
        "partmask": np.array([[0, 0], [-1, 0], [-1, -1]], np.float32),
    }
    nc = bacc.Bacc("TRN2", target_bir_lowering=False, num_devices=1)
    ins = {n: nc.dram_tensor(f"in_{n}", v.shape, mybir.dt.from_np(v.dtype), kind="ExternalInput").ap() for n, v in arrays.items()}
    out = nc.dram_tensor("out", (B, T, C), F32, kind="ExternalOutput").ap()
    chain_kernel(nc, ins, out)
    r = run_bass_kernel_spmd(nc, [{f"in_{n}": v for n, v in arrays.items()}], core_ids=[0])
    return r.results[0]["out"]
```

```python
from contextlib import ExitStack

import concourse.bass as bass
from concourse import mybir

F32 = mybir.dt.float32
BF16 = mybir.dt.bfloat16
ALU = mybir.AluOpType
ACT = mybir.ActivationFunctionType
AX_X = mybir.AxisListType.X

B, T, C = 4, 256, 128
NT = T // 128
SLOTS = 2
H, D = 16, 8
HP = H // 2
E3, HID0 = 3, 256
HID = 512
WIN, SHIFT = 64, 32
PARTS = 3
BLOCKS = 6
ROWS = BLOCKS * D
ROWSM = ROWS + 2
TURN_LAG = 1
VW = 32
PT_UNITS = 4
CHOSEN_BUFS = 3
SLOT_LAG = 8.0
NEG = -3.0e37

SCALE0 = float(C) ** -0.5
SCALE = float(D) ** -0.5

MATS = {
    "early": [("l0_q", C), ("l0_k", C), ("l0_v", C)],
    "l0": [("l0_router", 3 * E3)] + [(f"l0_w1_{e}_{i}", HID0) for e in range(E3) for i in range(3)]
    + [(f"l0_w2_{e}_{i}", C) for e in range(E3) for i in range(2)]
    + [(f"l0_g1_{i}", C) for i in range(3)] + [("l0_g2", C), ("l0_out", C)],
    "mod": [("mod", 14 * C), ("gate", 5 * C)],
    "l1": [("q0", C), ("k0", C), ("v0", C), ("o0", C)],
    "l2": [("q1", C), ("k1", C), ("v1", C), ("o1", C), ("q2", C), ("k2", C), ("v2", C), ("o2", C),
           ("l2_w1", HID), ("l2_w2", 4 * C)],
    "l3": [("q3", C), ("k3", C), ("v3", C), ("o3", C), ("q4", C), ("k4", C), ("v4", C), ("o4", C),
           ("l3_w1", 2 * HID), ("l3_w2", 4 * C)],
}
MAT_AT, _n = {}, 0
GROUP_AT = {}
for _g, _list in MATS.items():
    GROUP_AT[_g] = _n
    for _name, _cols in _list:
        MAT_AT[_name] = (_n, _cols)
        _n += _cols
MAT_COLS = _n

COLS = ["ln_g", "ln_b"] + [f"mod{i}" for i in range(14)] + [f"anchor{i}" for i in range(7)]
COLS += [f"{x}{a}" for a in range(5) for x in ("bq", "bk")]
COLS += ["n2_g", "n2_b"] + [f"l2_b1_{i}" for i in range(4)] + [f"l3_b1_{i}" for i in range(8)]
COL = {n: i for i, n in enumerate(COLS)}

ROWV = ["router", "e0", "e1", "e2", "g2", "out"] + [f"{x}{a}" for a in range(5) for x in ("bv", "bo")]
ROWV += ["l2_b2", "l3_b2"] + [f"gate{i}" for i in range(5)]
ROW = {n: i for i, n in enumerate(ROWV)}

SC = dict(q=0, kv=1, l2a=2, l2m=3, l3a=4, l3c=5, l3m=6)
SH = {k: v + 7 for k, v in SC.items()}
GATE = dict(l2a=0, l2m=1, l3a=2, l3c=3, l3m=4)

LN_L0, LN_Q, LN_KV, LN_2A, LN_2C, LN_2M, LN_3A, LN_3C, LN_3M = range(9)
EPS = [1e-5, 1e-5, 1e-5, 1e-6, 1e-6, 1e-6, 1e-6, 1e-6, 1e-6]
UPDATES_BEFORE = [0, 1, 0, 2, 3, 4, 5, 6, 7]

A_L1, A_2S, A_2C, A_3W, A_3C = range(5)
NORMS_FOR = [LN_KV, LN_2A, LN_2C, LN_3A, LN_3C]


def sequence_steps():
    def norm(*ns):
        return [(1.0, ("stats", n)) for n in ns] + [(0.8, ("apply", n)) for n in ns] + [(1.0, ("turn", n)) for n in ns]

    def attention(a):
        steps = [(3.5, ("qkv", a)), (3.0, ("stack_write", a)), (3.5, ("stack_read", a))]
        if a == A_3C:
            for j in range(HP + TURN_LAG + 1):
                if j < HP:
                    steps += [(2.5, ("top", j)), (2.5, ("rest", j))]
                if TURN_LAG <= j < HP + TURN_LAG:
                    steps.append((0.5, ("topT", j - TURN_LAG)))
                if j >= TURN_LAG + 1:
                    steps.append((0.5, ("values", a, j - TURN_LAG - 1)))
        elif a == A_3W:
            steps += [(1.8, ("windows", u)) for u in range(2)]
            steps += [(1.0, ("maxT", a)), (2.5, ("max_rows", a))]
            steps += [(1.8, ("windows_T", u)) for u in range(2)]
            steps += [(2.0, ("window_values", h)) for h in range(2)]
        else:
            steps += [(1.2, ("scores", a, j)) for j in range(HP)]
            steps += [(1.0, ("maxT", a)), (2.5, ("max_rows", a))]
            for j in range(HP + 1):
                if j < HP:
                    steps.append((0.5, ("scores_T", a, j)))
                if j >= 1:
                    steps.append((1.7, ("values", a, j - 1)))
        return steps + [(1.5, ("out_natural", a)), (1.0, ("out_turn", a)), (1.5, ("project", a))]

    steps = [(1.0, ("cond",))] + norm(LN_L0)
    steps += [(1.5, ("l0_qkv",)), (2.5, ("l0_scores",)), (1.0, ("l0_normalise",)), (1.2, ("l0_probs_turn",)), (0.6, ("mods",)),
              (1.2, ("l0_evidence",)), (0.6, ("gates",)),
              (2.0, ("l0_router",)), (1.0, ("l0_router_norm",)), (2.5, ("l0_hidden", 0)), (2.5, ("l0_hidden", 1)),
              (1.5, ("l0_experts",)), (1.5, ("l0_routed_turn",)), (2.5, ("l0_out",))]
    steps += norm(LN_Q, LN_KV) + attention(A_L1)
    steps += norm(LN_2A) + attention(A_2S)
    steps += norm(LN_2C) + attention(A_2C)
    steps += norm(LN_2M) + [(2.0, ("gelu",)), (2.5, ("mlp2",))]
    steps += norm(LN_3A) + attention(A_3W)
    steps += norm(LN_3C) + attention(A_3C)
    steps += norm(LN_3M) + [(2.0, ("swiglu",)), (2.5, ("swiglu_up",)), (2.5, ("mlp3",)), (1.0, ("store",)), (2.0, ("reload",))]
    return steps


def schedule():
    timed = []
    for s in range(SLOTS):
        at = s * SLOT_LAG
        for n, (takes, step) in enumerate(sequence_steps()):
            timed.append((at, s, n, step))
            at += takes
    return [(s, *step) for _, s, _, step in sorted(timed, key=lambda e: e[:3])]


def psum_plan(order):
    big, small = [], []
    for s, kind, *args in order:
        key = (s, kind, *args)
        if kind in ("gates", "l0_hidden", "l0_experts", "scores", "scores_T", "windows", "windows_T", "top", "topT", "out_natural",
                    "gelu", "swiglu", "swiglu_up"):
            big.append(key)
        elif kind in ("mods", "turn", "l0_scores", "l0_probs_turn", "l0_evidence", "l0_router", "l0_routed_turn", "maxT",
                      "out_turn", "project", "mlp2", "mlp3"):
            small.append(key)
        elif kind in ("l0_qkv", "qkv"):
            small.extend([key, (s, "v", *args)])
        elif kind == "l0_out":
            small.extend([(s, "l0_gate"), key])
    return big, small


NBIG, NSMALL = 2, 2


class Ring:

    def __init__(self, keys, size):
        self.size = size
        self.use = {k: n for n, k in enumerate(keys)}
        assert len(self.use) == len(keys)
        self.per_round = [len(range(e, len(keys), size)) for e in range(size)]

    def at(self, key):
        n = self.use[key]
        return n % self.size, n // self.size


def chain_kernel(nc: bass.Bass, ins, out):
    order = schedule()
    big_keys, small_keys = psum_plan(order)
    top_order = [(s, *a) for s, kind, *a in order if kind == "top"]
    top_unit = {key: n for n, key in enumerate(top_order)}
    big_ring, small_ring = Ring(big_keys, NBIG), Ring(small_keys, NSMALL)

    with ExitStack() as ctx:
        def sb(name, shape, dt=F32):
            return ctx.enter_context(nc.sbuf_tensor(name, shape, dt))

        def sem(name):
            return ctx.enter_context(nc.semaphore(name))

        def per_slot_sb(name, shape, dt=F32):
            return [sb(f"{name}{s}", shape, dt) for s in range(SLOTS)]

        W = sb("weights", [128, MAT_COLS])
        cols = sb("cols", [128, len(COLS)])
        ident = sb("ident", [128, 128])
        rows3 = sb("rows3", [3, len(ROWV), C], BF16)
        ones3 = sb("ones3", [3, 128], BF16)
        twos3 = sb("twos3", [3, 128], BF16)
        rowf = sb("row_vectors", [len(ROWV), C])
        row_parts = sb("row_parts", [len(ROWV), PARTS, C], BF16)
        minus_half = sb("minus_half", [128, NT])
        half_b = sb("half_b", [128, 4])

        x = per_slot_sb("x", [128, NT, C])
        cx = per_slot_sb("cx", [128, NT, C])
        cT = per_slot_sb("cT", [128, T])
        cond = per_slot_sb("cond", [128, 1])
        tc_ = per_slot_sb("tanh_cond", [128, 1])
        silu = per_slot_sb("silu_cond", [128, 1])
        condB = per_slot_sb("condB", [128, 128])
        siluB = per_slot_sb("siluB", [128, 128])
        mod = per_slot_sb("mod", [128, 21])
        half_anchor = per_slot_sb("half_anchor", [128, 7])
        gates = per_slot_sb("gates", [128, 5, C])
        stats = per_slot_sb("stats", [128, 2, NT, 6])
        mv = per_slot_sb("mv", [128, 2, NT, 2])
        ve = per_slot_sb("ve", [128, 2, NT])
        rstd = per_slot_sb("rstd", [128, 2, NT])
        xn = per_slot_sb("xn", [128, 2, NT, C])
        hT = per_slot_sb("hT", [128, T])
        kvT = per_slot_sb("kvT", [128, T])
        parts = per_slot_sb("parts", [128, PARTS, 2, T], BF16)
        resid = per_slot_sb("resid", [128, 2, T])
        Qs = per_slot_sb("Qs", [128, HP, T], BF16)
        Ks = per_slot_sb("Ks", [128, HP, T], BF16)
        V = per_slot_sb("V", [128, NT * H, VW])
        rowmax = per_slot_sb("rowmax", [128, NT, 2, HP])
        negmax = per_slot_sb("negmax", [16, 2, T], BF16)
        PT = per_slot_sb("PT", [128, 2 * PT_UNITS + 2, NT, T])
        rden = per_slot_sb("rden", [128, NT * H])
        oT = per_slot_sb("oT", [128, T])
        upd = per_slot_sb("upd", [128, NT, C])
        m0 = per_slot_sb("m0", [128, NT])
        nm0 = per_slot_sb("nm0", [128, NT])
        z0 = per_slot_sb("z0", [128, NT])
        rl = per_slot_sb("rl", [128, NT, E3])
        rm = per_slot_sb("rm", [128, NT])
        qk0 = resid
        on = [resid[s][:, 0, :].rearrange("p (t c) -> p t c", t=NT) for s in range(SLOTS)]
        hid = [PT[s][:, 0:4, :, :].rearrange("p a b t -> p (a b) t") for s in range(SLOTS)]
        th = [PT[s][:, 4:8, :, :].rearrange("p a b t -> p (a b) t") for s in range(SLOTS)]
        OT = [PT[s][:, 8:10].rearrange("p a b t -> p (a b) t") for s in range(SLOTS)]
        p0 = [PT[s][:, 8, :, :] for s in range(SLOTS)]
        p0T = [PT[s][:, 9, :, :] for s in range(SLOTS)]

        s1 = sb("s1", [128, 2, 4, T])
        m8 = sb("m8", [128, 2, 2, 4, 8])
        ntop = sb("ntop", [128, 2, 4])
        e_all = sb("e_all", [128, 2, 4, T])
        e_rest = sb("e_rest", [128, 2, 4, T])
        ptop = sb("ptop", [128, CHOSEN_BUFS, 4, T])

        BIG = [ctx.enter_context(nc.psum_tensor(f"big{e}", [128, 2, 512], F32)) for e in range(NBIG)]
        SMALL = [ctx.enter_context(nc.psum_tensor(f"small{e}", [128, 512], F32)) for e in range(NSMALL)]
        OUT = [ctx.enter_context(nc.psum_tensor(f"out{s}", [128, 512], F32)) for s in range(SLOTS)]
        scratch = [nc.dram_tensor(f"parts_scratch{s}", (2, BLOCKS, 128, T), BF16, kind="Internal").ap()
                   for s in range(SLOTS)]

        big_full = [sem(f"big_full{e}") for e in range(NBIG)]
        big_free = [sem(f"big_free{e}") for e in range(NBIG)]
        small_full = [sem(f"small_full{e}") for e in range(NSMALL)]
        small_free = [sem(f"small_free{e}") for e in range(NSMALL)]
        cols_loaded, ident_loaded, rows_loaded = sem("cols_loaded"), sem("ident_loaded"), sem("rows_loaded")
        group_loaded = {g: sem(f"{g}_loaded") for g in MATS}
        const_set = sem("const_set")
        pool_const = sem("pool_const")
        passed = {e: sem(f"passed_{e}") for e in ("sp", "pe", "dve", "pool")}
        split_step = sem("split_step")
        rows_spread = sem("rows_spread")

        PER_SEQ = dict(
            loaded=64, stored=16, tanh_cond=1, silu_step=4, mod_step=2,
            bn_done=9, mv_done=9, ve_done=9, rstd_done=9, xn_done=9,
            softmax0_step=4, router_step=4, router_exp=1, tanh0_done=2, silu0_step=2, routed_step=2,
            x_updated=8, out_full=10, out_free=10,
            part1_done=5, part2_done=5, parts_done=5, scratch_written=5 * 96, stacked=5 * 64,
            negmax_step=4, maxrow_loaded=4 * 64, rden_done=5, tanh3_done=1, swiglu_step=1,
        )
        S = {n: [sem(f"{n}{s}") for s in range(SLOTS)] for n in PER_SEQ}
        top_step = sem("top_step")
        e_done = sem("e_done")
        p_done = sem("p_done")

        CONSTS = 3
        POOL_CONSTS = 1 + 4 * SLOTS

        block = ctx.enter_context(nc.Block())

        def w(name, lo=0, n=None):
            at, width = MAT_AT[name]
            return W[:, at + lo:at + (width if n is None else lo + n)]

        def col(name, n=1):
            return cols[:, COL[name]:COL[name] + n]

        def row(name):
            return rows3[:, ROW[name]:ROW[name] + 1, :].to_broadcast([3, NT, C])

        def of(name, s, it, k):
            assert 0 < k <= PER_SEQ[name], (name, k)
            return S[name][s], it * PER_SEQ[name] + k

        def big_filled(it, key):
            e, k = big_ring.at(key)
            return big_full[e], it * big_ring.per_round[e] + k + 1

        def big_is_free(it, key):
            e, k = big_ring.at(key)
            return big_free[e], it * big_ring.per_round[e] + k + 1

        def small_filled(it, key):
            e, k = small_ring.at(key)
            return small_full[e], it * small_ring.per_round[e] + k + 1

        def small_is_free(it, key):
            e, k = small_ring.at(key)
            return small_free[e], it * small_ring.per_round[e] + k + 1

        def big_taken(it, key):
            f, v = big_is_free(it, key)
            return f, v + 1

        def small_taken(it, key):
            f, v = small_is_free(it, key)
            return f, v + 1

        def tiles(it, free=(), taken=()):
            need = {}
            for keys, extra in ((free, 1), (taken, 2)):
                for key in keys:
                    ring, sems, ready = (small_ring, small_free, "s") if key in small_ring.use else (big_ring, big_free, "b")
                    e, k = ring.at(key)
                    need[ready, e] = max(need.get((ready, e), (0,))[0], k + extra), sems[e], ring.per_round[e]
            return [(f, it * n + k) for k, f, n in need.values()]

        def big(key):
            return BIG[big_ring.at(key)[0]]

        def small(key):
            return SMALL[small_ring.at(key)[0]]

        def big_freed(key):
            return big_free[big_ring.at(key)[0]]

        def small_freed(key):
            return small_free[small_ring.at(key)[0]]

        def big_ready(key):
            return big_full[big_ring.at(key)[0]]

        def small_ready(key):
            return small_full[small_ring.at(key)[0]]

        def nat(ap):
            return ap[:, 0:T].rearrange("p (t c) -> p t c", t=NT)

        def follow(it, steps):
            for s, kind, *args in order:
                if kind in steps:
                    steps[kind](s, it, *args)

        @block.sync
        def _(sp):
            def load_inputs(s, b):
                sp.dma_start(x[s][:, :, :], ins["x"][bass.ds(b, 1)].rearrange("b (t p) c -> p (b t) c", p=128)).then_inc(S["loaded"][s], 16)
                sp.dma_start(cond[s][:, :], ins["condT"][bass.ds(b, 1)].rearrange("b p o -> p (b o)")).then_inc(S["loaded"][s], 16)
                sp.dma_start(cT[s][:, :], ins["ctxT"][bass.ds(b, 1)].rearrange("b p t -> p (b t)")).then_inc(S["loaded"][s], 16)
                sp.dma_start(cx[s][:, :, :], ins["ctx"][bass.ds(b, 1)].rearrange("b (t p) c -> p (b t) c", p=128)).then_inc(S["loaded"][s], 16)

            def stack_write(s, it, a):
                wr = S["scratch_written"][s]
                q_scr = scratch[s][0].rearrange("r c t -> c r t")
                k_scr = scratch[s][1].rearrange("r c t -> c r t")
                sp.wait_ge(*of("part1_done", s, it, a + 1))
                sp.dma_start(q_scr[:, 0:3], parts[s][:, 0:1, 0, :].to_broadcast([128, 3, T])).then_inc(wr, 16)
                sp.dma_start(k_scr[:, 5:6], parts[s][:, 0:1, 1, :]).then_inc(wr, 16)
                sp.wait_ge(*of("parts_done", s, it, a + 1))
                sp.dma_start(k_scr[:, 0:3], parts[s][:, 0:3, 1, :]).then_inc(wr, 16)
                sp.dma_start(k_scr[:, 3:5], parts[s][:, 0:2, 1, :]).then_inc(wr, 16)
                sp.dma_start(q_scr[:, 3:5], parts[s][:, 1:2, 0, :].to_broadcast([128, 2, T])).then_inc(wr, 16)
                sp.dma_start(q_scr[:, 5:6], parts[s][:, 2:3, 0, :]).then_inc(wr, 16)

            def stack_read(s, it, a):
                sp.wait_ge(*of("scratch_written", s, it, 96 * (a + 1)))
                for i, stacked in enumerate((Qs[s], Ks[s])):
                    for p in range(2):
                        src = scratch[s][i].rearrange("r (d p h) t -> p (r d) (h t)", p=2, d=D)[p]
                        dst = stacked[64 * p:64 * p + ROWS].rearrange("r h t -> r (h t)")
                        sp.dma_start(dst, src).then_inc(S["stacked"][s], 16)

            def max_rows(s, it, a):
                sp.wait_ge(*small_taken(it, (s, "maxT", a)))
                for part in range(2):
                    for p in range(2):
                        r = 64 * p + ROWS + part
                        sp.dma_start(Qs[s][r:r + 1, :, :], negmax[s][HP * p:HP * p + HP, part, :]).then_inc(S["maxrow_loaded"][s], 16)

            def store(s, it):
                sp.wait_ge(*of("x_updated", s, it, 8))
                sp.sem_inc(passed["sp"], 1)
                sp.dma_start(out[bass.ds(it * SLOTS + s, 1)].rearrange("b (t p) c -> p (b t) c", p=128), x[s][:, :, :]).then_inc(S["stored"][s], 16)

            def reload(s, it):
                sp.wait_ge(*of("stored", s, it, 16))
                sp.sem_inc(passed["sp"], 1)
                load_inputs(s, it * SLOTS + (SLOTS + s))

            sp.dma_start(rowf[:, :], ins["rows"]).then_inc(rows_loaded, 16)
            for s in range(SLOTS):
                load_inputs(s, s)
                if s == 0:
                    sp.dma_start(cols[:, :], ins["cols"]).then_inc(cols_loaded, 16)
                    sp.dma_start(ident[:, :], ins["ident"]).then_inc(ident_loaded, 16)
            sp.wait_ge(split_step, 5)
            for i in range(PARTS):
                sp.dma_start(rows3[i:i + 1, :, :], row_parts[:, i, :]).then_inc(rows_spread, 16)
            sp.wait_ge(pool_const, POOL_CONSTS)
            with sp.Fori(0, B // SLOTS) as it:
                follow(it, dict(stack_write=stack_write, stack_read=stack_read, max_rows=max_rows, store=store, reload=reload))
            for s in range(SLOTS):
                sp.wait_ge(S["loaded"][s], 64 * (B // SLOTS + 1))

        @block.tensor
        def _(pe):
            def turn(key, s, src, it, taken=()):
                for t in tiles(it, free=[key], taken=taken):
                    pe.wait_ge(*t)
                for t in range(NT):
                    mm = pe.transpose(small(key)[:, t * 128:(t + 1) * 128], src(t), ident[:, :])
                mm.then_inc(small_ready(key), 1)

            def bias_rows(dst, name, ones, start=True):
                return pe.matmul(dst, ones[:, :], row(name), start=start, stop=False, skip_group_check=True)

            def natural(key, it, terms, name, ones=None, taken=()):
                for t in tiles(it, free=[key], taken=taken):
                    pe.wait_ge(*t)
                dst = small(key)
                bias_rows(nat(dst), name, ones3 if ones is None else ones)
                for t in range(NT):
                    for i, (a, m) in enumerate(terms):
                        mm = pe.matmul(dst[:, t * 128:(t + 1) * 128], a[:, t * 128:(t + 1) * 128], m, start=False,
                                       stop=(i == len(terms) - 1), skip_group_check=True)
                mm.then_inc(small_ready(key), 1)

            def mods(s, it):
                key = (s, "mods")
                pe.wait_ge(group_loaded["l0"], 16)
                pe.wait_ge(group_loaded["mod"], 16)
                pe.wait_ge(*of("silu_step", s, it, 2))
                pe.wait_ge(*small_is_free(it, key))
                for i in range(14):
                    pe.matmul(small(key)[:, i:i + 1], w("mod", i * C, C), silu[s][:, :], start=True, stop=True)
                for i in range(7):
                    m = w(f"l0_w1_{i // 2}_2", (i % 2) * C, C) if i < 6 else w("l0_g1_2")
                    mm = pe.matmul(small(key)[:, 14 + i:15 + i], m, cond[s][:, :], start=True, stop=True)
                mm.then_inc(small_ready(key), 1)

            def gate_rows(s, it):
                key = (s, "gates")
                pe.wait_ge(rows_spread, 16 * PARTS)
                pe.wait_ge(*of("silu_step", s, it, 4))
                pe.wait_ge(*big_is_free(it, key))
                for bank, lo, n in ((0, 0, 2), (1, 2, 3)):
                    dst = big(key)[:, bank, 0:n * C]
                    pe.matmul(dst, ones3[:, :], rows3[:, ROW["gate0"] + lo:ROW["gate0"] + lo + n, :], start=True, stop=False, skip_group_check=True)
                    mm = pe.matmul(dst, siluB[s][:, :], w("gate", lo * C, n * C), start=False, stop=True, skip_group_check=True)
                mm.then_inc(big_ready(key), 1)

            def norm_turn(s, it, n):
                pe.wait_ge(*of("xn_done", s, it, n + 1))
                turn((s, "turn", n), s, lambda t: xn[s][:, n % 2, t, :], it)

            def l0_qkv(s, it):
                pe.wait_ge(group_loaded["early"], 16)
                key = (s, "l0_qkv")
                for t in tiles(it, free=[key], taken=[(s, "turn", LN_L0)]):
                    pe.wait_ge(*t)
                pe.matmul(small(key)[:, 0:T], w("l0_q"), hT[s][:, :], start=True, stop=True)
                pe.matmul(small(key)[:, T:2 * T], w("l0_k"), cT[s][:, :], start=True, stop=True).then_inc(small_ready(key), 1)
                key = (s, "v")
                pe.wait_ge(*small_is_free(it, key))
                for t in range(NT):
                    mm = pe.matmul(small(key)[:, t * C:(t + 1) * C], cT[s][:, t * 128:(t + 1) * 128], w("l0_v"), start=True, stop=True)
                mm.then_inc(small_ready(key), 1)

            def l0_scores(s, it):
                key = (s, "l0_scores")
                for t in tiles(it, free=[key], taken=[(s, "l0_qkv")]):
                    pe.wait_ge(*t)
                for t in range(NT):
                    mm = pe.matmul(small(key)[:, t * T:(t + 1) * T], qk0[s][:, 0, t * 128:(t + 1) * 128], qk0[s][:, 1, :], start=True, stop=True)
                mm.then_inc(small_ready(key), 1)

            def l0_probs_turn(s, it):
                key = (s, "l0_probs_turn")
                pe.wait_ge(*of("softmax0_step", s, it, 4))
                pe.wait_ge(*small_is_free(it, key))
                for k in range(NT):
                    for t in range(NT):
                        mm = pe.transpose(small(key)[:, k * T + t * 128:k * T + (t + 1) * 128], p0[s][:, t, k * 128:(k + 1) * 128], ident[:, :])
                mm.then_inc(small_ready(key), 1)

            def l0_evidence(s, it):
                key = (s, "l0_evidence")
                for t in tiles(it, free=[key], taken=[(s, "v"), (s, "l0_probs_turn")]):
                    pe.wait_ge(*t)
                for k in range(NT):
                    mm = pe.matmul(small(key)[:, 0:T], upd[s][:, k, :], p0T[s][:, k, :], start=(k == 0), stop=(k == NT - 1))
                mm.then_inc(small_ready(key), 1)

            def l0_router(s, it):
                key = (s, "l0_router")
                for t in tiles(it, free=[key], taken=[(s, "l0_evidence")]):
                    pe.wait_ge(*t)
                rw = w("l0_router")
                for t in range(NT):
                    dst = small(key)[:, 4 * t:4 * t + E3]
                    tt = slice(t * 128, (t + 1) * 128)
                    pe.matmul(dst, ones3[:, :], rows3[:, ROW["router"], 0:E3], start=True, stop=False, skip_group_check=True)
                    pe.matmul(dst, hT[s][:, tt], rw[:, 0:E3], start=False, stop=False, skip_group_check=True)
                    pe.matmul(dst, kvT[s][:, tt], rw[:, E3:2 * E3], start=False, stop=False, skip_group_check=True)
                    mm = pe.matmul(dst, condB[s][:, :], rw[:, 2 * E3:3 * E3], start=False, stop=True, skip_group_check=True)
                mm.then_inc(small_ready(key), 1)

            def l0_hidden(s, it, half):
                key = (s, "l0_hidden", half)
                pe.wait_ge(*big_is_free(it, key))
                for i in range(4 * half, min(4 * half + 4, 7)):
                    n = i - 4 * half
                    dst = big(key)[:, n // 2, (n % 2) * T:(n % 2 + 1) * T]
                    for j, act in enumerate((hT[s], kvT[s])):
                        m = w(f"l0_w1_{i // 2}_{j}", (i % 2) * C, C) if i < 6 else w(f"l0_g1_{j}")
                        mm = pe.matmul(dst, m, act[:, :], start=(j == 0), stop=(j == 1))
                mm.then_inc(big_ready(key), 1)

            def l0_experts(s, it):
                key = (s, "l0_experts")
                for t in tiles(it, free=[key], taken=[(s, "l0_hidden", 1)]):
                    pe.wait_ge(*t)
                for t in range(NT):
                    pe.matmul(big(key)[:, t, 0:E3 * C], twos3[:, :], rows3[:, ROW["e0"]:ROW["e0"] + E3, :], start=True, stop=False, skip_group_check=True)
                    for e in range(E3):
                        for c in range(2):
                            mm = pe.matmul(big(key)[:, t, e * C:(e + 1) * C], hid[s][:, 2 * e + c, t * 128:(t + 1) * 128], w(f"l0_w2_{e}_{c}"),
                                           start=False, stop=(c == 1), skip_group_check=True)
                mm.then_inc(big_ready(key), 1)

            def l0_routed_turn(s, it):
                pe.wait_ge(*big_taken(it, (s, "l0_experts")))
                turn((s, "l0_routed_turn"), s, lambda t: upd[s][:, t, :], it)

            def l0_out(s, it):
                natural((s, "l0_gate"), it, [(hid[s][:, 6, :], w("l0_g2"))], "g2", twos3)
                natural((s, "l0_out"), it, [(oT[s], w("l0_out"))], "out", taken=[(s, "l0_routed_turn")])

            def qkv(s, it, a):
                pe.wait_ge(group_loaded["l1" if a == A_L1 else "l2" if a in (A_2S, A_2C) else "l3"], 16)
                kv = {A_L1: kvT, A_2S: hT, A_2C: cT, A_3W: hT, A_3C: cT}[a][s]
                key = (s, "qkv", a)
                norms = [(s, "turn", NORMS_FOR[a])] + [(s, "turn", LN_Q)] * (a == A_L1)
                for t in tiles(it, free=[key], taken=norms):
                    pe.wait_ge(*t)
                pe.matmul(small(key)[:, 0:T], w(f"q{a}"), hT[s][:, :], start=True, stop=True)
                pe.matmul(small(key)[:, T:2 * T], w(f"k{a}"), kv[:, :], start=True, stop=True).then_inc(small_ready(key), 1)
                natural((s, "v", a), it, [(kv, w(f"v{a}"))], f"bv{a}")

            def scores(s, it, a, j):
                key = (s, "scores", a, j)
                if j == 0:
                    pe.wait_ge(*of("stacked", s, it, 64 * (a + 1)))
                pe.wait_ge(*big_is_free(it, key))
                for t in range(NT):
                    for p in range(2):
                        r = slice(64 * p, 64 * p + ROWS)
                        mm = pe.matmul(big(key)[:, p, t * T:(t + 1) * T], Qs[s][r, j, t * 128:(t + 1) * 128], Ks[s][r, j, :], start=True, stop=True)
                mm.then_inc(big_ready(key), 1)

            def scores_T(s, it, a, j):
                key = (s, "scores_T", a, j)
                if j == 0:
                    pe.wait_ge(*of("maxrow_loaded", s, it, 64 * (a + 1)))
                pe.wait_ge(*big_is_free(it, key))
                for k in range(NT):
                    for p in range(2):
                        r = slice(64 * p, 64 * p + ROWSM)
                        mm = pe.matmul(big(key)[:, p, k * T:(k + 1) * T], Ks[s][r, j, k * 128:(k + 1) * 128], Qs[s][r, j, :], start=True, stop=True)
                mm.then_inc(big_ready(key), 1)

            def window_scores(s, it, key, turned):
                u = key[2]
                if u == 0:
                    pe.wait_ge(*(of("maxrow_loaded", s, it, 64 * (A_3W + 1)) if turned else of("stacked", s, it, 64 * (A_3W + 1))))
                pe.wait_ge(*big_is_free(it, key))
                pe.sem_inc(passed["pe"], 1)
                for i in range(4):
                    for wdw in range(T // WIN):
                        for p in range(2):
                            r = slice(64 * p, 64 * p + (ROWSM if turned else ROWS))
                            q = Qs[s][r, 4 * u + i, wdw * WIN:(wdw + 1) * WIN]
                            k = Ks[s][r, 4 * u + i, wdw * WIN:(wdw + 1) * WIN]
                            c0 = ((wdw // 2) * 4 + i) * WIN
                            dst = big(key)[64 * (wdw % 2):64 * (wdw % 2) + 64, p, c0:c0 + WIN]
                            mm = pe.matmul(dst, k if turned else q, q if turned else k, start=True, stop=True)
                mm.then_inc(big_ready(key), 1)

            def windows(s, it, u):
                window_scores(s, it, (s, "windows", u), False)

            def windows_T(s, it, u):
                window_scores(s, it, (s, "windows_T", u), True)

            def max_turn(s, it, a):
                key, last = (s, "maxT", a), (s, "windows", 1) if a == A_3W else (s, "scores", a, HP - 1)
                for t in tiles(it, free=[key], taken=[last]):
                    pe.wait_ge(*t)
                for t in range(NT):
                    mm = pe.transpose(small(key)[0:16, t * 128:(t + 1) * 128], rowmax[s][:, t].rearrange("p a h -> p (a h)"), ident[:, :])
                mm.then_inc(small_ready(key), 1)

            def values(s, it, a, j):
                probs = (s, "topT", j) if a == A_3C else (s, "scores_T", a, j)
                for t in tiles(it, taken=[probs] + [(s, "v", a)] * (j == 0)):
                    pe.wait_ge(*t)
                if j == HP // 2:
                    pe.wait_ge(*of("out_free", s, it, 2 * a + 1))
                lo = (j // 2) % 2 * T
                for k in range(NT):
                    for p in range(2):
                        h = 2 * j + p
                        q4 = VW * (h % 4)
                        mm = pe.matmul(OUT[s][q4:q4 + VW, lo:lo + T], V[s][:, k * H + h, :], PT[s][:, h % (2 * PT_UNITS), k, :],
                                       start=(k == 0), stop=(k == NT - 1), skip_group_check=True)
                if j in (HP // 2 - 1, HP - 1):
                    mm.then_inc(S["out_full"][s], 1)

            def window_values(s, it, half):
                if half == 0:
                    for t in tiles(it, taken=[(s, "windows_T", 0), (s, "windows_T", 1), (s, "v", A_3W)]):
                        pe.wait_ge(*t)
                else:
                    pe.wait_ge(*of("out_free", s, it, 2 * A_3W + 1))
                pe.sem_inc(passed["pe"], 1)
                r = slice(64 * half, 64 * half + 64)
                for h in range(H):
                    i, p = h // 2, h % 2
                    probs = PT[s][r, (i // 4) * 2 + p].rearrange("p k t -> p (k t)")
                    q4 = VW * (h % 4)
                    for t in range(NT):
                        lo, b0 = (h // 4) * 128 + t * WIN, (t * 4 + i % 4) * WIN
                        mm = pe.matmul(OUT[s][q4:q4 + VW, lo:lo + WIN], V[s][r, t * H + h, :], probs[:, b0:b0 + WIN], start=True, stop=True)
                mm.then_inc(S["out_full"][s], 1)

            def top(s, it, j):
                key = (s, "top", j)
                if j == 0:
                    pe.wait_ge(*of("stacked", s, it, 64 * (A_3C + 1)))
                pe.wait_ge(*big_is_free(it, key))
                for t in range(NT):
                    for p in range(2):
                        r = slice(64 * p, 64 * p + ROWS)
                        mm = pe.matmul(big(key)[:, p, t * T:(t + 1) * T], Qs[s][r, j, t * 128:(t + 1) * 128], Ks[s][r, j, :], start=True, stop=True)
                mm.then_inc(big_ready(key), 1)

            def top_turn(s, it, j):
                key, g = (s, "topT", j), top_unit[s, j]
                pe.wait_ge(p_done, it * (SLOTS * HP) + g + 1)
                pe.wait_ge(*big_is_free(it, key))
                for p in range(2):
                    for k in range(NT):
                        for t in range(NT):
                            c0 = k * T + t * 128
                            mm = pe.transpose(big(key)[:, p, c0:c0 + 128], ptop[:, g % CHOSEN_BUFS, 2 * p + t, k * 128:(k + 1) * 128], ident[:, :])
                mm.then_inc(big_ready(key), 1)

            def out_natural(s, it, a):
                key = (s, "out_natural", a)
                pe.wait_ge(*of("out_free", s, it, 2 * a + 2))
                pe.wait_ge(*big_is_free(it, key))
                for g in range(H // 4):
                    for t in range(NT):
                        mm = pe.transpose(big(key)[:, t, g * 128:(g + 1) * 128], OT[s][:, g, t * 128:(t + 1) * 128], ident[:, :])
                mm.then_inc(big_ready(key), 1)

            def out_turn(s, it, a):
                pe.wait_ge(*big_taken(it, (s, "out_natural", a)))
                turn((s, "out_turn", a), s, lambda t: on[s][:, t, :], it)

            def project(s, it, a):
                natural((s, "project", a), it, [(oT[s], w(f"o{a}"))], f"bo{a}", taken=[(s, "out_turn", a)])

            def hidden(s, it, key, n, mat, lo):
                pe.wait_ge(*small_taken(it, (s, "turn", n)))
                pe.wait_ge(*big_is_free(it, key))
                for i in range(4):
                    mm = pe.matmul(big(key)[:, i // 2, (i % 2) * T:(i % 2 + 1) * T], w(mat, lo + i * C, C), hT[s][:, :], start=True, stop=True)
                mm.then_inc(big_ready(key), 1)

            def gelu_hidden(s, it):
                hidden(s, it, (s, "gelu"), LN_2M, "l2_w1", 0)

            def swiglu_gate(s, it):
                hidden(s, it, (s, "swiglu"), LN_3M, "l3_w1", 0)

            def swiglu_up(s, it):
                hidden(s, it, (s, "swiglu_up"), LN_3M, "l3_w1", HID)

            def mlp_out(s, it, key, done, mat, name, ones):
                pe.wait_ge(*big_taken(it, done))
                natural(key, it, [(hid[s][:, i, :], w(mat, i * C, C)) for i in range(4)], name, ones)

            def mlp2(s, it):
                mlp_out(s, it, (s, "mlp2"), (s, "gelu"), "l2_w2", "l2_b2", ones3)

            def mlp3(s, it):
                mlp_out(s, it, (s, "mlp3"), (s, "swiglu_up"), "l3_w2", "l3_b2", twos3)

            pe.wait_ge(ident_loaded, 16)
            pe.wait_ge(const_set, CONSTS)
            pe.wait_ge(pool_const, POOL_CONSTS)
            with pe.Fori(0, B // SLOTS) as it:
                follow(it, dict(
                    mods=mods, gates=gate_rows, turn=norm_turn, l0_qkv=l0_qkv, l0_scores=l0_scores, l0_probs_turn=l0_probs_turn,
                    l0_evidence=l0_evidence, l0_router=l0_router, l0_hidden=l0_hidden, l0_experts=l0_experts,
                    l0_routed_turn=l0_routed_turn, l0_out=l0_out, qkv=qkv, scores=scores, maxT=max_turn, scores_T=scores_T,
                    values=values, windows=windows, windows_T=windows_T, window_values=window_values, top=top, topT=top_turn,
                    out_natural=out_natural, out_turn=out_turn, project=project, gelu=gelu_hidden, mlp2=mlp2,
                    swiglu=swiglu_gate, swiglu_up=swiglu_up, mlp3=mlp3))

        @block.scalar
        def _(act):
            def tanh_cond(s, it):
                act.wait_ge(*of("loaded", s, it, 64))
                nc.scalar.activation(tc_[s][:, :], cond[s][:, :], ACT.Tanh, scale=0.5).then_inc(S["tanh_cond"][s], 1)

            def gates_out(s, it):
                key = (s, "gates")
                act.wait_ge(*big_filled(it, key))
                nc.scalar.copy(gates[s][:, 0:2, :].rearrange("p g c -> p (g c)"), big(key)[:, 0, 0:2 * C])
                nc.scalar.copy(gates[s][:, 2:5, :].rearrange("p g c -> p (g c)"), big(key)[:, 1, 0:3 * C]).then_inc(big_freed(key), 1)

            def take(s, it, key, dst, src):
                act.wait_ge(*small_filled(it, key))
                nc.scalar.copy(dst, src).then_inc(small_freed(key), 1)

            def norm_out(s, it, n):
                key = (s, "turn", n)
                if n == LN_L0:
                    sc, sh = col("ln_g"), col("ln_b")
                elif n == LN_2C:
                    sc, sh = col("n2_g"), col("n2_b")
                else:
                    m = {LN_Q: "q", LN_KV: "kv", LN_2A: "l2a", LN_2M: "l2m", LN_3A: "l3a", LN_3C: "l3c", LN_3M: "l3m"}[n]
                    sc, sh = mod[s][:, SC[m]:SC[m] + 1], mod[s][:, SH[m]:SH[m] + 1]
                act.wait_ge(*small_filled(it, key))
                dst, src = (kvT if n == LN_KV else hT)[s], small(key)
                if n == LN_3A:
                    nc.scalar.activation(dst[:, 0:T - SHIFT], src[:, SHIFT:T], ACT.Identity, scale=sc, bias=sh)
                    nc.scalar.activation(dst[:, T - SHIFT:T], src[:, 0:SHIFT], ACT.Identity, scale=sc, bias=sh).then_inc(small_freed(key), 1)
                else:
                    nc.scalar.activation(dst[:, :], src[:, 0:T], ACT.Identity, scale=sc, bias=sh).then_inc(small_freed(key), 1)

            def l0_exp(s, it):
                key = (s, "l0_scores")
                act.wait_ge(*of("softmax0_step", s, it, 2))
                for t in range(NT):
                    last = nc.scalar.activation(p0[s][:, t, :], small(key)[:, t * T:(t + 1) * T], ACT.Exp, scale=SCALE0,
                                                bias=nm0[s][:, t:t + 1], accum_out=z0[s][:, t:t + 1])
                last.then_inc(small_freed(key), 1)

            def l0_router_exp(s, it):
                act.wait_ge(*small_taken(it, (s, "l0_router")))
                nc.scalar.activation(rl[s][:, :, :], rl[s][:, :, :], ACT.Exp).then_inc(S["router_exp"][s], 1)

            def l0_tanh(s, it, half):
                key = (s, "l0_hidden", half)
                if half == 0:
                    act.wait_ge(*of("mod_step", s, it, 2))
                act.wait_ge(*big_filled(it, key))
                for i in range(4 * half, min(4 * half + 4, 7)):
                    n = i - 4 * half
                    last = nc.scalar.activation(th[s][:, i, :], big(key)[:, n // 2, (n % 2) * T:(n % 2 + 1) * T], ACT.Tanh,
                                                scale=0.5, bias=half_anchor[s][:, i:i + 1])
                last.then_inc(S["tanh0_done"][s], 1)

            def l0_gate_tanh(s, it):
                key = (s, "l0_gate")
                act.wait_ge(*small_filled(it, key))
                nc.scalar.activation(th[s][:, 7, :], small(key)[:, 0:T], ACT.Tanh, scale=0.25).then_inc(small_freed(key), 1)

            def first_parts(s, it, a):
                key = (s, "qkv", a)
                act.wait_ge(*small_filled(it, key))
                nc.scalar.activation(parts[s][:, 0, 0, :], small(key)[:, 0:T], ACT.Identity, bias=col(f"bq{a}"))
                nc.scalar.activation(parts[s][:, 0, 1, :], small(key)[:, T:2 * T], ACT.Identity, bias=col(f"bk{a}")).then_inc(S["part1_done"][s], 1)
                key = (s, "v", a)
                take(s, it, key, V[s][:, :, 0:D], small(key)[:, 0:T].rearrange("p (h d) -> p h d", d=D))

            def probabilities(s, it, a, j):
                key = (s, "scores_T", a, j)
                c = 2 * (j % PT_UNITS)
                act.wait_ge(*big_filled(it, key))
                nc.scalar.activation(PT[s][:, c:c + 2].rearrange("p a b t -> p a (b t)"), big(key)[:, :, :], ACT.Exp,
                                     scale=SCALE).then_inc(big_freed(key), 1)

            def window_probabilities(s, it, u):
                key = (s, "windows_T", u)
                act.wait_ge(*big_filled(it, key))
                nc.scalar.activation(PT[s][:, 2 * u:2 * u + 2].rearrange("p a b t -> p a (b t)"), big(key)[:, :, :], ACT.Exp,
                                     scale=SCALE).then_inc(big_freed(key), 1)

            def half_out(s, it, a, j):
                if j not in (HP // 2 - 1, HP - 1):
                    return
                half = j // (HP // 2)
                act.wait_ge(*of("out_full", s, it, 2 * a + half + 1))
                nc.scalar.copy(OT[s][:, 2 * half:2 * half + 2, :], OUT[s][:, :].rearrange("p (g t) -> p g t", g=2)).then_inc(S["out_free"][s], 1)

            def window_half_out(s, it, half):
                act.wait_ge(*of("out_full", s, it, 2 * A_3W + half + 1))
                dst = OT[s][:, :, :].rearrange("p g (t w q) -> p (g t) w q", t=NT, w=2)[:, :, half, :]
                nc.scalar.copy(dst, OUT[s][:, :].rearrange("p (g q) -> p g q", q=WIN)).then_inc(S["out_free"][s], 1)

            def output_out(s, it, a):
                key = (s, "out_turn", a)
                if a == A_3W:
                    act.wait_ge(*small_filled(it, key))
                    nc.scalar.copy(oT[s][:, SHIFT:T], small(key)[:, 0:T - SHIFT])
                    nc.scalar.copy(oT[s][:, 0:SHIFT], small(key)[:, T - SHIFT:T]).then_inc(small_freed(key), 1)
                else:
                    take(s, it, key, oT[s][:, :], small(key)[:, 0:T])

            def top_exp(s, it, j):
                key, g = (s, "top", j), top_unit[s, j]
                act.wait_ge(top_step, it * (SLOTS * HP * 4) + 4 * g + 2)
                if g >= 2:
                    act.wait_ge(p_done, it * (SLOTS * HP) + g - 1)
                for i in range(4):
                    last = nc.scalar.activation(e_all[:, g % 2, i, :], big(key)[:, i // 2, (i % 2) * T:(i % 2 + 1) * T], ACT.Exp,
                                                scale=SCALE, bias=ntop[:, g % 2, i:i + 1])
                last.then_inc(big_freed(key), 1)

            def rest_exp(s, it, j):
                g = top_unit[s, j]
                act.wait_ge(top_step, it * (SLOTS * HP * 4) + 4 * g + 4)
                for i in range(4):
                    last = nc.scalar.activation(e_rest[:, g % 2, i, :], s1[:, g % 2, i, :], ACT.Exp,
                                                scale=SCALE, bias=ntop[:, g % 2, i:i + 1])
                last.then_inc(e_done, 1)

            def chosen_out(s, it, j):
                key, c = (s, "topT", j), 2 * (j % PT_UNITS)
                act.wait_ge(*big_filled(it, key))
                nc.scalar.copy(PT[s][:, c:c + 2].rearrange("p a b t -> p a (b t)"), big(key)[:, :, :]).then_inc(big_freed(key), 1)

            def gelu(s, it):
                key = (s, "gelu")
                act.wait_ge(*big_filled(it, key))
                for i in range(4):
                    last = nc.scalar.activation(hid[s][:, i, :], big(key)[:, i // 2, (i % 2) * T:(i % 2 + 1) * T], ACT.Gelu_apprx_tanh,
                                                bias=col(f"l2_b1_{i}"))
                last.then_inc(big_freed(key), 1)

            def swiglu_tanh(s, it):
                key = (s, "swiglu")
                act.wait_ge(*big_filled(it, key))
                for i in range(4):
                    last = nc.scalar.activation(th[s][:, i, :], big(key)[:, i // 2, (i % 2) * T:(i % 2 + 1) * T], ACT.Tanh,
                                                scale=0.5, bias=half_b[:, i:i + 1])
                last.then_inc(S["tanh3_done"][s], 1)

            def l0_values_out(s, it):
                key = (s, "l0_qkv")
                take(s, it, key, qk0[s][:, :, :].rearrange("p a t -> p (a t)"), small(key)[:, :])
                key = (s, "v")
                take(s, it, key, upd[s][:, :, :], nat(small(key)))

            def l0_probs_out(s, it):
                key = (s, "l0_probs_turn")
                take(s, it, key, p0T[s][:, :, :].rearrange("p k t -> p (k t)"), small(key)[:, :])

            def l0_evidence_out(s, it):
                key = (s, "l0_evidence")
                take(s, it, key, kvT[s][:, :], small(key)[:, 0:T])

            def l0_routed_out(s, it):
                key = (s, "l0_routed_turn")
                take(s, it, key, oT[s][:, :], small(key)[:, 0:T])

            for g in MATS:
                lo = GROUP_AT[g]
                n = sum(c for _, c in MATS[g])
                act.dma_start(W[:, lo:lo + n], ins["mats"][:, lo:lo + n]).then_inc(group_loaded[g], 16)
            act.wait_ge(cols_loaded, 16)
            with act.Fori(0, B // SLOTS) as it:
                follow(it, dict(
                    cond=tanh_cond, gates=gates_out, turn=norm_out, l0_qkv=l0_values_out, l0_scores=l0_exp, l0_probs_turn=l0_probs_out,
                    l0_evidence=l0_evidence_out, l0_router=l0_router_exp, l0_hidden=l0_tanh, l0_routed_turn=l0_routed_out,
                    l0_out=l0_gate_tanh, qkv=first_parts, scores_T=probabilities, windows_T=window_probabilities,
                    values=half_out, window_values=window_half_out, top=top_exp, rest=rest_exp, topT=chosen_out,
                    out_turn=output_out, gelu=gelu, swiglu=swiglu_tanh))

        @block.vector
        def _(dve):
            def cond_silu(s, it):
                dve.wait_ge(*of("tanh_cond", s, it, 1))
                nc.vector.scalar_tensor_tensor(out=silu[s][:, :], in0=tc_[s][:, :], scalar=1.0, in1=cond[s][:, :],
                                               op0=ALU.add, op1=ALU.mult).then_inc(S["silu_step"][s], 1)
                dve.wait_ge(*of("silu_step", s, it, 1))
                nc.vector.tensor_scalar(silu[s][:, :], silu[s][:, :], 0.5, None, ALU.mult).then_inc(S["silu_step"][s], 1)
                nc.vector.tensor_copy(condB[s][:, :], cond[s][:, 0:1].to_broadcast([128, 128])).then_inc(S["silu_step"][s], 1)
                dve.wait_ge(*of("silu_step", s, it, 2))
                nc.vector.tensor_copy(siluB[s][:, :], silu[s][:, 0:1].to_broadcast([128, 128])).then_inc(S["silu_step"][s], 1)

            def mods_out(s, it):
                key = (s, "mods")
                dve.wait_ge(*small_filled(it, key))
                nc.vector.tensor_tensor(mod[s][:, :], small(key)[:, 0:21], col("mod0", 21), ALU.add).then_inc(small_freed(key), 1)
                dve.wait_ge(*small_taken(it, key))
                nc.vector.tensor_scalar(mod[s][:, 0:7], mod[s][:, 0:7], 1.0, None, ALU.add).then_inc(S["mod_step"][s], 1)
                nc.vector.tensor_scalar(half_anchor[s][:, :], mod[s][:, 14:21], 0.5, None, ALU.mult).then_inc(S["mod_step"][s], 1)

            def norm_stats(s, it, n):
                src = cx if n == LN_KV else x
                if n == LN_L0:
                    dve.wait_ge(*of("loaded", s, it, 64))
                elif n != LN_KV:
                    dve.wait_ge(*of("x_updated", s, it, UPDATES_BEFORE[n]))
                for t in range(NT):
                    last = nc.vector.bn_stats(stats[s][:, n % 2, t, :], src[s][:, t, :])
                last.then_inc(S["bn_done"][s], 1)
                dve.wait_ge(*of("bn_done", s, it, n + 1))
                dve.sem_inc(passed["dve"], 1)
                for t in range(NT):
                    last = nc.vector.bn_aggr(mv[s][:, n % 2, t, :], stats[s][:, n % 2, t, :])
                last.then_inc(S["mv_done"][s], 1)
                dve.wait_ge(*of("mv_done", s, it, n + 1))
                nc.vector.tensor_scalar(ve[s][:, n % 2, :], mv[s][:, n % 2, :, 1], EPS[n], None, ALU.add).then_inc(S["ve_done"][s], 1)

            def norm_apply(s, it, n):
                src = cx if n == LN_KV else x
                dve.wait_ge(*of("rstd_done", s, it, n + 1))
                for t in range(NT):
                    last = nc.vector.tensor_scalar(xn[s][:, n % 2, t, :], src[s][:, t, :], mv[s][:, n % 2, t, 0:1],
                                                   rstd[s][:, n % 2, t:t + 1], ALU.subtract, ALU.mult)
                last.then_inc(S["xn_done"][s], 1)

            def l0_max(s, it):
                key = (s, "l0_scores")
                dve.wait_ge(*small_filled(it, key))
                nc.vector.tensor_reduce(m0[s][:, :], small(key)[:, :].rearrange("p (t k) -> p t k", t=NT), AX_X, ALU.max)\
                    .then_inc(S["softmax0_step"][s], 1)
                dve.wait_ge(*of("softmax0_step", s, it, 1))
                nc.vector.tensor_scalar(nm0[s][:, :], m0[s][:, :], -SCALE0, None, ALU.mult).then_inc(S["softmax0_step"][s], 1)

            def l0_normalise(s, it):
                dve.wait_ge(*small_taken(it, (s, "l0_scores")))
                nc.vector.reciprocal(m0[s][:, :], z0[s][:, :]).then_inc(S["softmax0_step"][s], 1)
                dve.wait_ge(*of("softmax0_step", s, it, 3))
                for t in range(NT):
                    last = nc.vector.tensor_scalar(p0[s][:, t, :], p0[s][:, t, :], m0[s][:, t:t + 1], None, ALU.mult)
                last.then_inc(S["softmax0_step"][s], 1)

            def l0_router_max(s, it):
                key = (s, "l0_router")
                dve.wait_ge(*small_filled(it, key))
                logits = small(key)[:, 0:4 * NT].rearrange("p (t e) -> p t e", e=4)[:, :, 0:E3]
                nc.vector.tensor_reduce(rm[s][:, :], logits, AX_X, ALU.max).then_inc(S["router_step"][s], 1)
                dve.wait_ge(*of("router_step", s, it, 1))
                nc.vector.tensor_tensor(rl[s][:, :, :], logits, rm[s][:, :].unsqueeze(2).to_broadcast([128, NT, E3]), ALU.subtract)\
                    .then_inc(small_freed(key), 1)

            def l0_router_norm(s, it):
                dve.wait_ge(*of("router_exp", s, it, 1))
                nc.vector.tensor_reduce(rm[s][:, :], rl[s][:, :, :], AX_X, ALU.add).then_inc(S["router_step"][s], 1)
                dve.wait_ge(*of("router_step", s, it, 2))
                nc.vector.reciprocal(rm[s][:, :], rm[s][:, :]).then_inc(S["router_step"][s], 1)
                dve.wait_ge(*of("router_step", s, it, 3))
                nc.vector.scalar_tensor_tensor(out=rl[s][:, :, :], in0=rl[s][:, :, :], scalar=0.5,
                                               in1=rm[s][:, :].unsqueeze(2).to_broadcast([128, NT, E3]),
                                               op0=ALU.mult, op1=ALU.mult).then_inc(S["router_step"][s], 1)

            def l0_silu(s, it, half):
                key = (s, "l0_hidden", half)
                lo, hi = 4 * half, min(4 * half + 4, 7)
                dve.wait_ge(*of("tanh0_done", s, it, half + 1))
                nc.vector.tensor_scalar(th[s][:, lo:hi, :], th[s][:, lo:hi, :], 1.0, None, ALU.add).then_inc(S["silu0_step"][s], 1)
                dve.wait_ge(*of("silu0_step", s, it, half + 1))
                for i in range(lo, hi):
                    n = i - lo
                    last = nc.vector.scalar_tensor_tensor(out=hid[s][:, i, :], in0=big(key)[:, n // 2, (n % 2) * T:(n % 2 + 1) * T],
                                                          scalar=mod[s][:, 14 + i:15 + i], in1=th[s][:, i, :], op0=ALU.add, op1=ALU.mult)
                last.then_inc(big_freed(key), 1)

            def l0_route(s, it):
                key = (s, "l0_experts")
                dve.wait_ge(*of("router_step", s, it, 4))
                dve.wait_ge(*big_filled(it, key))
                for e in range(E3):
                    if e:
                        dve.wait_ge(*of("routed_step", s, it, e))
                    for t in range(NT):
                        src, prob = big(key)[:, t, e * C:(e + 1) * C], rl[s][:, t, e:e + 1]
                        if e == 0:
                            last = nc.vector.tensor_scalar(upd[s][:, t, :], src, prob, None, ALU.mult)
                        else:
                            last = nc.vector.scalar_tensor_tensor(out=upd[s][:, t, :], in0=src, scalar=prob, in1=upd[s][:, t, :],
                                                                  op0=ALU.mult, op1=ALU.add)
                    last.then_inc(S["routed_step"][s] if e < E3 - 1 else big_freed(key), 1)

            def l0_update(s, it):
                key = (s, "l0_out")
                dve.wait_ge(*small_taken(it, (s, "l0_gate")))
                dve.wait_ge(*small_filled(it, key))
                nc.vector.scalar_tensor_tensor(out=upd[s][:, :, :], in0=th[s][:, 7, :].rearrange("p (t c) -> p t c", t=NT), scalar=1.0,
                                               in1=nat(small(key)), op0=ALU.add, op1=ALU.mult).then_inc(small_freed(key), 1)
                dve.wait_ge(*small_taken(it, key))
                nc.vector.scalar_tensor_tensor(out=x[s][:, :, :], in0=upd[s][:, :, :], scalar=0.5, in1=x[s][:, :, :],
                                               op0=ALU.mult, op1=ALU.add).then_inc(S["x_updated"][s], 1)

            def update(s, it, key, gate=None, factor=1.0):
                dve.wait_ge(*small_filled(it, key))
                if gate is None:
                    nc.vector.tensor_tensor(upd[s][:, :, :], nat(small(key)), x[s][:, :, :], ALU.add).then_inc(small_freed(key), 1)
                    dve.wait_ge(*small_taken(it, key))
                    nc.vector.tensor_copy(x[s][:, :, :], upd[s][:, :, :]).then_inc(S["x_updated"][s], 1)
                else:
                    g = GATE[gate]
                    nc.vector.scalar_tensor_tensor(out=upd[s][:, :, :], in0=nat(small(key)), scalar=factor,
                                                   in1=gates[s][:, g:g + 1, :].to_broadcast([128, NT, C]),
                                                   op0=ALU.mult, op1=ALU.mult).then_inc(small_freed(key), 1)
                    dve.wait_ge(*small_taken(it, key))
                    nc.vector.tensor_tensor(x[s][:, :, :], upd[s][:, :, :], x[s][:, :, :], ALU.add).then_inc(S["x_updated"][s], 1)

            def residues(s, it, a):
                key = (s, "qkv", a)
                dve.wait_ge(*of("part1_done", s, it, a + 1))
                for i, b in enumerate((f"bq{a}", f"bk{a}")):
                    last = nc.vector.scalar_tensor_tensor(out=resid[s][:, i, :], in0=small(key)[:, i * T:(i + 1) * T], scalar=col(b),
                                                          in1=parts[s][:, 0, i, :], op0=ALU.add, op1=ALU.subtract)
                last.then_inc(small_freed(key), 1)
                dve.wait_ge(*small_taken(it, key))
                nc.vector.tensor_copy(parts[s][:, 1, :, :], resid[s][:, :, :]).then_inc(S["part2_done"][s], 1)
                dve.wait_ge(*of("part2_done", s, it, a + 1))
                nc.vector.tensor_tensor(parts[s][:, 2, :, :], resid[s][:, :, :], parts[s][:, 1, :, :], ALU.subtract)\
                    .then_inc(S["parts_done"][s], 1)

            def window_maxima(s, it, u):
                key = (s, "windows", u)
                dve.wait_ge(*big_filled(it, key))
                for p in range(2):
                    last = nc.vector.tensor_reduce(rowmax[s][:, :, p, 4 * u:4 * u + 4],
                                                   big(key)[:, p, :].rearrange("q (w i k) -> q w i k", w=NT, k=WIN), AX_X, ALU.max)
                last.then_inc(big_freed(key), 1)

            def maxima(s, it, a, j):
                key = (s, "scores", a, j)
                dve.wait_ge(*big_filled(it, key))
                nc.vector.tensor_reduce(rowmax[s][:, :, :, j].rearrange("q t p -> q p t"),
                                        big(key)[:, :, :].rearrange("q p (t k) -> q p t k", t=NT), AX_X, ALU.max)\
                    .then_inc(big_freed(key), 1)

            def minus_maxima(s, it, a):
                key = (s, "maxT", a)
                dve.wait_ge(*small_filled(it, key))
                nc.vector.tensor_scalar(negmax[s][:, 0, :], small(key)[0:16, 0:T], -1.0, None, ALU.mult).then_inc(S["negmax_step"][s], 1)
                dve.wait_ge(*of("negmax_step", s, it, a + 1))
                nc.vector.scalar_tensor_tensor(out=negmax[s][:, 1, :], in0=small(key)[0:16, 0:T], scalar=-1.0, in1=negmax[s][:, 0, :],
                                               op0=ALU.mult, op1=ALU.subtract).then_inc(small_freed(key), 1)

            def normalise(s, it, a):
                key = (s, "out_natural", a)
                dve.wait_ge(*big_filled(it, key))
                o = big(key)[:, :, :].rearrange("p t (h d) -> p t h d", d=VW)
                den = rden[s][:, :].rearrange("p (t h) -> p t h", t=NT)
                nc.vector.reciprocal(den, o[:, :, :, D]).then_inc(S["rden_done"][s], 1)
                dve.wait_ge(*of("rden_done", s, it, a + 1))
                for t in range(NT):
                    last = nc.vector.tensor_tensor(on[s][:, t, :].rearrange("p (h d) -> p h d", d=D), o[:, t, :, 0:D],
                                                   den[:, t, :].unsqueeze(2).to_broadcast([128, H, D]), ALU.mult)
                last.then_inc(big_freed(key), 1)

            def top_16(s, it, j):
                key, g = (s, "top", j), top_unit[s, j]
                b = g % 2
                tile = [big(key)[:, i // 2, (i % 2) * T:(i % 2 + 1) * T] for i in range(4)]
                done = it * (SLOTS * HP * 4) + 4 * g
                dve.wait_ge(*big_filled(it, key))
                dve.sem_inc(passed["dve"], 1)
                for i in range(4):
                    last = nc.vector.max(m8[:, b, 0, i, :], tile[i])
                last.then_inc(top_step, 1)
                if g >= 2:
                    dve.wait_ge(e_done, it * (SLOTS * HP) + g - 1)
                dve.wait_ge(top_step, done + 1)
                nc.vector.tensor_scalar(ntop[:, b, :], m8[:, b, 0, :, 0], -SCALE, None, ALU.mult)
                for i in range(4):
                    last = nc.vector.match_replace(s1[:, b, i, :], m8[:, b, 0, i, :], tile[i], NEG)
                last.then_inc(top_step, 1)
                dve.wait_ge(top_step, done + 2)
                dve.sem_inc(passed["dve"], 1)
                for i in range(4):
                    last = nc.vector.max(m8[:, b, 1, i, :], s1[:, b, i, :])
                last.then_inc(top_step, 1)
                dve.wait_ge(top_step, done + 3)
                dve.sem_inc(passed["dve"], 1)
                for i in range(4):
                    last = nc.vector.match_replace(s1[:, b, i, :], m8[:, b, 1, i, :], s1[:, b, i, :], NEG)
                last.then_inc(top_step, 1)

            def swiglu(s, it):
                ka = (s, "swiglu")
                dve.wait_ge(*of("tanh3_done", s, it, 1))
                nc.vector.tensor_scalar(th[s][:, 0:4, :], th[s][:, 0:4, :], 1.0, None, ALU.add).then_inc(S["swiglu_step"][s], 1)
                dve.wait_ge(*of("swiglu_step", s, it, 1))
                for i in range(4):
                    last = nc.vector.scalar_tensor_tensor(out=hid[s][:, i, :], in0=big(ka)[:, i // 2, (i % 2) * T:(i % 2 + 1) * T],
                                                          scalar=col(f"l3_b1_{i}"), in1=th[s][:, i, :], op0=ALU.add, op1=ALU.mult)
                last.then_inc(big_freed(ka), 1)

            def swiglu_up(s, it):
                ka, kb = (s, "swiglu"), (s, "swiglu_up")
                for t in [big_taken(it, ka), big_filled(it, kb)]:
                    dve.wait_ge(*t)
                for i in range(4):
                    last = nc.vector.scalar_tensor_tensor(out=hid[s][:, i, :], in0=big(kb)[:, i // 2, (i % 2) * T:(i % 2 + 1) * T],
                                                          scalar=col(f"l3_b1_{4 + i}"), in1=hid[s][:, i, :], op0=ALU.add, op1=ALU.mult)
                last.then_inc(big_freed(kb), 1)

            def project_out(s, it, a):
                update(s, it, (s, "project", a), {A_2S: "l2a", A_3W: "l3a", A_3C: "l3c"}.get(a))

            def mlp2_out(s, it):
                update(s, it, (s, "mlp2"), "l2m")

            def mlp3_out(s, it):
                update(s, it, (s, "mlp3"), "l3m", 0.5)

            both = range(SLOTS)
            for f in big_free + small_free:
                dve.sem_inc(f, 1)
            nc.vector.memset(ones3[:, :], 1.0).then_inc(const_set, 1)
            nc.vector.memset(twos3[:, :], 2.0).then_inc(const_set, 1)
            dve.wait_ge(rows_loaded, 16)
            for i in range(PARTS):
                nc.vector.tensor_copy(row_parts[:, i, :], rowf[:, :]).then_inc(split_step, 1)
                if i < PARTS - 1:
                    dve.wait_ge(split_step, 2 * i + 1)
                    nc.vector.tensor_tensor(rowf[:, :], rowf[:, :], row_parts[:, i, :], ALU.subtract).then_inc(split_step, 1)
                    dve.wait_ge(split_step, 2 * i + 2)
            dve.wait_ge(cols_loaded, 16)
            nc.vector.tensor_scalar(half_b[:, :], col("l3_b1_0", 4), 0.5, None, ALU.mult).then_inc(const_set, 1)

            with dve.Fori(0, B // SLOTS) as it:
                follow(it, dict(
                    cond=cond_silu, mods=mods_out, stats=norm_stats, apply=norm_apply, l0_scores=l0_max, l0_normalise=l0_normalise,
                    l0_router=l0_router_max, l0_router_norm=l0_router_norm, l0_hidden=l0_silu, l0_experts=l0_route,
                    l0_out=l0_update, qkv=residues, scores=maxima, windows=window_maxima, maxT=minus_maxima, top=top_16,
                    out_natural=normalise, project=project_out, mlp2=mlp2_out, swiglu=swiglu, swiglu_up=swiglu_up, mlp3=mlp3_out))

        @block.gpsimd
        def _(pool):
            def inverse_root(s, it, n):
                pool.wait_ge(*of("ve_done", s, it, n + 1))
                nc.gpsimd.tensor_tensor(rstd[s][:, n % 2, :], ve[s][:, n % 2, :], minus_half[:, :], ALU.pow).then_inc(S["rstd_done"][s], 1)

            def chosen(s, it, j):
                g = top_unit[s, j]
                pool.wait_ge(e_done, it * (SLOTS * HP) + g + 1)
                if g >= CHOSEN_BUFS:
                    t, i = top_order[g - CHOSEN_BUFS]
                    pool.wait_ge(*big_filled(it, (t, "topT", i)))
                nc.gpsimd.tensor_tensor(ptop[:, g % CHOSEN_BUFS, :, :], e_all[:, g % 2, :, :], e_rest[:, g % 2, :, :], ALU.subtract)\
                    .then_inc(p_done, 1)

            constants = [(minus_half[:, :], -0.5)]
            for s in range(SLOTS):
                constants += [(Ks[s][p:p + 32, :, :], 1.0) for p in (32, 96)]
                constants += [(V[s][:, :, D + 1:VW], 0.0), (V[s][:, :, D:D + 1], 1.0)]
            assert len(constants) == POOL_CONSTS
            for n, (dst, value) in enumerate(constants):
                nc.gpsimd.memset(dst, value).then_inc(pool_const, 1)
                pool.wait_ge(pool_const, n + 1)
            with pool.Fori(0, B // SLOTS) as it:
                follow(it, dict(stats=inverse_root, rest=chosen))


def kernel(**inputs):
    import numpy as np
    import concourse.bacc as bacc
    from concourse.bass_utils import run_bass_kernel_spmd

    a = {k: np.asarray(v) for k, v in inputs.items()}
    l0, l1, l2, l3 = ({k[len(p):]: v for k, v in a.items() if k.startswith(p)} for p in
                      ("L0_xcond_", "L1_xcond_", "L2_xcond_", "L3_xcond_"))
    turn = [(2 * h2 + p) * D + d for d in range(D) for p in range(2) for h2 in range(HP)]
    plain = list(range(C))

    def thirds(m, i):
        return m[..., i * C:(i + 1) * C]

    qkvo = [
        (l1["Wq"], l1["bq"], thirds(l1["Wkv"], 0), thirds(l1["bkv"], 0), thirds(l1["Wkv"], 1), thirds(l1["bkv"], 1), l1["Wp"], l1["bp"]),
        (*(f(l2[n], i) for i in (0, 1, 2) for f, n in ((thirds, "qkv_w"), (thirds, "qkv_b"))), l2["self_o_w"], l2["self_o_b"]),
        (l2["q_w"], l2["q_b"], thirds(l2["kv_w"], 0), thirds(l2["kv_b"], 0), thirds(l2["kv_w"], 1), thirds(l2["kv_b"], 1), l2["cross_o_w"], l2["cross_o_b"]),
        (*(f(l3[n], i) for i in (0, 1, 2) for f, n in ((thirds, "w_qkv"), (thirds, "b_qkv"))), l3["w_so"], l3["b_so"]),
        (l3["w_q"], l3["b_q"], thirds(l3["w_kv"], 0), thirds(l3["b_kv"], 0), thirds(l3["w_kv"], 1), thirds(l3["b_kv"], 1), l3["w_co"], l3["b_co"]),
    ]
    q_ss, kv_ss, ada2, ada3 = (l1["Wss_q"], l1["bss_q"]), (l1["Wss_kv"], l1["bss_kv"]), (l2["ada_w"], l2["ada_b"]), (l3["w_ada"], l3["b_ada"])
    scales = [(*q_ss, 0), (*kv_ss, 0), (*ada2, 1), (*ada2, 4), (*ada3, 1), (*ada3, 4), (*ada3, 7)]
    shifts = [(*q_ss, 1), (*kv_ss, 1), (*ada2, 0), (*ada2, 3), (*ada3, 0), (*ada3, 3), (*ada3, 6)]
    gates = [(*ada2, 2), (*ada2, 5), (*ada3, 2), (*ada3, 5), (*ada3, 8)]

    def by_rows(m):
        return np.concatenate([m[i * C:(i + 1) * C] for i in range(m.shape[0] // C)], axis=1)

    mats = {"l0_q": l0["Wq"], "l0_k": l0["Wk"], "l0_v": l0["Wv"], "l0_router": by_rows(l0["router_W"]), "l0_g2": l0["gate_w2"], "l0_out": l0["out_w"],
            "mod": np.concatenate([thirds(m, i) for m, _, i in scales + shifts], axis=1),
            "gate": np.concatenate([thirds(m, i) for m, _, i in gates], axis=1),
            "l2_w1": l2["mlp_w1"], "l2_w2": by_rows(l2["mlp_w2"]), "l3_w1": l3["w_m1"], "l3_w2": by_rows(l3["w_m2"])}
    vecs = {"ln_g": l0["ln_gamma"], "ln_b": l0["ln_beta"], "n2_g": l2["norm2_g"], "n2_b": l2["norm2_b"], "anchor6": l0["gate_b1"]}
    rows = {"router": l0["router_b"], "g2": l0["gate_b2"], "out": l0["out_b"], "l2_b2": l2["mlp_b2"], "l3_b2": l3["b_m2"]}
    for i in range(3):
        mats[f"l0_g1_{i}"] = l0["gate_w1"][i * C:(i + 1) * C]
    for e in range(E3):
        rows[f"e{e}"] = l0["e_b2"][e]
        for i in range(3):
            mats[f"l0_w1_{e}_{i}"] = l0["e_w1"][e, i * C:(i + 1) * C]
        for i in range(2):
            mats[f"l0_w2_{e}_{i}"] = l0["e_w2"][e, i * C:(i + 1) * C]
            vecs[f"anchor{2 * e + i}"] = l0["e_b1"][e, i * C:(i + 1) * C]
    for i, (_, b, n) in enumerate(scales + shifts):
        vecs[f"mod{i}"] = thirds(b, n)
    for i, (_, b, n) in enumerate(gates):
        rows[f"gate{i}"] = thirds(b, n)
    for n, (wq, bq, wk, bk, wv, bv, wo, bo) in enumerate(qkvo):
        mats[f"q{n}"], mats[f"k{n}"], mats[f"v{n}"], mats[f"o{n}"] = wq[:, turn], wk[:, turn], wv[:, plain], wo
        vecs[f"bq{n}"], vecs[f"bk{n}"], rows[f"bv{n}"], rows[f"bo{n}"] = bq[turn], bk[turn], bv, bo
    for i in range(4):
        vecs[f"l2_b1_{i}"] = l2["mlp_b1"][i * C:(i + 1) * C]
    for i in range(8):
        vecs[f"l3_b1_{i}"] = l3["b_m1"][i * C:(i + 1) * C]

    def with_more(v):
        return np.concatenate([v, v[:SLOTS]], axis=0)

    row_block = np.zeros((len(ROWV), C), np.float32)
    for name, i in ROW.items():
        row_block[i, :rows[name].shape[0]] = rows[name]
    arrays = {
        "x": with_more(a["x"]),
        "ctx": with_more(a["ctx_1024"]),
        "ctxT": with_more(np.transpose(a["ctx_1024"], (0, 2, 1))),
        "condT": with_more(a["cond_1024"][:, :, None]),
        "mats": np.ascontiguousarray(np.concatenate([mats[n] for g in MATS.values() for n, _ in g], axis=1)),
        "cols": np.ascontiguousarray(np.stack([vecs[n] for n in COLS], axis=1)),
        "rows": row_block,
        "ident": np.eye(128, dtype=np.float32),
    }
    nc = bacc.Bacc("TRN2", target_bir_lowering=False, num_devices=1)
    ins = {n: nc.dram_tensor(f"in_{n}", v.shape, mybir.dt.from_np(v.dtype), kind="ExternalInput").ap() for n, v in arrays.items()}
    out = nc.dram_tensor("out", (B, T, C), F32, kind="ExternalOutput").ap()
    chain_kernel(nc, ins, out)
    r = run_bass_kernel_spmd(nc, [{f"in_{n}": v for n, v in arrays.items()}], core_ids=[0])
    return r.results[0]["out"]
```

```python
from contextlib import ExitStack

import concourse.bass as bass
from concourse import mybir

F32 = mybir.dt.float32
BF16 = mybir.dt.bfloat16
ALU = mybir.AluOpType
ACT = mybir.ActivationFunctionType
AX_X = mybir.AxisListType.X

B, T, C = 4, 256, 128
NT = T // 128
SLOTS = 2
H, D = 16, 8
HP = H // 2
E3, HID0 = 3, 256
HID = 512
WIN, SHIFT = 64, 32
PARTS = 3
BLOCKS = 6
ROWS = BLOCKS * D
ROWSM = ROWS + 2
TURN_LAG = 1
MODS = 14 + 7 + 7
VW = 32
PT_UNITS = 4
CHOSEN_BUFS = 3
NEG = -3.0e37

SCALE0 = float(C) ** -0.5
SCALE = float(D) ** -0.5

MATS = {
    "mod": [("mod", 14 * C), ("gate", 5 * C)] + [(f"l0_w1_{e}_2", HID0) for e in range(E3)] + [("l0_g1_2", C)],
    "early": [("l0_q", C), ("l0_k", C), ("l0_v", C)],
    "l0": [("l0_router", 3 * E3)] + [(f"l0_w1_{e}_{i}", HID0) for e in range(E3) for i in range(2)]
    + [(f"l0_w2_{e}_{i}", C) for e in range(E3) for i in range(2)]
    + [(f"l0_g1_{i}", C) for i in range(2)] + [("l0_g2", C), ("l0_out", C)],
    "l1": [("q0", C), ("k0", C), ("v0", C), ("o0", C)],
    "l2": [("q1", C), ("k1", C), ("v1", C), ("o1", C), ("q2", C), ("k2", C), ("v2", C), ("o2", C),
           ("l2_w1", HID), ("l2_w2", 4 * C)],
    "l3": [("q3", C), ("k3", C), ("v3", C), ("o3", C), ("q4", C), ("k4", C), ("v4", C), ("o4", C),
           ("l3_w1", 2 * HID), ("l3_w2", 4 * C)],
}
MAT_AT, _n = {}, 0
GROUP_AT = {}
for _g, _list in MATS.items():
    GROUP_AT[_g] = _n
    for _name, _cols in _list:
        MAT_AT[_name] = (_n, _cols)
        _n += _cols
MAT_COLS = _n

COLS = ["ln_g", "ln_b"] + [f"mod{i}" for i in range(14)] + [f"anchor{i}" for i in range(7)]
COLS += [f"{x}{a}" for a in range(5) for x in ("bq", "bk")]
COLS += ["n2_g", "n2_b"] + [f"l2_b1_{i}" for i in range(4)] + [f"l3_b1_{i}" for i in range(8)]
COL = {n: i for i, n in enumerate(COLS)}

ROWV = ["router", "e0", "e1", "e2", "g2", "out"] + [f"{x}{a}" for a in range(5) for x in ("bv", "bo")]
ROWV += ["l2_b2", "l3_b2"] + [f"gate{i}" for i in range(5)]
ROW = {n: i for i, n in enumerate(ROWV)}

SC = dict(q=0, kv=1, l2a=2, l2m=3, l3a=4, l3c=5, l3m=6)
SH = {k: v + 7 for k, v in SC.items()}
GATE = dict(l2a=0, l2m=1, l3a=2, l3c=3, l3m=4)

LN_L0, LN_Q, LN_KV, LN_2A, LN_2C, LN_2M, LN_3A, LN_3C, LN_3M = range(9)
EPS = [1e-5, 1e-5, 1e-5, 1e-6, 1e-6, 1e-6, 1e-6, 1e-6, 1e-6]
UPDATES_BEFORE = [0, 1, 0, 2, 3, 4, 5, 6, 7]

A_L1, A_2S, A_2C, A_3W, A_3C = range(5)
NORMS_FOR = [LN_KV, LN_2A, LN_2C, LN_3A, LN_3C]


def sequence_steps():
    def norm(*ns):
        return [("stats", n) for n in ns] + [("apply", n) for n in ns] + [("turn", n) for n in ns]

    def attention(a):
        steps = [("qkv", a), ("stack_write", a), ("stack_read", a)]
        if a == A_3C:
            steps.append(("load_next",))
            for j in range(HP + TURN_LAG + 1):
                if j < HP:
                    steps += [("top", j), ("rest", j)]
                if TURN_LAG <= j < HP + TURN_LAG:
                    steps.append(("topT", j - TURN_LAG))
                if j >= TURN_LAG + 1:
                    steps.append(("values", a, j - TURN_LAG - 1))
        elif a == A_3W:
            for u in range(2):
                steps += [("windows", u), ("maxT", a, u), ("max_rows", a, u)]
            steps += [("windows_T", u) for u in range(2)]
            steps += [("window_values", half) for half in range(2)]
        else:
            for j in range(HP):
                steps.append(("scores", a, j))
                if j == HP // 2 + 1:
                    steps += [("maxT", a, 0), ("max_rows", a, 0)]
            steps += [("maxT", a, 1), ("max_rows", a, 1)]
            for j in range(HP + 1):
                if j < HP:
                    steps.append(("scores_T", a, j))
                if j >= 1:
                    steps.append(("values", a, j - 1))
        return steps + [("out_natural", a), ("out_turn", a), ("project", a)]

    steps = [("cond",)] + norm(LN_L0)
    steps += [("l0_qkv",), ("l0_scores",), ("l0_normalise",), ("l0_probs_turn",), ("l0_evidence",), ("l0_router",), ("l0_router_norm",),
              ("l0_hidden", 0), ("l0_hidden", 1), ("l0_experts",), ("l0_routed_turn",), ("l0_out",)]
    steps += norm(LN_Q, LN_KV) + attention(A_L1)
    steps += norm(LN_2A) + attention(A_2S)
    steps += norm(LN_2C) + attention(A_2C)
    steps += norm(LN_2M) + [("gelu",), ("mlp2",)]
    steps += norm(LN_3A) + attention(A_3W)
    steps += norm(LN_3C) + attention(A_3C)
    steps += norm(LN_3M) + [("swiglu",), ("swiglu_up",), ("mlp3",), ("store",), ("load_next_mods",)]
    return steps


TURNS = (
    "0101010101010101010101010101001100101000001110110010010000011111111110010101010101010011001100110011"
    "0001110101010101010101010001010101011100110101001111001100110011001100001100110101010101010101010101"
    "0110001010100110101000010011111100110011001100100111010101010100110101010011010101010101010101010101"
    "0101101101010110010101001010101110001110001011100010100001111110001111010001101110100010010101001011"
    "00101010"
)


def schedule():
    steps, at, order = sequence_steps(), [0] * SLOTS, []
    for turn in TURNS:
        s = int(turn)
        order.append((s, *steps[at[s]]))
        at[s] += 1
    assert at == [len(steps)] * SLOTS
    return order


def psum_plan(order):
    big, small = [], []
    for s, kind, *args in order:
        key = (s, kind, *args)
        if kind in ("l0_hidden", "l0_experts", "scores", "scores_T", "windows", "windows_T", "top", "topT", "out_natural",
                    "gelu", "swiglu", "swiglu_up"):
            big.append(key)
        elif kind in ("turn", "l0_scores", "l0_probs_turn", "l0_evidence", "l0_router", "l0_routed_turn", "maxT",
                      "out_turn", "project", "mlp2", "mlp3"):
            small.append(key)
        elif kind in ("l0_qkv", "qkv"):
            small.extend([key, (s, "v", *args)])
        elif kind == "l0_out":
            small.extend([(s, "l0_gate"), key])
    return big, small


NBIG, NSMALL = 2, 2


class Ring:

    def __init__(self, keys, size):
        self.size = size
        self.use = {k: n for n, k in enumerate(keys)}
        assert len(self.use) == len(keys)
        self.per_round = [len(range(e, len(keys), size)) for e in range(size)]

    def at(self, key):
        n = self.use[key]
        return n % self.size, n // self.size


def chain_kernel(nc: bass.Bass, ins, out):
    order = schedule()
    big_keys, small_keys = psum_plan(order)
    top_order = [(s, *a) for s, kind, *a in order if kind == "top"]
    top_unit = {key: n for n, key in enumerate(top_order)}
    big_ring, small_ring = Ring(big_keys, NBIG), Ring(small_keys, NSMALL)

    with ExitStack() as ctx:
        def sb(name, shape, dt=F32):
            return ctx.enter_context(nc.sbuf_tensor(name, shape, dt))

        def sem(name):
            return ctx.enter_context(nc.semaphore(name))

        def per_slot_sb(name, shape, dt=F32):
            return [sb(f"{name}{s}", shape, dt) for s in range(SLOTS)]

        W = sb("weights", [128, MAT_COLS])
        cols = sb("cols", [128, len(COLS)])
        ident = sb("ident", [128, 128])
        rows3 = sb("rows3", [3, len(ROWV), C], BF16)
        ones3 = sb("ones3", [3, 128], BF16)
        twos3 = sb("twos3", [3, 128], BF16)
        rowf = sb("row_vectors", [len(ROWV), C])
        row_parts = sb("row_parts", [len(ROWV), PARTS, C], BF16)
        minus_half = sb("minus_half", [128, NT])
        second_part = sb("second_part", [2 * HP, 1])
        half_b = sb("half_b", [128, 4])

        cond_all = sb("cond_all", [128, B])
        tanh_all = sb("tanh_all", [128, B])
        silu_all = sb("silu_all", [128, B])
        mods_all = sb("mods_all", [128, B, MODS])
        gates_all = sb("gates_all", [B, 5, C])

        xin = per_slot_sb("xin", [128, NT, C])
        x = per_slot_sb("x", [128, NT, C])
        xout = per_slot_sb("xout", [128, NT, C])
        cx = per_slot_sb("cx", [128, NT, C])
        cT = per_slot_sb("cT", [128, T])
        cond = per_slot_sb("cond", [128, 1])
        condB = per_slot_sb("condB", [128, 128])
        mod = per_slot_sb("mod", [128, MODS])
        gates = per_slot_sb("gates", [128, 5, C])
        stats = per_slot_sb("stats", [128, 2, NT, 6])
        mv = per_slot_sb("mv", [128, 2, NT, 2])
        ve = per_slot_sb("ve", [128, 2, NT])
        rstd = per_slot_sb("rstd", [128, 2, NT])
        xn = per_slot_sb("xn", [128, 2, NT, C])
        hT = per_slot_sb("hT", [128, T])
        kvT = per_slot_sb("kvT", [128, T])
        parts = per_slot_sb("parts", [128, PARTS, 2, T], BF16)
        resid = per_slot_sb("resid", [128, 2, T])
        QK = per_slot_sb("QK", [128, HP, 2, T], BF16)
        Qs, Ks = [[QK[s][:, :, i, :] for s in range(SLOTS)] for i in range(2)]
        V = per_slot_sb("V", [128, NT * H, VW])
        rowmax = per_slot_sb("rowmax", [128, NT, 2, 2, 2, HP // 2])
        negmax = [per_slot_sb(f"negmax{half}_", [2 * HP, T], BF16) for half in range(2)]
        PT = per_slot_sb("PT", [128, 2 * PT_UNITS + 2, NT, T])
        rden = per_slot_sb("rden", [128, NT * H])
        oT = per_slot_sb("oT", [128, T])
        upd = per_slot_sb("upd", [128, NT, C])
        m0 = per_slot_sb("m0", [128, NT])
        nm0 = per_slot_sb("nm0", [128, NT])
        z0 = per_slot_sb("z0", [128, NT])
        rl = per_slot_sb("rl", [128, NT, E3])
        rm = per_slot_sb("rm", [128, NT])
        qk0 = resid
        on = [resid[s][:, 0, :].rearrange("p (t c) -> p t c", t=NT) for s in range(SLOTS)]
        hid = [PT[s][:, 0:4, :, :].rearrange("p a b t -> p (a b) t") for s in range(SLOTS)]
        th = [PT[s][:, 4:8, :, :].rearrange("p a b t -> p (a b) t") for s in range(SLOTS)]
        OT = [PT[s][:, 8:10].rearrange("p a b t -> p (a b) t") for s in range(SLOTS)]
        p0 = [PT[s][:, 8, :, :] for s in range(SLOTS)]
        p0T = [PT[s][:, 9, :, :] for s in range(SLOTS)]

        s1 = sb("s1", [128, 2, 4, T])
        m8 = sb("m8", [128, 2, 2, 4, 8])
        ntop = sb("ntop", [128, 2, 4])
        e_all = sb("e_all", [128, 2, 4, T])
        e_rest = sb("e_rest", [128, 2, 4, T])
        ptop = sb("ptop", [128, CHOSEN_BUFS, 4, T])

        BIG = [ctx.enter_context(nc.psum_tensor(f"big{e}", [128, 2, 512], F32)) for e in range(NBIG)]
        SMALL = [ctx.enter_context(nc.psum_tensor(f"small{e}", [128, 512], F32)) for e in range(NSMALL)]
        OUT = [ctx.enter_context(nc.psum_tensor(f"out{s}", [128, 512], F32)) for s in range(SLOTS)]
        scratch = [nc.dram_tensor(f"parts_scratch{s}", (BLOCKS, 128, 2, T), BF16, kind="Internal").ap()
                   for s in range(SLOTS)]

        mods_scratch = nc.dram_tensor("mods_scratch", (B + SLOTS, 128, MODS), F32, kind="Internal").ap()
        gates_scratch = nc.dram_tensor("gates_scratch", (B + SLOTS, 5 * C), F32, kind="Internal").ap()

        big_full = [sem(f"big_full{e}") for e in range(NBIG)]
        big_free = [sem(f"big_free{e}") for e in range(NBIG)]
        small_full = [sem(f"small_full{e}") for e in range(NSMALL)]
        small_free = [sem(f"small_free{e}") for e in range(NSMALL)]
        cols_loaded, ident_loaded, rows_loaded = sem("cols_loaded"), sem("ident_loaded"), sem("rows_loaded")
        mask_loaded = sem("mask_loaded")
        group_loaded = {g: sem(f"{g}_loaded") for g in MATS}
        conds_loaded = sem("conds_loaded")
        tanh_all_done = sem("tanh_all_done")
        silu_all_step = sem("silu_all_step")
        mods_made = sem("mods_made")
        mods_step = sem("mods_step")
        mods_written = sem("mods_written")
        const_set = sem("const_set")
        pool_const = sem("pool_const")
        passed = {e: sem(f"passed_{e}") for e in ("sp", "pe", "dve", "pool")}
        split_step = sem("split_step")
        rows_spread = sem("rows_spread")

        PER_SEQ = dict(
            loaded=64, mods_loaded=32, stored=16, cond_spread=1,
            bn_done=9, mv_done=9, ve_done=9, rstd_done=9, xn_done=9,
            softmax0_step=4, router_step=4, router_exp=1, tanh0_done=2, silu0_step=2, routed_step=2,
            x_updated=8, out_full=10, out_free=10,
            part1_done=5, part2_done=5, parts_done=5, scratch_written=5 * 80, stacked=5 * 32,
            negmax_step=16, maxrows0_loaded=4 * 32, maxrows1_loaded=4 * 32, rden_done=5, tanh3_done=1, swiglu_step=1,
        )
        S = {n: [sem(f"{n}{s}") for s in range(SLOTS)] for n in PER_SEQ}
        top_step = sem("top_step")
        e_done = sem("e_done")
        p_done = sem("p_done")

        CONSTS = 3
        MODS_STEPS = 5
        POOL_CONSTS = 1 + 4 * SLOTS

        block = ctx.enter_context(nc.Block())

        def w(name, lo=0, n=None):
            at, width = MAT_AT[name]
            return W[:, at + lo:at + (width if n is None else lo + n)]

        def col(name, n=1):
            return cols[:, COL[name]:COL[name] + n]

        def row(name):
            return rows3[:, ROW[name]:ROW[name] + 1, :].to_broadcast([3, NT, C])

        def of(name, s, it, k):
            assert 0 < k <= PER_SEQ[name], (name, k)
            return S[name][s], it * PER_SEQ[name] + k

        def big_filled(it, key):
            e, k = big_ring.at(key)
            return big_full[e], it * big_ring.per_round[e] + k + 1

        def big_is_free(it, key):
            e, k = big_ring.at(key)
            return big_free[e], it * big_ring.per_round[e] + k + 1

        def small_filled(it, key):
            e, k = small_ring.at(key)
            return small_full[e], it * small_ring.per_round[e] + k + 1

        def small_is_free(it, key):
            e, k = small_ring.at(key)
            return small_free[e], it * small_ring.per_round[e] + k + 1

        def big_taken(it, key):
            f, v = big_is_free(it, key)
            return f, v + 1

        def small_taken(it, key):
            f, v = small_is_free(it, key)
            return f, v + 1

        def tiles(it, free=(), taken=()):
            need = {}
            for keys, extra in ((free, 1), (taken, 2)):
                for key in keys:
                    ring, sems, ready = (small_ring, small_free, "s") if key in small_ring.use else (big_ring, big_free, "b")
                    e, k = ring.at(key)
                    need[ready, e] = max(need.get((ready, e), (0,))[0], k + extra), sems[e], ring.per_round[e]
            return [(f, it * n + k) for k, f, n in need.values()]

        def big(key):
            return BIG[big_ring.at(key)[0]]

        def small(key):
            return SMALL[small_ring.at(key)[0]]

        def big_freed(key):
            return big_free[big_ring.at(key)[0]]

        def small_freed(key):
            return small_free[small_ring.at(key)[0]]

        def big_ready(key):
            return big_full[big_ring.at(key)[0]]

        def small_ready(key):
            return small_full[small_ring.at(key)[0]]

        def nat(ap):
            return ap[:, 0:T].rearrange("p (t c) -> p t c", t=NT)

        def follow(it, steps):
            for s, kind, *args in order:
                if kind in steps:
                    steps[kind](s, it, *args)

        @block.sync
        def _(sp):
            def load_mods(s, b):
                sp.dma_start(mod[s][:, :], mods_scratch[bass.ds(b, 1)].rearrange("b p m -> p (b m)")).then_inc(S["mods_loaded"][s], 16)
                sp.dma_start(gates[s][:, :, :].rearrange("p g c -> p (g c)"), gates_scratch[bass.ds(b, 1)].to_broadcast([128, 5 * C]))\
                    .then_inc(S["mods_loaded"][s], 16)

            def load_inputs(s, b):
                sp.dma_start(xin[s][:, :, :], ins["x"][bass.ds(b, 1)].rearrange("b (t p) c -> p (b t) c", p=128)).then_inc(S["loaded"][s], 16)
                sp.dma_start(cond[s][:, :], ins["condT"][bass.ds(b, 1)].rearrange("b p o -> p (b o)")).then_inc(S["loaded"][s], 16)
                sp.dma_start(cT[s][:, :], ins["ctxT"][bass.ds(b, 1)].rearrange("b p t -> p (b t)")).then_inc(S["loaded"][s], 16)
                sp.dma_start(cx[s][:, :, :], ins["ctx"][bass.ds(b, 1)].rearrange("b (t p) c -> p (b t) c", p=128)).then_inc(S["loaded"][s], 16)

            def stack_write(s, it, a):
                wr = S["scratch_written"][s]
                both_scr = scratch[s][0:2].rearrange("r c i t -> c r (i t)")
                rest = scratch[s][2:BLOCKS].rearrange("(u v) c i t -> i v c u t", v=2)
                sp.wait_ge(*of("part1_done", s, it, a + 1))
                for i in range(2):
                    sp.dma_start(rest[i, i], parts[s][:, 0:1, i, :].to_broadcast([128, 2, T])).then_inc(wr, 16)
                sp.wait_ge(*of("parts_done", s, it, a + 1))
                sp.dma_start(both_scr, parts[s][:, 0:2, :, :].rearrange("c r i t -> c r (i t)")).then_inc(wr, 16)
                for i in range(2):
                    sp.dma_start(rest[i, 1 - i], parts[s][:, 1:3, i, :]).then_inc(wr, 16)

            def stack_read(s, it, a):
                sp.wait_ge(*of("scratch_written", s, it, 80 * (a + 1)))
                for p in range(2):
                    src = scratch[s].rearrange("r (d p h) i t -> p (r d) (h i t)", p=2, d=D)[p]
                    sp.dma_start(QK[s][64 * p:64 * p + ROWS].rearrange("r h i t -> r (h i t)"), src).then_inc(S["stacked"][s], 16)

            def max_rows(s, it, a, half):
                sp.wait_ge(*small_taken(it, (s, "maxT", a, half)))
                n = HP // 2
                for p in range(2):
                    r = 64 * p + ROWS
                    sp.dma_start(QK[s][r:r + 2, n * half:n * half + n, 0, :], negmax[half][s][HP * p:HP * p + HP, :])\
                        .then_inc(S[f"maxrows{half}_loaded"][s], 16)

            def store(s, it):
                sp.wait_ge(*of("x_updated", s, it, 8))
                sp.sem_inc(passed["sp"], 1)
                sp.dma_start(out[bass.ds(it * SLOTS + s, 1)].rearrange("b (t p) c -> p (b t) c", p=128), xout[s][:, :, :]).then_inc(S["stored"][s], 16)

            def load_next(s, it):
                sp.wait_ge(*small_taken(it, (s, "v", A_3C)))
                sp.sem_inc(passed["sp"], 1)
                load_inputs(s, it * SLOTS + (SLOTS + s))

            def load_next_mods(s, it):
                sp.wait_ge(*of("stored", s, it, 16))
                sp.sem_inc(passed["sp"], 1)
                load_mods(s, it * SLOTS + (SLOTS + s))

            sp.dma_start(cond_all[:, :], ins["cond_all"]).then_inc(conds_loaded, 16)
            sp.dma_start(rowf[:, :], ins["rows"]).then_inc(rows_loaded, 16)
            sp.dma_start(cols[:, :], ins["cols"]).then_inc(cols_loaded, 16)
            sp.dma_start(ident[:, :], ins["ident"]).then_inc(ident_loaded, 16)
            sp.dma_start(second_part[:, :], ins["second_part"]).then_inc(mask_loaded, 16)
            for s in range(SLOTS):
                load_inputs(s, s)
            sp.wait_ge(split_step, 5)
            for i in range(PARTS):
                sp.dma_start(rows3[i:i + 1, :, :], row_parts[:, i, :]).then_inc(rows_spread, 16)
            sp.wait_ge(pool_const, POOL_CONSTS)
            sp.wait_ge(mods_step, MODS_STEPS)
            for lo, n in ((0, B), (B, SLOTS)):
                sp.dma_start(mods_scratch[lo:lo + n].rearrange("b p m -> p b m"), mods_all[:, 0:n, :]).then_inc(mods_written, 16)
                sp.dma_start(gates_scratch[lo:lo + n], gates_all[0:n].rearrange("b g c -> b (g c)")).then_inc(mods_written, 16)
            sp.wait_ge(mods_written, 64)
            for s in range(SLOTS):
                load_mods(s, s)
            with sp.Fori(0, B // SLOTS) as it:
                follow(it, dict(stack_write=stack_write, stack_read=stack_read, max_rows=max_rows, store=store, load_next=load_next, load_next_mods=load_next_mods))
            for s in range(SLOTS):
                sp.wait_ge(S["loaded"][s], 64 * (B // SLOTS + 1))
                sp.wait_ge(S["mods_loaded"][s], 32 * (B // SLOTS + 1))

        @block.tensor
        def _(pe):
            def turn(key, src, it):
                pe.wait_ge(*small_is_free(it, key))
                for t in range(NT):
                    mm = pe.transpose(small(key)[:, t * 128:(t + 1) * 128], src(t), ident[:, :])
                mm.then_inc(small_ready(key), 1)

            def bias_rows(dst, name, ones, start=True):
                return pe.matmul(dst, ones[:, :], row(name), start=start, stop=False, skip_group_check=True)

            def natural(key, it, terms, name, ones=None, taken=()):
                for t in tiles(it, free=[key], taken=taken):
                    pe.wait_ge(*t)
                dst = small(key)
                bias_rows(nat(dst), name, ones3 if ones is None else ones)
                for t in range(NT):
                    for i, (a, m) in enumerate(terms):
                        mm = pe.matmul(dst[:, t * 128:(t + 1) * 128], a[:, t * 128:(t + 1) * 128], m, start=False,
                                       stop=(i == len(terms) - 1), skip_group_check=True)
                mm.then_inc(small_ready(key), 1)

            def condition_products():
                pe.wait_ge(silu_all_step, 2)
                for i in range(14):
                    pe.matmul(OUT[0][:, i * B:(i + 1) * B], w("mod", i * C, C), silu_all[:, :], start=True, stop=True)
                for i in range(7):
                    m = w(f"l0_w1_{i // 2}_2", (i % 2) * C, C) if i < 6 else w("l0_g1_2")
                    pe.matmul(OUT[0][:, (14 + i) * B:(15 + i) * B], m, cond_all[:, :], start=True, stop=True)
                pe.wait_ge(rows_spread, 16 * PARTS)
                for dst, lo, n in ((OUT[0][0:B, 256:512], 0, 2), (OUT[1][0:B, 0:3 * C], 2, 3)):
                    pe.matmul(dst, ones3[:, 0:B], rows3[:, ROW["gate0"] + lo:ROW["gate0"] + lo + n, :], start=True, stop=False, skip_group_check=True)
                    mm = pe.matmul(dst, silu_all[:, :], w("gate", lo * C, n * C), start=False, stop=True, skip_group_check=True)
                mm.then_inc(mods_made, 1)

            def norm_turn(s, it, n):
                pe.wait_ge(*of("xn_done", s, it, n + 1))
                turn((s, "turn", n), lambda t: xn[s][:, n % 2, t, :], it)

            def l0_qkv(s, it):
                pe.wait_ge(group_loaded["early"], 16)
                key = (s, "l0_qkv")
                for t in tiles(it, free=[key], taken=[(s, "turn", LN_L0)]):
                    pe.wait_ge(*t)
                pe.matmul(small(key)[:, 0:T], w("l0_q"), hT[s][:, :], start=True, stop=True)
                pe.matmul(small(key)[:, T:2 * T], w("l0_k"), cT[s][:, :], start=True, stop=True).then_inc(small_ready(key), 1)
                key = (s, "v")
                pe.wait_ge(*small_is_free(it, key))
                for t in range(NT):
                    mm = pe.matmul(small(key)[:, t * C:(t + 1) * C], cT[s][:, t * 128:(t + 1) * 128], w("l0_v"), start=True, stop=True)
                mm.then_inc(small_ready(key), 1)

            def l0_scores(s, it):
                key = (s, "l0_scores")
                for t in tiles(it, free=[key], taken=[(s, "l0_qkv")]):
                    pe.wait_ge(*t)
                for t in range(NT):
                    mm = pe.matmul(small(key)[:, t * T:(t + 1) * T], qk0[s][:, 0, t * 128:(t + 1) * 128], qk0[s][:, 1, :], start=True, stop=True)
                mm.then_inc(small_ready(key), 1)

            def l0_probs_turn(s, it):
                key = (s, "l0_probs_turn")
                pe.wait_ge(*of("softmax0_step", s, it, 4))
                pe.wait_ge(*small_is_free(it, key))
                for k in range(NT):
                    for t in range(NT):
                        mm = pe.transpose(small(key)[:, k * T + t * 128:k * T + (t + 1) * 128], p0[s][:, t, k * 128:(k + 1) * 128], ident[:, :])
                mm.then_inc(small_ready(key), 1)

            def l0_evidence(s, it):
                key = (s, "l0_evidence")
                for t in tiles(it, free=[key], taken=[(s, "v"), (s, "l0_probs_turn")]):
                    pe.wait_ge(*t)
                for k in range(NT):
                    mm = pe.matmul(small(key)[:, 0:T], upd[s][:, k, :], p0T[s][:, k, :], start=(k == 0), stop=(k == NT - 1))
                mm.then_inc(small_ready(key), 1)

            def l0_router(s, it):
                pe.wait_ge(group_loaded["l0"], 16)
                key = (s, "l0_router")
                for t in tiles(it, free=[key], taken=[(s, "l0_evidence")]):
                    pe.wait_ge(*t)
                rw = w("l0_router")
                for t in range(NT):
                    dst = small(key)[:, 4 * t:4 * t + E3]
                    tt = slice(t * 128, (t + 1) * 128)
                    pe.matmul(dst, ones3[:, :], rows3[:, ROW["router"], 0:E3], start=True, stop=False, skip_group_check=True)
                    pe.matmul(dst, hT[s][:, tt], rw[:, 0:E3], start=False, stop=False, skip_group_check=True)
                    pe.matmul(dst, kvT[s][:, tt], rw[:, E3:2 * E3], start=False, stop=False, skip_group_check=True)
                    mm = pe.matmul(dst, condB[s][:, :], rw[:, 2 * E3:3 * E3], start=False, stop=True, skip_group_check=True)
                mm.then_inc(small_ready(key), 1)

            def l0_hidden(s, it, half):
                key = (s, "l0_hidden", half)
                pe.wait_ge(*big_is_free(it, key))
                for i in range(4 * half, min(4 * half + 4, 7)):
                    n = i - 4 * half
                    dst = big(key)[:, n // 2, (n % 2) * T:(n % 2 + 1) * T]
                    for j, act in enumerate((hT[s], kvT[s])):
                        m = w(f"l0_w1_{i // 2}_{j}", (i % 2) * C, C) if i < 6 else w(f"l0_g1_{j}")
                        mm = pe.matmul(dst, m, act[:, :], start=(j == 0), stop=(j == 1))
                mm.then_inc(big_ready(key), 1)

            def l0_experts(s, it):
                key = (s, "l0_experts")
                for t in tiles(it, free=[key], taken=[(s, "l0_hidden", 1)]):
                    pe.wait_ge(*t)
                for t in range(NT):
                    pe.matmul(big(key)[:, t, 0:E3 * C], twos3[:, :], rows3[:, ROW["e0"]:ROW["e0"] + E3, :], start=True, stop=False, skip_group_check=True)
                    for e in range(E3):
                        for c in range(2):
                            mm = pe.matmul(big(key)[:, t, e * C:(e + 1) * C], hid[s][:, 2 * e + c, t * 128:(t + 1) * 128], w(f"l0_w2_{e}_{c}"),
                                           start=False, stop=(c == 1), skip_group_check=True)
                mm.then_inc(big_ready(key), 1)

            def l0_routed_turn(s, it):
                pe.wait_ge(*big_taken(it, (s, "l0_experts")))
                turn((s, "l0_routed_turn"), lambda t: upd[s][:, t, :], it)

            def l0_out(s, it):
                natural((s, "l0_gate"), it, [(hid[s][:, 6, :], w("l0_g2"))], "g2", twos3)
                natural((s, "l0_out"), it, [(oT[s], w("l0_out"))], "out", taken=[(s, "l0_routed_turn")])

            def qkv(s, it, a):
                pe.wait_ge(group_loaded["l1" if a == A_L1 else "l2" if a in (A_2S, A_2C) else "l3"], 16)
                kv = {A_L1: kvT, A_2S: hT, A_2C: cT, A_3W: hT, A_3C: cT}[a][s]
                key = (s, "qkv", a)
                norms = [(s, "turn", NORMS_FOR[a])] + [(s, "turn", LN_Q)] * (a == A_L1)
                for t in tiles(it, free=[key], taken=norms):
                    pe.wait_ge(*t)
                pe.matmul(small(key)[:, 0:T], w(f"q{a}"), hT[s][:, :], start=True, stop=True)
                pe.matmul(small(key)[:, T:2 * T], w(f"k{a}"), kv[:, :], start=True, stop=True).then_inc(small_ready(key), 1)
                natural((s, "v", a), it, [(kv, w(f"v{a}"))], f"bv{a}")

            def scores(s, it, a, j):
                key = (s, "scores", a, j)
                if j == 0:
                    pe.wait_ge(*of("stacked", s, it, 32 * (a + 1)))
                pe.wait_ge(*big_is_free(it, key))
                for t in range(NT):
                    for p in range(2):
                        r = slice(64 * p, 64 * p + ROWS)
                        mm = pe.matmul(big(key)[:, p, t * T:(t + 1) * T], Qs[s][r, j, t * 128:(t + 1) * 128], Ks[s][r, j, :], start=True, stop=True)
                mm.then_inc(big_ready(key), 1)

            def scores_T(s, it, a, j):
                key = (s, "scores_T", a, j)
                if j in (0, HP // 2):
                    pe.wait_ge(*of(f"maxrows{2 * j // HP}_loaded", s, it, 32 * (a + 1)))
                pe.wait_ge(*big_is_free(it, key))
                for k in range(NT):
                    for p in range(2):
                        r = slice(64 * p, 64 * p + ROWSM)
                        mm = pe.matmul(big(key)[:, p, k * T:(k + 1) * T], Ks[s][r, j, k * 128:(k + 1) * 128], Qs[s][r, j, :], start=True, stop=True)
                mm.then_inc(big_ready(key), 1)

            def window_scores(s, it, key, turned):
                u = key[2]
                if turned:
                    pe.wait_ge(*of(f"maxrows{u}_loaded", s, it, 32 * (A_3W + 1)))
                elif u == 0:
                    pe.wait_ge(*of("stacked", s, it, 32 * (A_3W + 1)))
                pe.wait_ge(*big_is_free(it, key))
                pe.sem_inc(passed["pe"], 1)
                for i in range(4):
                    for wdw in range(T // WIN):
                        for p in range(2):
                            r = slice(64 * p, 64 * p + (ROWSM if turned else ROWS))
                            q = Qs[s][r, 4 * u + i, wdw * WIN:(wdw + 1) * WIN]
                            k = Ks[s][r, 4 * u + i, wdw * WIN:(wdw + 1) * WIN]
                            c0 = ((wdw // 2) * 4 + i) * WIN
                            dst = big(key)[64 * (wdw % 2):64 * (wdw % 2) + 64, p, c0:c0 + WIN]
                            mm = pe.matmul(dst, k if turned else q, q if turned else k, start=True, stop=True)
                mm.then_inc(big_ready(key), 1)

            def windows(s, it, u):
                window_scores(s, it, (s, "windows", u), False)

            def windows_T(s, it, u):
                window_scores(s, it, (s, "windows_T", u), True)

            def max_turn(s, it, a, half):
                key = (s, "maxT", a, half)
                pe.wait_ge(*of("negmax_step", s, it, 4 * a + 2 * half + 1))
                pe.wait_ge(*small_is_free(it, key))
                for t in range(NT):
                    mm = pe.transpose(small(key)[0:2 * HP, t * 128:(t + 1) * 128],
                                      rowmax[s][:, t, half].rearrange("q p a h -> q (p a h)"), ident[:, :])
                mm.then_inc(small_ready(key), 1)

            def values(s, it, a, j):
                probs = (s, "topT", j) if a == A_3C else (s, "scores_T", a, j)
                for t in tiles(it, taken=[probs] + [(s, "v", a)] * (j == 0)):
                    pe.wait_ge(*t)
                if j == HP // 2:
                    pe.wait_ge(*of("out_free", s, it, 2 * a + 1))
                lo = (j // 2) % 2 * T
                for k in range(NT):
                    for p in range(2):
                        h = 2 * j + p
                        q4 = VW * (h % 4)
                        mm = pe.matmul(OUT[s][q4:q4 + VW, lo:lo + T], V[s][:, k * H + h, :], PT[s][:, h % (2 * PT_UNITS), k, :],
                                       start=(k == 0), stop=(k == NT - 1), skip_group_check=True)
                if j in (HP // 2 - 1, HP - 1):
                    mm.then_inc(S["out_full"][s], 1)

            def window_values(s, it, half):
                if half == 0:
                    for t in tiles(it, taken=[(s, "windows_T", 0), (s, "windows_T", 1), (s, "v", A_3W)]):
                        pe.wait_ge(*t)
                else:
                    pe.wait_ge(*of("out_free", s, it, 2 * A_3W + 1))
                pe.sem_inc(passed["pe"], 1)
                r = slice(64 * half, 64 * half + 64)
                for h in range(H):
                    i, p = h // 2, h % 2
                    probs = PT[s][r, (i // 4) * 2 + p].rearrange("p k t -> p (k t)")
                    q4 = VW * (h % 4)
                    for t in range(NT):
                        lo, b0 = (h // 4) * 128 + t * WIN, (t * 4 + i % 4) * WIN
                        mm = pe.matmul(OUT[s][q4:q4 + VW, lo:lo + WIN], V[s][r, t * H + h, :], probs[:, b0:b0 + WIN], start=True, stop=True)
                mm.then_inc(S["out_full"][s], 1)

            def top(s, it, j):
                key = (s, "top", j)
                if j == 0:
                    pe.wait_ge(*of("stacked", s, it, 32 * (A_3C + 1)))
                pe.wait_ge(*big_is_free(it, key))
                for t in range(NT):
                    for p in range(2):
                        r = slice(64 * p, 64 * p + ROWS)
                        mm = pe.matmul(big(key)[:, p, t * T:(t + 1) * T], Qs[s][r, j, t * 128:(t + 1) * 128], Ks[s][r, j, :], start=True, stop=True)
                mm.then_inc(big_ready(key), 1)

            def top_turn(s, it, j):
                key, g = (s, "topT", j), top_unit[s, j]
                pe.wait_ge(p_done, it * (SLOTS * HP) + g + 1)
                pe.wait_ge(*big_is_free(it, key))
                for p in range(2):
                    for k in range(NT):
                        for t in range(NT):
                            c0 = k * T + t * 128
                            mm = pe.transpose(big(key)[:, p, c0:c0 + 128], ptop[:, g % CHOSEN_BUFS, 2 * p + t, k * 128:(k + 1) * 128], ident[:, :])
                mm.then_inc(big_ready(key), 1)

            def out_natural(s, it, a):
                key = (s, "out_natural", a)
                pe.wait_ge(*of("out_free", s, it, 2 * a + 2))
                pe.wait_ge(*big_is_free(it, key))
                for g in range(H // 4):
                    for t in range(NT):
                        mm = pe.transpose(big(key)[:, t, g * 128:(g + 1) * 128], OT[s][:, g, t * 128:(t + 1) * 128], ident[:, :])
                mm.then_inc(big_ready(key), 1)

            def out_turn(s, it, a):
                pe.wait_ge(*big_taken(it, (s, "out_natural", a)))
                turn((s, "out_turn", a), lambda t: on[s][:, t, :], it)

            def project(s, it, a):
                natural((s, "project", a), it, [(oT[s], w(f"o{a}"))], f"bo{a}", taken=[(s, "out_turn", a)])

            def hidden(s, it, key, n, mat, lo):
                pe.wait_ge(*small_taken(it, (s, "turn", n)))
                pe.wait_ge(*big_is_free(it, key))
                for i in range(4):
                    mm = pe.matmul(big(key)[:, i // 2, (i % 2) * T:(i % 2 + 1) * T], w(mat, lo + i * C, C), hT[s][:, :], start=True, stop=True)
                mm.then_inc(big_ready(key), 1)

            def gelu_hidden(s, it):
                hidden(s, it, (s, "gelu"), LN_2M, "l2_w1", 0)

            def swiglu_gate(s, it):
                hidden(s, it, (s, "swiglu"), LN_3M, "l3_w1", 0)

            def swiglu_up(s, it):
                hidden(s, it, (s, "swiglu_up"), LN_3M, "l3_w1", HID)

            def mlp_out(s, it, key, done, mat, name, ones):
                pe.wait_ge(*big_taken(it, done))
                natural(key, it, [(hid[s][:, i, :], w(mat, i * C, C)) for i in range(4)], name, ones)

            def mlp2(s, it):
                mlp_out(s, it, (s, "mlp2"), (s, "gelu"), "l2_w2", "l2_b2", ones3)

            def mlp3(s, it):
                mlp_out(s, it, (s, "mlp3"), (s, "swiglu_up"), "l3_w2", "l3_b2", twos3)

            pe.wait_ge(const_set, CONSTS)
            pe.wait_ge(group_loaded["mod"], 16)
            condition_products()
            pe.wait_ge(mods_step, MODS_STEPS)
            pe.wait_ge(ident_loaded, 16)
            pe.wait_ge(pool_const, POOL_CONSTS)
            with pe.Fori(0, B // SLOTS) as it:
                follow(it, dict(
                    turn=norm_turn, l0_qkv=l0_qkv, l0_scores=l0_scores, l0_probs_turn=l0_probs_turn,
                    l0_evidence=l0_evidence, l0_router=l0_router, l0_hidden=l0_hidden, l0_experts=l0_experts,
                    l0_routed_turn=l0_routed_turn, l0_out=l0_out, qkv=qkv, scores=scores, maxT=max_turn, scores_T=scores_T,
                    values=values, windows=windows, windows_T=windows_T, window_values=window_values, top=top, topT=top_turn,
                    out_natural=out_natural, out_turn=out_turn, project=project, gelu=gelu_hidden, mlp2=mlp2,
                    swiglu=swiglu_gate, swiglu_up=swiglu_up, mlp3=mlp3))

        @block.scalar
        def _(act):
            def take(s, it, key, dst, src):
                act.wait_ge(*small_filled(it, key))
                nc.scalar.copy(dst, src).then_inc(small_freed(key), 1)

            def norm_out(s, it, n):
                key = (s, "turn", n)
                if n == LN_L0:
                    sc, sh = col("ln_g"), col("ln_b")
                elif n == LN_2C:
                    sc, sh = col("n2_g"), col("n2_b")
                else:
                    m = {LN_Q: "q", LN_KV: "kv", LN_2A: "l2a", LN_2M: "l2m", LN_3A: "l3a", LN_3C: "l3c", LN_3M: "l3m"}[n]
                    sc, sh = mod[s][:, SC[m]:SC[m] + 1], mod[s][:, SH[m]:SH[m] + 1]
                act.wait_ge(*small_filled(it, key))
                dst, src = (kvT if n == LN_KV else hT)[s], small(key)
                if n == LN_3A:
                    nc.scalar.activation(dst[:, 0:T - SHIFT], src[:, SHIFT:T], ACT.Identity, scale=sc, bias=sh)
                    nc.scalar.activation(dst[:, T - SHIFT:T], src[:, 0:SHIFT], ACT.Identity, scale=sc, bias=sh).then_inc(small_freed(key), 1)
                else:
                    nc.scalar.activation(dst[:, :], src[:, 0:T], ACT.Identity, scale=sc, bias=sh).then_inc(small_freed(key), 1)

            def l0_exp(s, it):
                key = (s, "l0_scores")
                act.wait_ge(*of("softmax0_step", s, it, 2))
                for t in range(NT):
                    last = nc.scalar.activation(p0[s][:, t, :], small(key)[:, t * T:(t + 1) * T], ACT.Exp, scale=SCALE0,
                                                bias=nm0[s][:, t:t + 1], accum_out=z0[s][:, t:t + 1])
                last.then_inc(small_freed(key), 1)

            def l0_router_exp(s, it):
                act.wait_ge(*small_taken(it, (s, "l0_router")))
                nc.scalar.activation(rl[s][:, :, :], rl[s][:, :, :], ACT.Exp).then_inc(S["router_exp"][s], 1)

            def l0_tanh(s, it, half):
                key = (s, "l0_hidden", half)
                if half == 0:
                    act.wait_ge(*of("mods_loaded", s, it, 32))
                act.wait_ge(*big_filled(it, key))
                for i in range(4 * half, min(4 * half + 4, 7)):
                    n = i - 4 * half
                    last = nc.scalar.activation(th[s][:, i, :], big(key)[:, n // 2, (n % 2) * T:(n % 2 + 1) * T], ACT.Tanh,
                                                scale=0.5, bias=mod[s][:, 21 + i:22 + i])
                last.then_inc(S["tanh0_done"][s], 1)

            def l0_gate_tanh(s, it):
                key = (s, "l0_gate")
                act.wait_ge(*small_filled(it, key))
                nc.scalar.activation(th[s][:, 7, :], small(key)[:, 0:T], ACT.Tanh, scale=0.25).then_inc(small_freed(key), 1)

            def first_parts(s, it, a):
                key = (s, "qkv", a)
                act.wait_ge(*small_filled(it, key))
                nc.scalar.activation(parts[s][:, 0, 0, :], small(key)[:, 0:T], ACT.Identity, bias=col(f"bq{a}"))
                nc.scalar.activation(parts[s][:, 0, 1, :], small(key)[:, T:2 * T], ACT.Identity, bias=col(f"bk{a}")).then_inc(S["part1_done"][s], 1)
                key = (s, "v", a)
                take(s, it, key, V[s][:, :, 0:D], small(key)[:, 0:T].rearrange("p (h d) -> p h d", d=D))

            def probabilities(s, it, a, j):
                key = (s, "scores_T", a, j)
                c = 2 * (j % PT_UNITS)
                act.wait_ge(*big_filled(it, key))
                nc.scalar.activation(PT[s][:, c:c + 2].rearrange("p a b t -> p a (b t)"), big(key)[:, :, :], ACT.Exp,
                                     scale=SCALE).then_inc(big_freed(key), 1)

            def window_probabilities(s, it, u):
                key = (s, "windows_T", u)
                act.wait_ge(*big_filled(it, key))
                nc.scalar.activation(PT[s][:, 2 * u:2 * u + 2].rearrange("p a b t -> p a (b t)"), big(key)[:, :, :], ACT.Exp,
                                     scale=SCALE).then_inc(big_freed(key), 1)

            def half_out(s, it, a, j):
                if j not in (HP // 2 - 1, HP - 1):
                    return
                half = j // (HP // 2)
                act.wait_ge(*of("out_full", s, it, 2 * a + half + 1))
                nc.scalar.copy(OT[s][:, 2 * half:2 * half + 2, :], OUT[s][:, :].rearrange("p (g t) -> p g t", g=2)).then_inc(S["out_free"][s], 1)

            def window_half_out(s, it, half):
                act.wait_ge(*of("out_full", s, it, 2 * A_3W + half + 1))
                dst = OT[s][:, :, :].rearrange("p g (t w q) -> p (g t) w q", t=NT, w=2)[:, :, half, :]
                nc.scalar.copy(dst, OUT[s][:, :].rearrange("p (g q) -> p g q", q=WIN)).then_inc(S["out_free"][s], 1)

            def output_out(s, it, a):
                key = (s, "out_turn", a)
                if a == A_3W:
                    act.wait_ge(*small_filled(it, key))
                    nc.scalar.copy(oT[s][:, SHIFT:T], small(key)[:, 0:T - SHIFT])
                    nc.scalar.copy(oT[s][:, 0:SHIFT], small(key)[:, T - SHIFT:T]).then_inc(small_freed(key), 1)
                else:
                    take(s, it, key, oT[s][:, :], small(key)[:, 0:T])

            def top_exp(s, it, j):
                key, g = (s, "top", j), top_unit[s, j]
                act.wait_ge(top_step, it * (SLOTS * HP * 8) + 8 * g + 4)
                if g >= 2:
                    act.wait_ge(p_done, it * (SLOTS * HP) + g - 1)
                for i in range(4):
                    last = nc.scalar.activation(e_all[:, g % 2, i, :], big(key)[:, i // 2, (i % 2) * T:(i % 2 + 1) * T], ACT.Exp,
                                                scale=SCALE, bias=ntop[:, g % 2, i:i + 1])
                last.then_inc(big_freed(key), 1)

            def rest_exp(s, it, j):
                g = top_unit[s, j]
                act.wait_ge(top_step, it * (SLOTS * HP * 8) + 8 * g + 8)
                for i in range(4):
                    last = nc.scalar.activation(e_rest[:, g % 2, i, :], s1[:, g % 2, i, :], ACT.Exp,
                                                scale=SCALE, bias=ntop[:, g % 2, i:i + 1])
                last.then_inc(e_done, 1)

            def chosen_out(s, it, j):
                key, c = (s, "topT", j), 2 * (j % PT_UNITS)
                act.wait_ge(*big_filled(it, key))
                nc.scalar.copy(PT[s][:, c:c + 2].rearrange("p a b t -> p a (b t)"), big(key)[:, :, :]).then_inc(big_freed(key), 1)

            def gelu(s, it):
                key = (s, "gelu")
                act.wait_ge(*big_filled(it, key))
                for i in range(4):
                    last = nc.scalar.activation(hid[s][:, i, :], big(key)[:, i // 2, (i % 2) * T:(i % 2 + 1) * T], ACT.Gelu_apprx_tanh,
                                                bias=col(f"l2_b1_{i}"))
                last.then_inc(big_freed(key), 1)

            def swiglu_tanh(s, it):
                key = (s, "swiglu")
                act.wait_ge(*big_filled(it, key))
                for i in range(4):
                    last = nc.scalar.activation(th[s][:, i, :], big(key)[:, i // 2, (i % 2) * T:(i % 2 + 1) * T], ACT.Tanh,
                                                scale=0.5, bias=half_b[:, i:i + 1])
                last.then_inc(S["tanh3_done"][s], 1)

            def l0_values_out(s, it):
                key = (s, "l0_qkv")
                take(s, it, key, qk0[s][:, :, :].rearrange("p a t -> p (a t)"), small(key)[:, :])
                key = (s, "v")
                take(s, it, key, upd[s][:, :, :], nat(small(key)))

            def l0_probs_out(s, it):
                key = (s, "l0_probs_turn")
                take(s, it, key, p0T[s][:, :, :].rearrange("p k t -> p (k t)"), small(key)[:, :])

            def l0_evidence_out(s, it):
                key = (s, "l0_evidence")
                take(s, it, key, kvT[s][:, :], small(key)[:, 0:T])

            def l0_routed_out(s, it):
                key = (s, "l0_routed_turn")
                take(s, it, key, oT[s][:, :], small(key)[:, 0:T])

            def load_matrices(*groups):
                for g in groups:
                    lo = GROUP_AT[g]
                    n = sum(c for _, c in MATS[g])
                    act.dma_start(W[:, lo:lo + n], ins["mats"][:, lo:lo + n]).then_inc(group_loaded[g], 16)

            load_matrices("mod", "early", "l0")
            act.wait_ge(conds_loaded, 16)
            nc.scalar.activation(tanh_all[:, :], cond_all[:, :], ACT.Tanh, scale=0.5).then_inc(tanh_all_done, 1)
            act.wait_ge(group_loaded["early"], 16)
            load_matrices("l1", "l2", "l3")
            act.wait_ge(cols_loaded, 16)
            with act.Fori(0, B // SLOTS) as it:
                follow(it, dict(
                    turn=norm_out, l0_qkv=l0_values_out, l0_scores=l0_exp, l0_probs_turn=l0_probs_out,
                    l0_evidence=l0_evidence_out, l0_router=l0_router_exp, l0_hidden=l0_tanh, l0_routed_turn=l0_routed_out,
                    l0_out=l0_gate_tanh, qkv=first_parts, scores_T=probabilities, windows_T=window_probabilities,
                    values=half_out, window_values=window_half_out, top=top_exp, rest=rest_exp, topT=chosen_out,
                    out_turn=output_out, gelu=gelu, swiglu=swiglu_tanh))

        @block.vector
        def _(dve):
            def cond_spread(s, it):
                dve.wait_ge(*of("loaded", s, it, 64))
                nc.vector.tensor_copy(condB[s][:, :], cond[s][:, 0:1].to_broadcast([128, 128])).then_inc(S["cond_spread"][s], 1)

            def norm_stats(s, it, n):
                src = {LN_L0: xin, LN_KV: cx}.get(n, x)
                if n == LN_L0:
                    dve.wait_ge(*of("loaded", s, it, 64))
                elif n != LN_KV:
                    dve.wait_ge(*of("x_updated", s, it, UPDATES_BEFORE[n]))
                for t in range(NT):
                    last = nc.vector.bn_stats(stats[s][:, n % 2, t, :], src[s][:, t, :])
                last.then_inc(S["bn_done"][s], 1)
                dve.wait_ge(*of("bn_done", s, it, n + 1))
                dve.sem_inc(passed["dve"], 1)
                for t in range(NT):
                    last = nc.vector.bn_aggr(mv[s][:, n % 2, t, :], stats[s][:, n % 2, t, :])
                last.then_inc(S["mv_done"][s], 1)
                dve.wait_ge(*of("mv_done", s, it, n + 1))
                nc.vector.tensor_scalar(ve[s][:, n % 2, :], mv[s][:, n % 2, :, 1], EPS[n], None, ALU.add).then_inc(S["ve_done"][s], 1)

            def norm_apply(s, it, n):
                src = {LN_L0: xin, LN_KV: cx}.get(n, x)
                dve.wait_ge(*of("rstd_done", s, it, n + 1))
                for t in range(NT):
                    last = nc.vector.tensor_scalar(xn[s][:, n % 2, t, :], src[s][:, t, :], mv[s][:, n % 2, t, 0:1],
                                                   rstd[s][:, n % 2, t:t + 1], ALU.subtract, ALU.mult)
                last.then_inc(S["xn_done"][s], 1)

            def l0_max(s, it):
                key = (s, "l0_scores")
                dve.wait_ge(*small_filled(it, key))
                nc.vector.tensor_reduce(m0[s][:, :], small(key)[:, :].rearrange("p (t k) -> p t k", t=NT), AX_X, ALU.max)\
                    .then_inc(S["softmax0_step"][s], 1)
                dve.wait_ge(*of("softmax0_step", s, it, 1))
                nc.vector.tensor_scalar(nm0[s][:, :], m0[s][:, :], -SCALE0, None, ALU.mult).then_inc(S["softmax0_step"][s], 1)

            def l0_normalise(s, it):
                dve.wait_ge(*small_taken(it, (s, "l0_scores")))
                nc.vector.reciprocal(m0[s][:, :], z0[s][:, :]).then_inc(S["softmax0_step"][s], 1)
                dve.wait_ge(*of("softmax0_step", s, it, 3))
                for t in range(NT):
                    last = nc.vector.tensor_scalar(p0[s][:, t, :], p0[s][:, t, :], m0[s][:, t:t + 1], None, ALU.mult)
                last.then_inc(S["softmax0_step"][s], 1)

            def l0_router_max(s, it):
                key = (s, "l0_router")
                dve.wait_ge(*small_filled(it, key))
                logits = small(key)[:, 0:4 * NT].rearrange("p (t e) -> p t e", e=4)[:, :, 0:E3]
                nc.vector.tensor_reduce(rm[s][:, :], logits, AX_X, ALU.max).then_inc(S["router_step"][s], 1)
                dve.wait_ge(*of("router_step", s, it, 1))
                nc.vector.tensor_tensor(rl[s][:, :, :], logits, rm[s][:, :].unsqueeze(2).to_broadcast([128, NT, E3]), ALU.subtract)\
                    .then_inc(small_freed(key), 1)

            def l0_router_norm(s, it):
                dve.wait_ge(*of("router_exp", s, it, 1))
                nc.vector.tensor_reduce(rm[s][:, :], rl[s][:, :, :], AX_X, ALU.add).then_inc(S["router_step"][s], 1)
                dve.wait_ge(*of("router_step", s, it, 2))
                nc.vector.reciprocal(rm[s][:, :], rm[s][:, :]).then_inc(S["router_step"][s], 1)
                dve.wait_ge(*of("router_step", s, it, 3))
                nc.vector.scalar_tensor_tensor(out=rl[s][:, :, :], in0=rl[s][:, :, :], scalar=0.5,
                                               in1=rm[s][:, :].unsqueeze(2).to_broadcast([128, NT, E3]),
                                               op0=ALU.mult, op1=ALU.mult).then_inc(S["router_step"][s], 1)

            def l0_silu(s, it, half):
                key = (s, "l0_hidden", half)
                lo, hi = 4 * half, min(4 * half + 4, 7)
                dve.wait_ge(*of("tanh0_done", s, it, half + 1))
                nc.vector.tensor_scalar(th[s][:, lo:hi, :], th[s][:, lo:hi, :], 1.0, None, ALU.add).then_inc(S["silu0_step"][s], 1)
                dve.wait_ge(*of("silu0_step", s, it, half + 1))
                for i in range(lo, hi):
                    n = i - lo
                    last = nc.vector.scalar_tensor_tensor(out=hid[s][:, i, :], in0=big(key)[:, n // 2, (n % 2) * T:(n % 2 + 1) * T],
                                                          scalar=mod[s][:, 14 + i:15 + i], in1=th[s][:, i, :], op0=ALU.add, op1=ALU.mult)
                last.then_inc(big_freed(key), 1)

            def l0_route(s, it):
                key = (s, "l0_experts")
                dve.wait_ge(*of("router_step", s, it, 4))
                dve.wait_ge(*big_filled(it, key))
                for e in range(E3):
                    if e:
                        dve.wait_ge(*of("routed_step", s, it, e))
                    for t in range(NT):
                        src, prob = big(key)[:, t, e * C:(e + 1) * C], rl[s][:, t, e:e + 1]
                        if e == 0:
                            last = nc.vector.tensor_scalar(upd[s][:, t, :], src, prob, None, ALU.mult)
                        else:
                            last = nc.vector.scalar_tensor_tensor(out=upd[s][:, t, :], in0=src, scalar=prob, in1=upd[s][:, t, :],
                                                                  op0=ALU.mult, op1=ALU.add)
                    last.then_inc(S["routed_step"][s] if e < E3 - 1 else big_freed(key), 1)

            def l0_update(s, it):
                key = (s, "l0_out")
                dve.wait_ge(*small_taken(it, (s, "l0_gate")))
                dve.wait_ge(*small_filled(it, key))
                nc.vector.scalar_tensor_tensor(out=upd[s][:, :, :], in0=th[s][:, 7, :].rearrange("p (t c) -> p t c", t=NT), scalar=1.0,
                                               in1=nat(small(key)), op0=ALU.add, op1=ALU.mult).then_inc(small_freed(key), 1)
                dve.wait_ge(*small_taken(it, key))
                nc.vector.scalar_tensor_tensor(out=x[s][:, :, :], in0=upd[s][:, :, :], scalar=0.5, in1=xin[s][:, :, :],
                                               op0=ALU.mult, op1=ALU.add).then_inc(S["x_updated"][s], 1)

            def update(s, it, key, gate=None, factor=1.0, dst=None):
                dve.wait_ge(*small_filled(it, key))
                if gate is None:
                    nc.vector.tensor_tensor(upd[s][:, :, :], nat(small(key)), x[s][:, :, :], ALU.add).then_inc(small_freed(key), 1)
                    dve.wait_ge(*small_taken(it, key))
                    nc.vector.tensor_copy(x[s][:, :, :], upd[s][:, :, :]).then_inc(S["x_updated"][s], 1)
                else:
                    g = GATE[gate]
                    nc.vector.scalar_tensor_tensor(out=upd[s][:, :, :], in0=nat(small(key)), scalar=factor,
                                                   in1=gates[s][:, g:g + 1, :].to_broadcast([128, NT, C]),
                                                   op0=ALU.mult, op1=ALU.mult).then_inc(small_freed(key), 1)
                    dve.wait_ge(*small_taken(it, key))
                    nc.vector.tensor_tensor((dst or x[s])[:, :, :], upd[s][:, :, :], x[s][:, :, :], ALU.add).then_inc(S["x_updated"][s], 1)

            def residues(s, it, a):
                key = (s, "qkv", a)
                dve.wait_ge(*of("part1_done", s, it, a + 1))
                for i, b in enumerate((f"bq{a}", f"bk{a}")):
                    last = nc.vector.scalar_tensor_tensor(out=resid[s][:, i, :], in0=small(key)[:, i * T:(i + 1) * T], scalar=col(b),
                                                          in1=parts[s][:, 0, i, :], op0=ALU.add, op1=ALU.subtract)
                last.then_inc(small_freed(key), 1)
                dve.wait_ge(*small_taken(it, key))
                nc.vector.tensor_copy(parts[s][:, 1, :, :], resid[s][:, :, :]).then_inc(S["part2_done"][s], 1)
                dve.wait_ge(*of("part2_done", s, it, a + 1))
                nc.vector.tensor_tensor(parts[s][:, 2, :, :], resid[s][:, :, :], parts[s][:, 1, :, :], ALU.subtract)\
                    .then_inc(S["parts_done"][s], 1)

            def both_parts(s, it, last, half):
                dve.wait_ge(*big_taken(it, last))
                nc.vector.tensor_copy(rowmax[s][:, :, half, :, 1, :], rowmax[s][:, :, half, :, 0, :]).then_inc(S["negmax_step"][s], 1)

            def window_maxima(s, it, u):
                key = (s, "windows", u)
                dve.wait_ge(*big_filled(it, key))
                for p in range(2):
                    last = nc.vector.tensor_reduce(rowmax[s][:, :, u, p, 0, :],
                                                   big(key)[:, p, :].rearrange("q (w i k) -> q w i k", w=NT, k=WIN), AX_X, ALU.max)
                last.then_inc(big_freed(key), 1)
                both_parts(s, it, key, u)

            def maxima(s, it, a, j):
                key = (s, "scores", a, j)
                dve.wait_ge(*big_filled(it, key))
                nc.vector.tensor_reduce(rowmax[s][:, :, 2 * j // HP, :, 0, j % (HP // 2)].rearrange("q t p -> q p t"),
                                        big(key)[:, :, :].rearrange("q p (t k) -> q p t k", t=NT), AX_X, ALU.max)\
                    .then_inc(big_freed(key), 1)
                if j % (HP // 2) == HP // 2 - 1:
                    both_parts(s, it, key, 2 * j // HP)

            def minus_maxima(s, it, a, half):
                key, minus = (s, "maxT", a, half), negmax[half][s]
                dve.wait_ge(*small_filled(it, key))
                nc.vector.tensor_copy(minus[:, :], small(key)[0:2 * HP, 0:T]).then_inc(S["negmax_step"][s], 1)
                dve.wait_ge(*of("negmax_step", s, it, 4 * a + 2 * half + 2))
                nc.vector.scalar_tensor_tensor(out=minus[:, :], in0=minus[:, :], scalar=second_part[:, 0:1], in1=small(key)[0:2 * HP, 0:T],
                                               op0=ALU.mult, op1=ALU.subtract).then_inc(small_freed(key), 1)

            def normalise(s, it, a):
                key = (s, "out_natural", a)
                dve.wait_ge(*big_filled(it, key))
                o = big(key)[:, :, :].rearrange("p t (h d) -> p t h d", d=VW)
                den = rden[s][:, :].rearrange("p (t h) -> p t h", t=NT)
                nc.vector.reciprocal(den, o[:, :, :, D]).then_inc(S["rden_done"][s], 1)
                dve.wait_ge(*of("rden_done", s, it, a + 1))
                for t in range(NT):
                    last = nc.vector.tensor_tensor(on[s][:, t, :].rearrange("p (h d) -> p h d", d=D), o[:, t, :, 0:D],
                                                   den[:, t, :].unsqueeze(2).to_broadcast([128, H, D]), ALU.mult)
                last.then_inc(big_freed(key), 1)

            def top_16(s, it, j):
                key, g = (s, "top", j), top_unit[s, j]
                b = g % 2
                tile = [big(key)[:, i // 2, (i % 2) * T:(i % 2 + 1) * T] for i in range(4)]
                done = it * (SLOTS * HP * 8) + 8 * g
                dve.wait_ge(*big_filled(it, key))
                dve.sem_inc(passed["dve"], 1)
                for p in range(2):
                    for i in (2 * p, 2 * p + 1):
                        last = nc.vector.max(m8[:, b, 0, i, :], tile[i])
                    last.then_inc(top_step, 1)
                if g >= 2:
                    dve.wait_ge(e_done, it * (SLOTS * HP) + g - 1)
                for p in range(2):
                    dve.wait_ge(top_step, done + 1 + p)
                    dve.sem_inc(passed["dve"], 1)
                    if p == 1:
                        nc.vector.tensor_scalar(ntop[:, b, :], m8[:, b, 0, :, 0], -SCALE, None, ALU.mult)
                    for i in (2 * p, 2 * p + 1):
                        last = nc.vector.match_replace(s1[:, b, i, :], m8[:, b, 0, i, :], tile[i], NEG)
                    last.then_inc(top_step, 1)
                for p in range(2):
                    dve.wait_ge(top_step, done + 3 + p)
                    dve.sem_inc(passed["dve"], 1)
                    for i in (2 * p, 2 * p + 1):
                        last = nc.vector.max(m8[:, b, 1, i, :], s1[:, b, i, :])
                    last.then_inc(top_step, 1)
                for p in range(2):
                    dve.wait_ge(top_step, done + 5 + p)
                    dve.sem_inc(passed["dve"], 1)
                    for i in (2 * p, 2 * p + 1):
                        last = nc.vector.match_replace(s1[:, b, i, :], m8[:, b, 1, i, :], s1[:, b, i, :], NEG)
                    last.then_inc(top_step, 1)

            def swiglu(s, it):
                ka = (s, "swiglu")
                dve.wait_ge(*of("tanh3_done", s, it, 1))
                nc.vector.tensor_scalar(th[s][:, 0:4, :], th[s][:, 0:4, :], 1.0, None, ALU.add).then_inc(S["swiglu_step"][s], 1)
                dve.wait_ge(*of("swiglu_step", s, it, 1))
                for i in range(4):
                    last = nc.vector.scalar_tensor_tensor(out=hid[s][:, i, :], in0=big(ka)[:, i // 2, (i % 2) * T:(i % 2 + 1) * T],
                                                          scalar=col(f"l3_b1_{i}"), in1=th[s][:, i, :], op0=ALU.add, op1=ALU.mult)
                last.then_inc(big_freed(ka), 1)

            def swiglu_up(s, it):
                ka, kb = (s, "swiglu"), (s, "swiglu_up")
                for t in [big_taken(it, ka), big_filled(it, kb)]:
                    dve.wait_ge(*t)
                for i in range(4):
                    last = nc.vector.scalar_tensor_tensor(out=hid[s][:, i, :], in0=big(kb)[:, i // 2, (i % 2) * T:(i % 2 + 1) * T],
                                                          scalar=col(f"l3_b1_{4 + i}"), in1=hid[s][:, i, :], op0=ALU.add, op1=ALU.mult)
                last.then_inc(big_freed(kb), 1)

            def project_out(s, it, a):
                update(s, it, (s, "project", a), {A_2S: "l2a", A_3W: "l3a", A_3C: "l3c"}.get(a))

            def mlp2_out(s, it):
                update(s, it, (s, "mlp2"), "l2m")

            def mlp3_out(s, it):
                update(s, it, (s, "mlp3"), "l3m", 0.5, xout[s])

            both = range(SLOTS)
            for f in big_free + small_free:
                dve.sem_inc(f, 1)
            nc.vector.memset(ones3[:, :], 1.0).then_inc(const_set, 1)
            nc.vector.memset(twos3[:, :], 2.0).then_inc(const_set, 1)
            dve.wait_ge(rows_loaded, 16)
            for i in range(PARTS):
                nc.vector.tensor_copy(row_parts[:, i, :], rowf[:, :]).then_inc(split_step, 1)
                if i < PARTS - 1:
                    dve.wait_ge(split_step, 2 * i + 1)
                    nc.vector.tensor_tensor(rowf[:, :], rowf[:, :], row_parts[:, i, :], ALU.subtract).then_inc(split_step, 1)
                    dve.wait_ge(split_step, 2 * i + 2)
            dve.wait_ge(cols_loaded, 16)
            nc.vector.tensor_scalar(half_b[:, :], col("l3_b1_0", 4), 0.5, None, ALU.mult).then_inc(const_set, 1)

            dve.wait_ge(mask_loaded, 16)
            dve.wait_ge(tanh_all_done, 1)
            nc.vector.scalar_tensor_tensor(out=silu_all[:, :], in0=tanh_all[:, :], scalar=1.0, in1=cond_all[:, :],
                                           op0=ALU.add, op1=ALU.mult).then_inc(silu_all_step, 1)
            dve.wait_ge(silu_all_step, 1)
            nc.vector.tensor_scalar(silu_all[:, :], silu_all[:, :], 0.5, None, ALU.mult).then_inc(silu_all_step, 1)
            dve.wait_ge(mods_made, 1)
            nc.vector.tensor_tensor(mods_all[:, :, 0:21].rearrange("p b m -> p m b"),
                                    OUT[0][:, 0:21 * B].rearrange("p (m b) -> p m b", b=B),
                                    col("mod0", 21).unsqueeze(2).to_broadcast([128, 21, B]), ALU.add).then_inc(mods_step, 1)
            nc.vector.tensor_copy(gates_all[:, 0:2, :].rearrange("b g c -> b (g c)"), OUT[0][0:B, 256:512]).then_inc(mods_step, 1)
            nc.vector.tensor_copy(gates_all[:, 2:5, :].rearrange("b g c -> b (g c)"), OUT[1][0:B, 0:3 * C]).then_inc(mods_step, 1)
            dve.wait_ge(mods_step, 1)
            nc.vector.tensor_scalar(mods_all[:, :, 0:7], mods_all[:, :, 0:7], 1.0, None, ALU.add).then_inc(mods_step, 1)
            nc.vector.tensor_scalar(mods_all[:, :, 21:28], mods_all[:, :, 14:21], 0.5, None, ALU.mult).then_inc(mods_step, 1)

            with dve.Fori(0, B // SLOTS) as it:
                follow(it, dict(
                    cond=cond_spread, stats=norm_stats, apply=norm_apply, l0_scores=l0_max, l0_normalise=l0_normalise,
                    l0_router=l0_router_max, l0_router_norm=l0_router_norm, l0_hidden=l0_silu, l0_experts=l0_route,
                    l0_out=l0_update, qkv=residues, scores=maxima, windows=window_maxima, maxT=minus_maxima, top=top_16,
                    out_natural=normalise, project=project_out, mlp2=mlp2_out, swiglu=swiglu, swiglu_up=swiglu_up, mlp3=mlp3_out))

        @block.gpsimd
        def _(pool):
            def inverse_root(s, it, n):
                pool.wait_ge(*of("ve_done", s, it, n + 1))
                nc.gpsimd.tensor_tensor(rstd[s][:, n % 2, :], ve[s][:, n % 2, :], minus_half[:, :], ALU.pow).then_inc(S["rstd_done"][s], 1)

            def chosen(s, it, j):
                g = top_unit[s, j]
                pool.wait_ge(e_done, it * (SLOTS * HP) + g + 1)
                if g >= CHOSEN_BUFS:
                    t, i = top_order[g - CHOSEN_BUFS]
                    pool.wait_ge(*big_filled(it, (t, "topT", i)))
                nc.gpsimd.tensor_tensor(ptop[:, g % CHOSEN_BUFS, :, :], e_all[:, g % 2, :, :], e_rest[:, g % 2, :, :], ALU.subtract)\
                    .then_inc(p_done, 1)

            constants = [(minus_half[:, :], -0.5)]
            for s in range(SLOTS):
                constants += [(Ks[s][p:p + 32, :, :], 1.0) for p in (32, 96)]
                constants += [(V[s][:, :, D + 1:VW], 0.0), (V[s][:, :, D:D + 1], 1.0)]
            assert len(constants) == POOL_CONSTS
            for n, (dst, value) in enumerate(constants):
                nc.gpsimd.memset(dst, value).then_inc(pool_const, 1)
                pool.wait_ge(pool_const, n + 1)
            with pool.Fori(0, B // SLOTS) as it:
                follow(it, dict(stats=inverse_root, rest=chosen))


def kernel(**inputs):
    import numpy as np
    import concourse.bacc as bacc
    from concourse.bass_utils import run_bass_kernel_spmd

    a = {k: np.asarray(v) for k, v in inputs.items()}
    l0, l1, l2, l3 = ({k[len(p):]: v for k, v in a.items() if k.startswith(p)} for p in
                      ("L0_xcond_", "L1_xcond_", "L2_xcond_", "L3_xcond_"))
    turn = [(2 * h2 + p) * D + d for d in range(D) for p in range(2) for h2 in range(HP)]

    def thirds(m, i):
        return m[..., i * C:(i + 1) * C]

    qkvo = [
        (l1["Wq"], l1["bq"], thirds(l1["Wkv"], 0), thirds(l1["bkv"], 0), thirds(l1["Wkv"], 1), thirds(l1["bkv"], 1), l1["Wp"], l1["bp"]),
        (*(f(l2[n], i) for i in (0, 1, 2) for f, n in ((thirds, "qkv_w"), (thirds, "qkv_b"))), l2["self_o_w"], l2["self_o_b"]),
        (l2["q_w"], l2["q_b"], thirds(l2["kv_w"], 0), thirds(l2["kv_b"], 0), thirds(l2["kv_w"], 1), thirds(l2["kv_b"], 1), l2["cross_o_w"], l2["cross_o_b"]),
        (*(f(l3[n], i) for i in (0, 1, 2) for f, n in ((thirds, "w_qkv"), (thirds, "b_qkv"))), l3["w_so"], l3["b_so"]),
        (l3["w_q"], l3["b_q"], thirds(l3["w_kv"], 0), thirds(l3["b_kv"], 0), thirds(l3["w_kv"], 1), thirds(l3["b_kv"], 1), l3["w_co"], l3["b_co"]),
    ]
    q_ss, kv_ss, ada2, ada3 = (l1["Wss_q"], l1["bss_q"]), (l1["Wss_kv"], l1["bss_kv"]), (l2["ada_w"], l2["ada_b"]), (l3["w_ada"], l3["b_ada"])
    scales = [(*q_ss, 0), (*kv_ss, 0), (*ada2, 1), (*ada2, 4), (*ada3, 1), (*ada3, 4), (*ada3, 7)]
    shifts = [(*q_ss, 1), (*kv_ss, 1), (*ada2, 0), (*ada2, 3), (*ada3, 0), (*ada3, 3), (*ada3, 6)]
    gates = [(*ada2, 2), (*ada2, 5), (*ada3, 2), (*ada3, 5), (*ada3, 8)]

    def by_rows(m):
        return np.concatenate([m[i * C:(i + 1) * C] for i in range(m.shape[0] // C)], axis=1)

    mats = {"l0_q": l0["Wq"], "l0_k": l0["Wk"], "l0_v": l0["Wv"], "l0_router": by_rows(l0["router_W"]), "l0_g2": l0["gate_w2"], "l0_out": l0["out_w"],
            "mod": np.concatenate([thirds(m, i) for m, _, i in scales + shifts], axis=1),
            "gate": np.concatenate([thirds(m, i) for m, _, i in gates], axis=1),
            "l2_w1": l2["mlp_w1"], "l2_w2": by_rows(l2["mlp_w2"]), "l3_w1": l3["w_m1"], "l3_w2": by_rows(l3["w_m2"])}
    vecs = {"ln_g": l0["ln_gamma"], "ln_b": l0["ln_beta"], "n2_g": l2["norm2_g"], "n2_b": l2["norm2_b"], "anchor6": l0["gate_b1"]}
    rows = {"router": l0["router_b"], "g2": l0["gate_b2"], "out": l0["out_b"], "l2_b2": l2["mlp_b2"], "l3_b2": l3["b_m2"]}
    for i in range(3):
        mats[f"l0_g1_{i}"] = l0["gate_w1"][i * C:(i + 1) * C]
    for e in range(E3):
        rows[f"e{e}"] = l0["e_b2"][e]
        for i in range(3):
            mats[f"l0_w1_{e}_{i}"] = l0["e_w1"][e, i * C:(i + 1) * C]
        for i in range(2):
            mats[f"l0_w2_{e}_{i}"] = l0["e_w2"][e, i * C:(i + 1) * C]
            vecs[f"anchor{2 * e + i}"] = l0["e_b1"][e, i * C:(i + 1) * C]
    for i, (_, b, n) in enumerate(scales + shifts):
        vecs[f"mod{i}"] = thirds(b, n)
    for i, (_, b, n) in enumerate(gates):
        rows[f"gate{i}"] = thirds(b, n)
    for n, (wq, bq, wk, bk, wv, bv, wo, bo) in enumerate(qkvo):
        mats[f"q{n}"], mats[f"k{n}"], mats[f"v{n}"], mats[f"o{n}"] = wq[:, turn], wk[:, turn], wv, wo
        vecs[f"bq{n}"], vecs[f"bk{n}"], rows[f"bv{n}"], rows[f"bo{n}"] = bq[turn], bk[turn], bv, bo
    for i in range(4):
        vecs[f"l2_b1_{i}"] = l2["mlp_b1"][i * C:(i + 1) * C]
    for i in range(8):
        vecs[f"l3_b1_{i}"] = l3["b_m1"][i * C:(i + 1) * C]

    def with_more(v):
        return np.concatenate([v, v[:SLOTS]], axis=0)

    row_block = np.zeros((len(ROWV), C), np.float32)
    for name, i in ROW.items():
        row_block[i, :rows[name].shape[0]] = rows[name]
    arrays = {
        "x": with_more(a["x"]),
        "ctx": with_more(a["ctx_1024"]),
        "ctxT": with_more(np.transpose(a["ctx_1024"], (0, 2, 1))),
        "second_part": np.tile(np.repeat([0.0, 1.0], HP // 2), 2).astype(np.float32)[:, None],
        "cond_all": np.ascontiguousarray(a["cond_1024"].T),
        "condT": with_more(a["cond_1024"][:, :, None]),
        "mats": np.ascontiguousarray(np.concatenate([mats[n] for g in MATS.values() for n, _ in g], axis=1)),
        "cols": np.ascontiguousarray(np.stack([vecs[n] for n in COLS], axis=1)),
        "rows": row_block,
        "ident": np.eye(128, dtype=np.float32),
    }
    nc = bacc.Bacc("TRN2", target_bir_lowering=False, num_devices=1)
    ins = {n: nc.dram_tensor(f"in_{n}", v.shape, mybir.dt.from_np(v.dtype), kind="ExternalInput").ap() for n, v in arrays.items()}
    out = nc.dram_tensor("out", (B, T, C), F32, kind="ExternalOutput").ap()
    chain_kernel(nc, ins, out)
    r = run_bass_kernel_spmd(nc, [{f"in_{n}": v for n, v in arrays.items()}], core_ids=[0])
    return r.results[0]["out"]
```
